# Optimizing a Trainium2 kernel written in Bass

```python
import numpy as np
import jax
import jax.numpy as jnp

def _softmax(x, axis=-1):
    return jax.nn.softmax(x, axis=axis)

def _gelu(x):
    return jax.nn.gelu(x, approximate=True)

def _silu(x):
    return jax.nn.silu(x)

def _sigmoid(x):
    return jax.nn.sigmoid(x)

def _layernorm(x, axis=-1, eps=1e-05):
    m = jnp.mean(x, axis=axis, keepdims=True)
    v = jnp.var(x, axis=axis, keepdims=True)
    return (x - m) / jnp.sqrt(v + eps)

def _scatter_add(tgt, idx, src, axis=0):
    return tgt.at[idx].add(src)

def _segment_sum(src, seg, n):
    return jax.ops.segment_sum(src, seg, n)
kernel_name = 'mk_decoder_postln_d1_seqx_r8_fd9726'

def setup_inputs(seed: int=0):
    np.random.seed(seed)
    _w = jnp.asarray

    def _rec_inputs():
        import jax
        import jax.numpy as jnp
        _rk = jax.random.key(seed)
        x = -0.0002928 + 1 * jax.random.normal(jax.random.fold_in(_rk, 1), (8, 128, 128), jnp.float32)
        _lenS = 128 - jax.random.randint(jax.random.fold_in(_rk, 7), (8,), 0, max(1, 128 // 4) + 1, jnp.int32)
        _lenS2 = 128 - jax.random.randint(jax.random.fold_in(_rk, 8), (8,), 0, max(1, 128 // 4) + 1, jnp.int32)
        _ctx_1024P = jax.random.normal(jax.random.fold_in(_rk, 11), (8, 16, 128), jnp.float32)
        _ctx_1024c = jax.random.dirichlet(jax.random.fold_in(_rk, 511), 0.3 * jnp.ones((16,), jnp.float32), (8, 128))
        _ctx_1024t = jnp.einsum('bsk,bkd->bsd', _ctx_1024c, _ctx_1024P)
        _ctx_1024t = _ctx_1024t * jax.lax.rsqrt(jnp.mean(jnp.square(_ctx_1024t)) + 1e-12) * 0.953939
        ctx_1024 = -1.39393e-06 + 0.999914 * (_ctx_1024t + 0.3 * jax.random.normal(jax.random.fold_in(_rk, 611), (8, 128, 128), jnp.float32))
        return (x, ctx_1024)
    x, ctx_1024 = _rec_inputs()

    def _L0_attn_setup():
        import jax, jax.numpy as jnp
        import numpy as np
        D_MODEL = 128
        D_STATE = 16
        D_CONV = 4
        EXPAND = 2
        D_INNER = EXPAND * D_MODEL
        DT_RANK = (D_MODEL + 15) // 16
        BATCH = 2
        SEQLEN = 128

        def _causal_conv_silu(x, w, b):
            k = w.shape[-1]
            y = jax.lax.conv_general_dilated(x, w, window_strides=(1,), padding=[(k - 1, 0)], dimension_numbers=('NCH', 'OIH', 'NCH'), feature_group_count=x.shape[1])
            return jax.nn.silu(y + b[None, :, None])

        def _ssm_scan(dA, dBx):

            def op(e1, e2):
                a1, b1 = e1
                a2, b2 = e2
                return (a1 * a2, a2 * b1 + b2)
            return jax.lax.associative_scan(op, (dA, dBx), axis=2)[1]

        def _mamba_dir(xz, conv_w, conv_b, xproj_w, dtproj_w, dt_bias, A_log, Dp):
            d_inner = xz.shape[1] // 2
            x, z = (xz[:, :d_inner], xz[:, d_inner:])
            u = _causal_conv_silu(x, conv_w, conv_b)
            x_dbl = jnp.einsum('bdl,kd->bkl', u, xproj_w)
            n = A_log.shape[1]
            r = dtproj_w.shape[1]
            delta = jnp.einsum('dr,brl->bdl', dtproj_w, x_dbl[:, :r])
            Bm = x_dbl[:, r:r + n]
            Cm = x_dbl[:, r + n:]
            delta = jax.nn.softplus(delta + dt_bias[None, :, None])
            A = -jnp.exp(A_log)
            dA = jnp.exp(jnp.einsum('bdl,dn->bdln', delta, A))
            dBx = jnp.einsum('bdl,bnl,bdl->bdln', delta, Bm, u)
            h = _ssm_scan(dA, dBx)
            y = jnp.einsum('bdln,bnl->bdl', h, Cm)
            y = y + Dp[None, :, None] * u
            return y * jax.nn.silu(z)
        key = jax.random.key(seed)
        ks = jax.random.split(key, 16)
        s_in = 1.0 / np.sqrt(D_MODEL)
        s_x = 1.0 / np.sqrt(D_INNER)
        dt_std = DT_RANK ** (-0.5)

        def dt_bias_init(k):
            dt = jnp.exp(jax.random.uniform(k, (D_INNER,)) * (np.log(0.1) - np.log(0.001)) + np.log(0.001))
            dt = jnp.clip(dt, 0.0001, None)
            return dt + jnp.log(-jnp.expm1(-dt))
        A_log = jnp.log(jnp.tile(jnp.arange(1, D_STATE + 1, dtype=jnp.float32)[None, :], (D_INNER, 1)))
        inp = {'hidden_states': jax.random.normal(ks[0], (BATCH, SEQLEN, D_MODEL), jnp.float32), 'in_proj_w': jax.random.normal(ks[1], (2 * D_INNER, D_MODEL), jnp.float32) * s_in, 'conv_w': jax.random.normal(ks[2], (D_INNER, 1, D_CONV), jnp.float32) * 0.3, 'conv_bias': jnp.zeros((D_INNER,), jnp.float32), 'x_proj_w': jax.random.normal(ks[3], (DT_RANK + 2 * D_STATE, D_INNER), jnp.float32) * s_x, 'dt_proj_w': jax.random.uniform(ks[4], (D_INNER, DT_RANK), jnp.float32, -dt_std, dt_std), 'dt_proj_bias': dt_bias_init(ks[5]), 'A_log': A_log, 'D_skip': jnp.ones((D_INNER,), jnp.float32), 'convb_w': jax.random.normal(ks[6], (D_INNER, 1, D_CONV), jnp.float32) * 0.3, 'convb_bias': jnp.zeros((D_INNER,), jnp.float32), 'x_proj_b_w': jax.random.normal(ks[7], (DT_RANK + 2 * D_STATE, D_INNER), jnp.float32) * s_x, 'dt_proj_b_w': jax.random.uniform(ks[8], (D_INNER, DT_RANK), jnp.float32, -dt_std, dt_std), 'dt_proj_b_bias': dt_bias_init(ks[9]), 'A_b_log': A_log, 'D_b_skip': jnp.ones((D_INNER,), jnp.float32), 'out_proj_w': jax.random.normal(ks[10], (D_MODEL, D_INNER), jnp.float32) * s_x}
        return inp
    _L0_attn_all = _L0_attn_setup()
    _L0_attn_in = {k: v for k, v in _L0_attn_all.items() if k in ('in_proj_w', 'conv_w', 'conv_bias', 'x_proj_w', 'dt_proj_w', 'dt_proj_bias', 'A_log', 'D_skip', 'convb_w', 'convb_bias', 'x_proj_b_w', 'dt_proj_b_w', 'dt_proj_b_bias', 'A_b_log', 'D_b_skip', 'out_proj_w')}
    del _L0_attn_all

    def _L0_xattn_setup():
        import jax, jax.numpy as jnp
        import numpy as np
        EMBED_DIM = 128
        N_HEADS = 16
        HEAD_DIM = EMBED_DIM // N_HEADS
        B, S = (2, 256)
        key = jax.random.key(seed)
        ks = jax.random.split(key, 7)
        scale = 1.0 / np.sqrt(EMBED_DIM)
        return {'query': jax.random.normal(ks[0], (B, S, EMBED_DIM), dtype=jnp.float32), 'key': jax.random.normal(ks[1], (B, S, EMBED_DIM), dtype=jnp.float32), 'value': jax.random.normal(ks[2], (B, S, EMBED_DIM), dtype=jnp.float32), 'Wq': jax.random.normal(ks[3], (EMBED_DIM, EMBED_DIM), dtype=jnp.float32) * scale, 'Wk': jax.random.normal(ks[4], (EMBED_DIM, EMBED_DIM), dtype=jnp.float32) * scale, 'Wv': jax.random.normal(ks[5], (EMBED_DIM, EMBED_DIM), dtype=jnp.float32) * scale, 'Wo': jax.random.normal(ks[6], (EMBED_DIM, EMBED_DIM), dtype=jnp.float32) * scale}
    _L0_xattn_all = _L0_xattn_setup()
    _L0_xattn_in = {k: v for k, v in _L0_xattn_all.items() if k in ('Wq', 'Wk', 'Wv', 'Wo')}
    del _L0_xattn_all

    def _L0_ffn_setup():
        import jax, jax.numpy as jnp
        import numpy as np
        B, S, D = (4, 256, 128)
        E = 8
        F = 512
        T = B * S
        CAP = 160
        key = jax.random.key(seed)
        k1, k2, k3, k4 = jax.random.split(key, 4)
        inputs = jax.random.normal(k1, (B, S, D), dtype=jnp.float32)
        gate_w = jax.random.normal(k2, (D, E), dtype=jnp.float32) / np.sqrt(D)
        w1 = jax.random.normal(k3, (E, D, F), dtype=jnp.float32) / np.sqrt(D)
        w2 = jax.random.normal(k4, (E, F, D), dtype=jnp.float32) / np.sqrt(F)
        return {'inputs': inputs, 'gate_w': gate_w, 'w1': w1, 'w2': w2}
    _L0_ffn_all = _L0_ffn_setup()
    _L0_ffn_in = {k: v for k, v in _L0_ffn_all.items() if k in ('gate_w', 'w1', 'w2')}
    del _L0_ffn_all
    return {'x': x, 'ctx_1024': ctx_1024, 'L0_attn_in_proj_w': _L0_attn_in['in_proj_w'], 'L0_attn_conv_w': _L0_attn_in['conv_w'], 'L0_attn_conv_bias': _L0_attn_in['conv_bias'], 'L0_attn_x_proj_w': _L0_attn_in['x_proj_w'], 'L0_attn_dt_proj_w': _L0_attn_in['dt_proj_w'], 'L0_attn_dt_proj_bias': _L0_attn_in['dt_proj_bias'], 'L0_attn_A_log': _L0_attn_in['A_log'], 'L0_attn_D_skip': _L0_attn_in['D_skip'], 'L0_attn_convb_w': _L0_attn_in['convb_w'], 'L0_attn_convb_bias': _L0_attn_in['convb_bias'], 'L0_attn_x_proj_b_w': _L0_attn_in['x_proj_b_w'], 'L0_attn_dt_proj_b_w': _L0_attn_in['dt_proj_b_w'], 'L0_attn_dt_proj_b_bias': _L0_attn_in['dt_proj_b_bias'], 'L0_attn_A_b_log': _L0_attn_in['A_b_log'], 'L0_attn_D_b_skip': _L0_attn_in['D_b_skip'], 'L0_attn_out_proj_w': _L0_attn_in['out_proj_w'], 'L0_xattn_Wq': _L0_xattn_in['Wq'], 'L0_xattn_Wk': _L0_xattn_in['Wk'], 'L0_xattn_Wv': _L0_xattn_in['Wv'], 'L0_xattn_Wo': _L0_xattn_in['Wo'], 'L0_ffn_gate_w': _L0_ffn_in['gate_w'], 'L0_ffn_w1': _L0_ffn_in['w1'], 'L0_ffn_w2': _L0_ffn_in['w2']}

def reference(x, ctx_1024, L0_attn_in_proj_w, L0_attn_conv_w, L0_attn_conv_bias, L0_attn_x_proj_w, L0_attn_dt_proj_w, L0_attn_dt_proj_bias, L0_attn_A_log, L0_attn_D_skip, L0_attn_convb_w, L0_attn_convb_bias, L0_attn_x_proj_b_w, L0_attn_dt_proj_b_w, L0_attn_dt_proj_b_bias, L0_attn_A_b_log, L0_attn_D_b_skip, L0_attn_out_proj_w, L0_xattn_Wq, L0_xattn_Wk, L0_xattn_Wv, L0_xattn_Wo, L0_ffn_gate_w, L0_ffn_w1, L0_ffn_w2):
    import jax
    import jax.numpy as jnp

    def _L0_attn_ref(hidden_states, in_proj_w, conv_w, conv_bias, x_proj_w, dt_proj_w, dt_proj_bias, A_log, D_skip, convb_w, convb_bias, x_proj_b_w, dt_proj_b_w, dt_proj_b_bias, A_b_log, D_b_skip, out_proj_w):
        import jax, jax.numpy as jnp
        import numpy as np
        D_MODEL = 128
        D_STATE = 16
        D_CONV = 4
        EXPAND = 2
        D_INNER = EXPAND * D_MODEL
        DT_RANK = (D_MODEL + 15) // 16
        BATCH = 2
        SEQLEN = 128

        def _causal_conv_silu(x, w, b):
            k = w.shape[-1]
            y = jax.lax.conv_general_dilated(x, w, window_strides=(1,), padding=[(k - 1, 0)], dimension_numbers=('NCH', 'OIH', 'NCH'), feature_group_count=x.shape[1])
            return jax.nn.silu(y + b[None, :, None])

        def _ssm_scan(dA, dBx):

            def op(e1, e2):
                a1, b1 = e1
                a2, b2 = e2
                return (a1 * a2, a2 * b1 + b2)
            return jax.lax.associative_scan(op, (dA, dBx), axis=2)[1]

        def _mamba_dir(xz, conv_w, conv_b, xproj_w, dtproj_w, dt_bias, A_log, Dp):
            d_inner = xz.shape[1] // 2
            x, z = (xz[:, :d_inner], xz[:, d_inner:])
            u = _causal_conv_silu(x, conv_w, conv_b)
            x_dbl = jnp.einsum('bdl,kd->bkl', u, xproj_w)
            n = A_log.shape[1]
            r = dtproj_w.shape[1]
            delta = jnp.einsum('dr,brl->bdl', dtproj_w, x_dbl[:, :r])
            Bm = x_dbl[:, r:r + n]
            Cm = x_dbl[:, r + n:]
            delta = jax.nn.softplus(delta + dt_bias[None, :, None])
            A = -jnp.exp(A_log)
            dA = jnp.exp(jnp.einsum('bdl,dn->bdln', delta, A))
            dBx = jnp.einsum('bdl,bnl,bdl->bdln', delta, Bm, u)
            h = _ssm_scan(dA, dBx)
            y = jnp.einsum('bdln,bnl->bdl', h, Cm)
            y = y + Dp[None, :, None] * u
            return y * jax.nn.silu(z)
        xz = jnp.einsum('ed,bld->bel', in_proj_w, hidden_states)
        out_f = _mamba_dir(xz, conv_w, conv_bias, x_proj_w, dt_proj_w, dt_proj_bias, A_log, D_skip)
        out_b = _mamba_dir(xz[:, :, ::-1], convb_w, convb_bias, x_proj_b_w, dt_proj_b_w, dt_proj_b_bias, A_b_log, D_b_skip)[:, :, ::-1]
        return jnp.einsum('bdl,od->blo', out_f + out_b, out_proj_w)

    def _L0_xattn_ref(query, key, value, Wq, Wk, Wv, Wo):
        import jax, jax.numpy as jnp
        import numpy as np
        EMBED_DIM = 128
        N_HEADS = 16
        HEAD_DIM = EMBED_DIM // N_HEADS
        B, S = (2, 256)
        Q = query @ Wq.T
        K = key @ Wk.T
        V = value @ Wv.T
        b, s, _ = Q.shape
        Qh = Q.reshape(b, s, N_HEADS, HEAD_DIM)
        Kh = K.reshape(b, s, N_HEADS, HEAD_DIM)
        Vh = V.reshape(b, s, N_HEADS, HEAD_DIM)
        scores = jnp.einsum('bqhd,bkhd->bhqk', Qh, Kh) / jnp.sqrt(jnp.asarray(HEAD_DIM, dtype=Qh.dtype))
        attn = jax.nn.softmax(scores, axis=-1)
        out = jnp.einsum('bhqk,bkhd->bqhd', attn, Vh)
        out = out.reshape(b, s, N_HEADS * HEAD_DIM)
        return out @ Wo.T

    def _L0_ffn_ref(inputs, gate_w, w1, w2):
        import jax, jax.numpy as jnp
        import numpy as np
        B, S, D = (4, 256, 128)
        E = 8
        F = 512
        T = B * S
        CAP = 160
        tokens = inputs.reshape(-1, D)
        logits = tokens @ gate_w
        probs = jax.nn.softmax(logits, axis=-1)
        expert_idx = jnp.argmax(probs, axis=-1)
        mask1 = jax.nn.one_hot(expert_idx, E, dtype=tokens.dtype)
        pos = (jnp.cumsum(mask1, axis=0) - 1.0).astype(jnp.int32)
        sec_mask = mask1[:, :, None] * jax.nn.one_hot(pos, CAP, dtype=tokens.dtype)
        combine_weights = probs[:, :, None] * sec_mask
        expert_input = jnp.einsum('tec,td->ecd', sec_mask, tokens)
        h = jax.nn.relu(jnp.einsum('ecd,edf->ecf', expert_input, w1))
        expert_output = jnp.einsum('ecf,efd->ecd', h, w2)
        out = jnp.einsum('tec,ecd->td', combine_weights, expert_output)
        return out.reshape(inputs.shape)
    x = _layernorm(x + _L0_attn_ref(x, L0_attn_in_proj_w, L0_attn_conv_w, L0_attn_conv_bias, L0_attn_x_proj_w, L0_attn_dt_proj_w, L0_attn_dt_proj_bias, L0_attn_A_log, L0_attn_D_skip, L0_attn_convb_w, L0_attn_convb_bias, L0_attn_x_proj_b_w, L0_attn_dt_proj_b_w, L0_attn_dt_proj_b_bias, L0_attn_A_b_log, L0_attn_D_b_skip, L0_attn_out_proj_w), axis=-1)
    x = _layernorm(x + _L0_xattn_ref(x, ctx_1024, ctx_1024, L0_xattn_Wq, L0_xattn_Wk, L0_xattn_Wv, L0_xattn_Wo), axis=-1)
    x = _layernorm(x + _L0_ffn_ref(x, L0_ffn_gate_w, L0_ffn_w1, L0_ffn_w2), axis=-1)
    return x

_drawn_inputs = setup_inputs


def setup_inputs(seed=0):
    import zlib

    import numpy as np

    out = dict(_drawn_inputs(seed))
    spreads = {'L0_attn_conv_bias': (0.0, 0.1),
     'L0_attn_D_skip': (1.0, 0.2),
     'L0_attn_convb_bias': (0.0, 0.1),
     'L0_attn_D_b_skip': (1.0, 0.2)}
    factors = {'L0_attn_x_proj_w': 2.838,
     'L0_attn_dt_proj_w': 6.031,
     'L0_attn_dt_proj_bias': 3.822,
     'L0_attn_A_log': 3.238,
     'L0_attn_x_proj_b_w': 3.238,
     'L0_attn_dt_proj_b_w': 8.0,
     'L0_attn_dt_proj_b_bias': 4.197,
     'L0_attn_A_b_log': 3.857}
    for name, (base, spread) in spreads.items():
        noise = np.random.default_rng([zlib.crc32(name.encode()), seed]).standard_normal(out[name].shape)
        drawn = base * np.exp(spread * noise) if base else spread * noise
        out[name] = jnp.asarray(drawn.astype(out[name].dtype))
    for name, factor in factors.items():
        out[name] = (out[name] * factor).astype(out[name].dtype)
    return out
```

```python
from contextlib import ExitStack

import concourse.bass as bass
from concourse import mybir

F32 = mybir.dt.float32
BF16 = mybir.dt.bfloat16
U32 = mybir.dt.uint32
ALU = mybir.AluOpType
ACT = mybir.ActivationFunctionType
AX = mybir.AxisListType
P = 128
BANK = 512
EPS = 1e-5


def decoder_layer_kernel(nc, x, ctx_1024, in_proj_w, conv_w, conv_bias, x_proj_w, dt_proj_w, dt_proj_bias,
                         A_log, D_skip, convb_w, convb_bias, x_proj_b_w, dt_proj_b_w, dt_proj_b_bias,
                         A_b_log, D_b_skip, out_proj_w, Wq, Wk, Wv, Wo, gate_w, w1, w2, out):
    B, S, D = x.shape
    T = B * S
    TH = T // 2
    HB = B // 2
    DI = in_proj_w.shape[0] // 2
    NH = DI // P
    N = A_log.shape[1]
    R = dt_proj_w.shape[1]
    K = conv_w.shape[2]
    PAD = K - 1
    SP = S + 2 * PAD
    NB = 2 * N
    DT0 = 3 * NB
    XM = DT0 + R
    HEADS = 16
    DH = D // HEADS
    GH = 4
    CH = 8
    E = gate_w.shape[1]
    F = w1.shape[2]
    FC = F // P
    CAP = 160
    HC = CAP // 2
    SLOTS = E * CAP
    ST = SLOTS // P
    SCALE = float(DH) ** -0.5
    assert S == P and D == P and TH == BANK and NH == 2 and CH * S == 2 * BANK

    d_slots = nc.dram_tensor("dispatched_tokens", (SLOTS + T, D), F32).ap()
    d_expert = nc.dram_tensor("expert_outputs", (SLOTS + P, D), F32).ap()

    with ExitStack() as ctx:
        def sb(name, shape, dt=F32):
            return ctx.enter_context(nc.sbuf_tensor(name, shape, dt))

        def sem(name):
            return ctx.enter_context(nc.semaphore(name))

        bank = ctx.enter_context(nc.psum_tensor("bank", [P, 8, BANK], F32))

        ident = sb("ident", [P, P])
        x_tok = sb("x_tok", [P, B, D])
        ctx_tok = sb("ctx_tok", [P, B, D])
        b_row = sb("b_row", [P, 2, T])
        early = b_row[:, :, :].rearrange("p a t -> p (a t)")
        win = early[:, 0:512].rearrange("p (c d) -> p c d", c=2 * NH)
        wqkvo = early[:, 512:1024].rearrange("p (n d) -> p n d", n=4)
        wout = early[:, 1024:1280]
        xproj = early[0:R + NB, 1280:1792].rearrange("p (a d) -> p a d", a=2)
        cw = sb("cw", [P, 2, NH, K])
        a_log = sb("a_log", [P, 2, NH, N])
        a_neg = sb("a_neg", [P, 2, NH, N])
        vec_rows = sb("vec_rows", [6 * NH, P])
        vec_cols = sb("vec_cols", [P, 6 * NH])
        dtw = sb("dtw", [P, 2, NH, XM])
        gate = sb("gate", [P, E])
        w1_sb = sb("w1_sb", [P, E, F])
        w2_sb = sb("w2_sb", [P, E, FC, D])

        xT = sb("xT", [P, B, SP])
        wkT = sb("wkT", [P, 2, NH, K, P])
        wzT = sb("wzT", [P, NH, P])
        woutT = sb("woutT", [P, NH, D])
        xprojT = sb("xprojT", [P, 2, NH, XM])
        dtT = sb("dtT", [P, 2, NH, P])
        qkvoT = sb("qkvoT", [P, 4, D])
        diag_d = sb("diag_d", [P, 2, NH, P])
        sel = sb("sel", [3 * NB, NB, P], BF16)
        sel_id = sb("sel_id", [3 * NB, NB])
        uT = sb("uT", [P, 2, NH, T])
        szT = sb("szT", [P, NH, T])
        parts = sb("parts", [3 * NB, 2, T], BF16)
        delta = sb("delta", [P, 2, NH, T])
        du = uT
        arena = sb("arena", [P, 12, T])
        head_mask = sb("head_mask", [P, GH])
        k_maskT = sb("k_maskT", [P, B, GH, S])
        v_ext = sb("v_ext", [P, B, HEADS, DH + 1])
        x1 = x_tok
        x2 = ctx_tok
        stats = sb("stats", [P, B, 6])
        moments = sb("moments", [P, B, 2])
        rstd = sb("rstd", [P, B])
        neg_half = sb("neg_half", [P, B])
        rmax = sb("rmax", [P, 2, CH])
        rinv = sb("rinv", [P, HEADS])
        route = sb("route", [P, 3, B, E])
        route_b = sb("route_b", [P, 8, B])
        zeros = sb("zeros", [P, D])
        tri = sb("tri", [P, P], BF16)
        ones = sb("ones", [P, P], BF16)
        route_mask_bf = sb("route_mask_bf", [P, B, E], BF16)
        rev_e = sb("rev_e", [P, B, E])
        dump = sb("dump", [P, B])
        slot_u = sb("slot_u", [P, B], U32)
        take_u = sb("take_u", [P, B], U32)

        wk = arena[:, 8:10, :].rearrange("p a (x k d) -> p a x k d", x=NH, k=K)
        dt_rows = arena[:, 8:10, :]
        ctxT = arena[:, 10, :]
        dA = [[arena[:, 2 * (g % 2) + h, :] for h in range(NH)] for g in range(2)]
        dBx = [[arena[:, 4 + 2 * (g % 2) + h, :] for h in range(NH)] for g in range(2)]
        hs = [[arena[:, 8 + 2 * (g % 2) + h, :] for h in range(NH)] for g in range(2)]
        rests = arena[0:3 * NB, 11, :]
        yzT = arena[:, 4:6, :]
        res1 = arena[:, 8, :].rearrange("p (b d) -> p b d", b=B)
        x1T = arena[:, 9, :]
        qT = arena[:, 10, :]
        prob = [arena[:, c, :].rearrange("p (h k) -> p h k", h=CH) for c in range(2)]
        probT = [arena[:, 2 + c, :].rearrange("p (h k) -> p h k", h=CH) for c in range(2)]
        attn = arena[:, 6, :].rearrange("p (b d) -> p b d", b=B)
        attnT = arena[:, 7, :].rearrange("p (b d) -> p b d", b=B)
        res2 = arena[:, 8, :].rearrange("p (b d) -> p b d", b=B)
        x2T = arena[:, 9, :]
        xe = arena[:, 0:2, :].rearrange("p a t -> p (a t)")[:, 0:SLOTS].rearrange("p (j d) -> p j d", j=ST)
        xeT = arena[:, 2:4, :].rearrange("p a t -> p (a t)")[:, 0:SLOTS]
        hid = [arena[:, 4 + e, 0:FC * CAP].rearrange("p (c s) -> p c s", c=FC) for e in range(2)]
        eo = arena[:, 6:8, :].rearrange("p a (e s d) -> p (a e) s d", s=2, d=D)
        back = arena[:, 10, :].rearrange("p (b d) -> p b d", b=B)
        res3 = arena[:, 8, :].rearrange("p (b d) -> p b d", b=B)
        y_out = arena[:, 11, :].rearrange("p (b d) -> p b d", b=B)
        mamba_in = [(conv_w, conv_bias, x_proj_w, dt_proj_w, dt_proj_bias, A_log, D_skip),
                    (convb_w, convb_bias, x_proj_b_w, dt_proj_b_w, dt_proj_b_bias, A_b_log, D_b_skip)]

        def col(vec, h):
            return vec_cols[:, NH * vec + h:NH * vec + h + 1]

        x_in, win_in, small_in, wout_in = sem("x_in"), sem("win_in"), sem("small_in"), sem("wout_in")
        small_gp_in = sem("small_gp_in")
        ctx_in, attn_w_in, moe_w_in = sem("ctx_in"), sem("attn_w_in"), sem("moe_w_in")
        full = [sem(f"bank{i}_full") for i in range(8)]
        read = [sem(f"bank{i}_read") for i in range(8)]
        dve, act, pool = sem("dve_steps"), sem("act_steps"), sem("pool_steps")
        ident_ok, consts_ok, dtw_ok, pads_ok = sem("ident_ok"), sem("consts_ok"), sem("dtw_ok"), sem("pads_ok")
        wk_ok, diag_ok, sel_ok, head_mask_ok = sem("wk_ok"), sem("diag_ok"), sem("sel_ok"), sem("head_mask_ok")
        dt_rows_ok, parts_ok, a_exp, a_ok = sem("dt_rows_ok"), sem("parts_ok"), sem("a_exp"), sem("a_ok")
        soft_in, delta_ok, du_ok = sem("softplus_terms"), sem("delta_ok"), sem("du_ok")
        b_bc, c_bc, b_sb = sem("b_broadcast"), sem("c_broadcast"), sem("b_in_sbuf")
        dA_ok, dBx_ok, scanned = sem("dA_ok"), sem("dBx_ok"), sem("scanned")
        hc_ok, summed, yz_ok = sem("hc_ok"), sem("summed"), sem("yz_ok")
        var_ok, rstd_ok, x1_ok, x2_ok = sem("var_ok"), sem("rstd_ok"), sem("x1_ok"), sem("x2_ok")
        exp_ok = sem("exp_ok")
        gate_d, gate_exp, route_mask = sem("gate_shifted"), sem("gate_exp"), sem("route_mask")
        slots_ok, zero_ok, dispatched, xe_in = sem("slots_ok"), sem("zero_ok"), sem("dispatched"), sem("xe_in")
        eo_out, gathered, y_ok, stored = sem("eo_out"), sem("gathered"), sem("y_ok"), sem("stored")

        plan = [("xT0", 0), ("xT1", 1), ("wkT00", 2), ("wkT01", 3), ("wz_out", 4), ("xproj", 5), ("dtw", 6),
                ("wkT10", 7), ("wkT11", 0), ("qkvo", 1)]
        plan += [(f"u0{h}{th}", 2 + 2 * h + th) for h in range(NH) for th in range(2)]
        plan += [(f"z{h}{th}", (6, 7, 0, 1)[2 * h + th]) for h in range(NH) for th in range(2)]
        plan += [(f"u1{h}{th}", 2 + 2 * h + th) for h in range(NH) for th in range(2)]
        plan += [("ctxT0", 6), ("ctxT1", 7), ("k0", 6), ("k1", 7), ("v0", 4), ("v1", 5)]
        plan += [("x0_0", 6), ("x0_1", 7)]
        plan += [(f"d0{h}{th}", 4 + 2 * h + th) for h in range(NH) for th in range(2)]
        plan += [("x1_0", 4), ("x1_1", 5)]
        plan += [(f"d1{h}{th}", (6, 7, 4, 5)[2 * h + th]) for h in range(NH) for th in range(2)]
        scan_from = len(plan)
        plan += [("o0", 4), ("o1", 5), ("x1T0", 6), ("x1T1", 7), ("q0", 4), ("q1", 5)]
        plan += [("s0", 0, 2)]
        for i in range(1, 2 * B + 6):
            if i < 2 * B:
                plan += [(f"s{i}", 2 * (i % 2), 2)]
            if i <= 2 * B:
                plan += [(f"pT{i - 1}", 4, 2)]
            if i % 2 == 1 and 3 <= i < 2 * B + 3:
                plan += [(f"av{i // 2 - 1}", 6)]
            if i % 2 == 0 and 4 <= i < 2 * B + 4:
                plan += [(f"oT{i // 2 - 2}", 7)]
            if i % 2 == 1 and 5 <= i < 2 * B + 5:
                plan += [(f"wo{i // 2 - 2}", 7)]
        plan += [("x2T0", 4), ("x2T1", 5), ("logits", 6), ("count", 7), ("xeT0", 0), ("xeT1", 1), ("xeT2", 2)]
        for e in range(E + 1):
            plan += [(f"h{e}", 2 * (e % 2), 2)] if e < E else []
            plan += [(f"eo{e - 1}", 4 + (e - 1) % 2)] if e else []
        where, before, holder, uses = {}, {}, [None] * 8, [0] * 8
        for n, (name, i, *width) in enumerate(plan):
            if n == scan_from:
                held_at_scan, holder = holder, [None] * 8
            banks = range(i, i + (width or [1])[0])
            where[name] = (i, uses[i])
            before[name] = sorted({holder[k] for k in banks} - {None})
            uses[i] += 1
            for k in banks:
                holder[k] = name

        def wait_read(eng, name):
            i, n = where[name]
            eng.wait_ge(read[i], n + 1)

        def to_fill(pe, name):
            for old in before[name]:
                wait_read(pe, old)
            return bank[:, where[name][0], :]

        def filled(name, last):
            last.then_inc(full[where[name][0]], 1)

        def to_read(eng, name):
            i, n = where[name]
            eng.wait_ge(full[i], n + 1)
            return bank[:, i, :]

        def was_read(name, last):
            last.then_inc(read[where[name][0]], 1)

        def half(th):
            return slice(TH * th, TH * th + TH)

        def group(g):
            return slice(HB * g, HB * g + HB)

        def tiles(ap, n):
            return ap.rearrange("p (a c) -> p a c", a=n)

        block = ctx.enter_context(nc.Block())

        @block.sync
        def _(sp):
            sp.dma_start(x_tok[:, :, :], x.rearrange("b s d -> s b d")).then_inc(x_in, 16)
            sp.dma_start(win, in_proj_w.rearrange("(c p) d -> p c d", p=P)).then_inc(win_in, 16)
            for dr in range(2):
                sp.dma_start(cw[:, dr, :, :],
                             mamba_in[dr][0].rearrange("(h p) a k -> p h (a k)", p=P)).then_inc(win_in, 16)
            for dr in range(2):
                _, cb, xp, _, dtb, _, dsk = mamba_in[dr]
                for v, vec in ((dr, cb), (2 + dr, dtb), (4 + dr, dsk)):
                    sp.dma_start(vec_rows[NH * v:NH * v + NH, :],
                                 vec.rearrange("(h p) -> h p", p=P)).then_inc(small_in, 16)
                sp.dma_start(xproj[:, dr, :], xp).then_inc(small_in, 16)
            sp.dma_start(wout, out_proj_w).then_inc(wout_in, 16)
            for n, w in enumerate((Wq, Wk, Wv, Wo)):
                sp.dma_start(wqkvo[:, n, :], w).then_inc(attn_w_in, 16)
            sp.dma_start(ctx_tok[:, :, :], ctx_1024.rearrange("b s d -> s b d")).then_inc(ctx_in, 16)
            sp.dma_start(gate[:, :], gate_w).then_inc(moe_w_in, 16)
            sp.dma_start(w1_sb[:, :, :], w1.rearrange("e d f -> d e f")).then_inc(moe_w_in, 16)
            sp.dma_start(w2_sb[:, :, :, :], w2.rearrange("e (c p) d -> p e c d", p=P)).then_inc(moe_w_in, 16)
            sp.wait_ge(consts_ok, 1)
            sp.dma_start(d_slots[0:SLOTS, :].rearrange("(j p) d -> p j d", p=P),
                         zeros[:, :].unsqueeze(1).to_broadcast([P, ST, D])).then_inc(zero_ok, 16)
            sp.dma_start(d_expert[SLOTS:SLOTS + P, :], zeros[:, :]).then_inc(zero_ok, 16)
            sp.wait_ge(dispatched, 16 * B)
            sp.dma_start(xe, d_slots[0:SLOTS, :].rearrange("(j p) d -> p j d", p=P)).then_inc(xe_in, 16)
            d_eo = d_expert[0:SLOTS, :].rearrange("(e s p) d -> p e s d", e=E, s=2)
            for e in range(0, E, 2):
                wait_read(sp, f"eo{e}")
                wait_read(sp, f"eo{e + 1}")
                sp.dma_start(d_eo[:, e:e + 2, :, :], eo[0:HC, e:e + 2, :, :]).then_inc(eo_out, 16)
            for g in range(2):
                sp.wait_ge(y_ok, HB * (g + 1))
                sp.dma_start(out[HB * g:HB * g + HB].rearrange("b s d -> s b d"),
                             y_out[:, group(g), :]).then_inc(stored, 16)
            sp.wait_ge(stored, 32)

        @block.gpsimd
        def _(gp):
            steps = [0]

            def link(ins):
                steps[0] += 1
                ins.then_inc(pool, 1)
                gp.wait_ge(pool, steps[0])

            link(gp.memset(ident[:, :], 0.0))
            gp.affine_select(out=ident[:, :], in_=ident[:, :], compare_op=ALU.not_equal, fill=1.0, base=0,
                             pattern=[[-1, P]], channel_multiplier=1).then_inc(ident_ok, 1)
            for dr in range(2):
                gp.dma_start(dtw[:, dr, :, DT0:XM],
                             mamba_in[dr][3].rearrange("(h p) r -> p h r", p=P)).then_inc(small_gp_in, 16)
                gp.dma_start(a_log[:, dr, :, :],
                             mamba_in[dr][5].rearrange("(h p) n -> p h n", p=P)).then_inc(small_gp_in, 16)
            gp.memset(xT[:, :, 0:PAD], 0.0).then_inc(pads_ok, 1)
            gp.memset(xT[:, :, PAD + S:SP], 0.0).then_inc(pads_ok, 1)
            gp.memset(dtw[:, :, :, 0:DT0], 0.0).then_inc(dtw_ok, 1)
            gp.memset(zeros[:, :], 0.0).then_inc(consts_ok, 1)
            gp.memset(v_ext[:, :, :, DH:DH + 1], 1.0).then_inc(consts_ok, 1)
            gp.memset(neg_half[:, :], -0.5).then_inc(consts_ok, 1)
            gp.memset(ones[:, :], 1.0).then_inc(consts_ok, 1)
            link(gp.memset(tri[:, :], 1.0))
            gp.affine_select(out=tri[:, :], in_=tri[:, :], compare_op=ALU.is_ge, fill=0.0, base=0,
                             pattern=[[1, P]], channel_multiplier=-1).then_inc(consts_ok, 1)
            gp.iota(rev_e[:, :, :], pattern=[[0, B], [-1, E]], base=E, channel_multiplier=0,
                    allow_small_or_imprecise_dtypes=True).then_inc(consts_ok, 1)
            gp.iota(dump[:, :], pattern=[[S, B]], base=SLOTS, channel_multiplier=1,
                    allow_small_or_imprecise_dtypes=True).then_inc(consts_ok, 1)
            for j in range(2 * NH):
                dr, h = j // NH, j % NH
                gp.wait_ge(delta_ok, j + 1)
                for th in range(2):
                    wait_read(gp, f"u{dr}{h}{th}")
                gp.tensor_tensor(du[:, dr, h, :], delta[:, dr, h, :], uT[:, dr, h, :], ALU.mult).then_inc(du_ok, 1)

            def dbx_step(g, slot, dr, restarts=False):
                gp.wait_ge(b_sb, g + 1)
                for h in range(NH):
                    if not isinstance(g, int) or g >= 2:
                        gp.wait_ge(scanned, NH * (g - 2) + h + 1)
                    if restarts:
                        edge = (S - 1) * dr
                        link(gp.memset(tiles(dA[slot][h], B)[:, :, edge:edge + 1], 0.0))
                    gp.tensor_tensor(dBx[slot][h], du[:, dr, h, :], b_row[:, slot, :], ALU.mult).then_inc(dBx_ok, 1)

            gp.wait_ge(du_ok, 2 * NH)
            for dr in range(2):
                for j in range(2):
                    dbx_step(N * dr + j, j, dr, restarts=True)
                with gp.Fori(1, N // 2, 1) as i:
                    for j in range(2):
                        dbx_step(N * dr + 2 * i + j, j, dr)

            def rstds(norm):
                for g in range(2):
                    gp.wait_ge(var_ok, B * norm + HB * g + HB)
                    link(gp.tensor_scalar(rstd[:, group(g)], moments[:, group(g), 1], EPS, None, ALU.add))
                    gp.tensor_tensor(rstd[:, group(g)], rstd[:, group(g)], neg_half[:, group(g)],
                                     ALU.pow).then_inc(rstd_ok, 1)

            rstds(0)
            rstds(1)
            gp.wait_ge(zero_ok, 32)
            gp.wait_ge(slots_ok, 1)
            for b in range(B):
                gp.indirect_dma_start(d_slots, bass.IndirectOffsetOnAxis(slot_u[:, b:b + 1], 0),
                                      x2[:, b, :], None).then_inc(dispatched, 16)
            gp.wait_ge(slots_ok, 2)
            gp.wait_ge(eo_out, 16 * (E // 2))
            for b in range(B):
                gp.indirect_dma_start(back[:, b, :], None, d_expert,
                                      bass.IndirectOffsetOnAxis(take_u[:, b:b + 1], 0)).then_inc(gathered, 16)
            rstds(2)

        @block.scalar
        def _(sc):
            def evacuate(name, dst, rearranged=lambda ap: ap, func=ACT.Copy, **how):
                was_read(name, sc.activation(dst, rearranged(to_read(sc, name)), func, **how))

            evacuate("xT1", xT[:, group(1), PAD:PAD + S], lambda ap: tiles(ap, HB))
            evacuate("wkT00", wkT[:, 0, 0, :, :], lambda ap: tiles(ap, K))
            src = tiles(to_read(sc, "wz_out"), 2 * NH)
            sc.activation(wzT[:, :, :], src[:, 0:NH, :], ACT.Copy)
            was_read("wz_out", sc.activation(woutT[:, :, :], src[:, NH:2 * NH, :], ACT.Copy))
            evacuate("dtw", dtT[DT0:XM, :, :, :].rearrange("p a h e -> p (a h) e"),
                     lambda ap: tiles(ap, 2 * NH)[DT0:XM, :, :])
            evacuate("wkT10", wkT[:, 1, 0, :, :], lambda ap: tiles(ap, K))
            evacuate("qkvo", qkvoT[:, :, :], lambda ap: tiles(ap, 4))

            wait_read(sc, "xproj")
            for dr in range(2):
                for h in range(NH):
                    for th in range(2):
                        evacuate(f"u{dr}{h}{th}", uT[:, dr, h, half(th)], func=ACT.Silu, bias=col(dr, h))
                if dr == 0:
                    for h in range(NH):
                        for th in range(2):
                            evacuate(f"z{h}{th}", szT[:, h, half(th)], func=ACT.Silu)
            for g in range(2):
                evacuate(f"ctxT{g}", ctxT[:, half(g)])
            for g in range(2):
                evacuate(f"v{g}", v_ext[:, group(g), :, 0:DH].rearrange("p b h e -> p (b h) e"),
                         lambda ap: tiles(ap, HB * HEADS))
            sc.wait_ge(small_gp_in, 16 * 4)
            sc.activation(a_neg[:, :, :, :], a_log[:, :, :, :], ACT.Exp).then_inc(a_exp, 1)

            for dr in range(2):
                for th in range(2):
                    sc.activation(dt_rows[DT0:XM, dr, half(th)], to_read(sc, f"x{dr}_{th}")[DT0:XM, :],
                                  ACT.Copy).then_inc(dt_rows_ok, 1)
                for h in range(NH):
                    j = NH * dr + h
                    e, relu, ln = (arena[:, 4 * (j % 2) + k, :] for k in range(3))
                    if j >= 2:
                        sc.wait_ge(delta_ok, j - 1)
                    for th in range(2):
                        name = f"d{dr}{h}{th}"
                        sc.activation(e[:, half(th)], to_read(sc, name), ACT.Abs, bias=col(2 + dr, h)).then_inc(act, 1)
                        evacuate(name, relu[:, half(th)], func=ACT.Relu, bias=col(2 + dr, h))
                    sc.wait_ge(act, 3 * j + 2)
                    sc.activation(e, e, ACT.Exp, scale=-1.0).then_inc(act, 1)
                    sc.wait_ge(act, 3 * j + 3)
                    sc.activation(ln, e, ACT.Ln, bias=1.0).then_inc(soft_in, 1)

            def scan_step(g, n, slot, dr):
                sc.wait_ge(b_bc, g + 1)
                if not isinstance(g, int) or g >= 2:
                    sc.wait_ge(dBx_ok, NH * (g - 1))
                sc.activation(b_row[:, slot, :], bank[:, 4:6, :].rearrange("p a t -> p (a t)"),
                              ACT.Copy).then_inc(b_sb, 1)
                inner = slice(1 - dr, S - dr)
                for h in range(NH):
                    if not isinstance(g, int) or g >= 2:
                        sc.wait_ge(scanned, NH * (g - 2) + h + 1)
                    sc.activation(tiles(dA[slot][h], B)[:, :, inner], tiles(delta[:, dr, h, :], B)[:, :, inner],
                                  ACT.Exp, scale=a_neg[:, dr, h, bass.ds(n, 1)]).then_inc(dA_ok, 1)

            sc.wait_ge(a_ok, 1)
            sc.wait_ge(delta_ok, 2 * NH)
            for dr in range(2):
                for j in range(2):
                    scan_step(N * dr + j, j, j, dr)
                with sc.Fori(1, N // 2, 1) as i:
                    for j in range(2):
                        scan_step(N * dr + 2 * i + j, 2 * i + j, j, dr)

            evacuate("x1T1", x1T[:, half(1)])
            for g in range(2):
                evacuate(f"q{g}", qT[:, half(g)])
            for i in range(2 * B + 1):
                if i < 2 * B:
                    wait_read(sc, f"s{i}")
                    sc.activation(prob[i % 2], prob[i % 2], ACT.Exp, scale=SCALE).then_inc(exp_ok, 1)
                if i >= 1:
                    c = i - 1
                    to_read(sc, f"pT{c}")
                    was_read(f"pT{c}", sc.activation(probT[c % 2].rearrange("p h k -> p (h k)"),
                                                     bank[:, 4:6, :].rearrange("p a t -> p (a t)"), ACT.Copy))
            evacuate("x2T1", x2T[:, half(1)])
            sc.wait_ge(gate_d, 1)
            sc.activation(route[:, 1, :, :], route[:, 0, :, :], ACT.Exp).then_inc(gate_exp, 1)
            evacuate("xeT0", xeT[:, 0:BANK])
            evacuate("xeT2", xeT[:, 2 * BANK:SLOTS], lambda ap: ap[:, 0:SLOTS - 2 * BANK])
            for e in range(E):
                to_read(sc, f"h{e}")
                if e >= 2:
                    to_read(sc, f"eo{e - 2}")
                i = where[f"h{e}"][0]
                was_read(f"h{e}", sc.activation(
                    hid[e % 2], bank[:, i:i + 2, :].rearrange("p a (c s) -> p (a c) s", c=2)[:, :, 0:CAP], ACT.Relu))

        @block.tensor
        def _(pe):
            def turn(dst, src):
                return pe.transpose(dst, src, ident[0:src.shape[0], 0:src.shape[0]])

            def turn_group(name, sources):
                dst = to_fill(pe, name)
                for n, src in enumerate(sources):
                    last = turn(dst[0:src.shape[1], src.shape[0] * n:src.shape[0] * (n + 1)], src)
                filled(name, last)

            pe.wait_ge(ident_ok, 1)
            pe.wait_ge(x_in, 16)
            for g in range(2):
                turn_group(f"xT{g}", [x_tok[:, b, :] for b in range(HB * g, HB * g + HB)])
            for h in range(NH):
                pe.wait_ge(wk_ok, K * (h + 1))
                turn_group(f"wkT0{h}", [wk[:, 0, h, k, :] for k in range(K)])
            pe.wait_ge(wout_in, 16)
            turn_group("wz_out", [win[:, NH + h, :] for h in range(NH)] + [wout[:, P * h:P * h + P] for h in range(NH)])
            pe.wait_ge(small_in, 16 * 8)
            dst = to_fill(pe, "xproj")
            for j in range(2 * NH):
                turn(dst[:, (R + NB) * j:(R + NB) * (j + 1)], xproj[:, j // NH, P * (j % NH):P * (j % NH) + P])
            filled("xproj", turn(dst[:, 256:256 + 6 * NH], vec_rows[:, :]))
            pe.wait_ge(dtw_ok, 1)
            pe.wait_ge(small_gp_in, 16 * 4)
            turn_group("dtw", [dtw[:, j // NH, j % NH, :] for j in range(2 * NH)])
            for h in range(NH):
                pe.wait_ge(wk_ok, K * (NH + h + 1))
                turn_group(f"wkT1{h}", [wk[:, 1, h, k, :] for k in range(K)])
            pe.wait_ge(attn_w_in, 64)
            turn_group("qkvo", [wqkvo[:, n, :] for n in range(4)])

            def conv(dr):
                for h in range(NH):
                    wait_read(pe, f"wkT{dr}{h}")
                    for th in range(2):
                        dst = to_fill(pe, f"u{dr}{h}{th}")
                        for k in range(K):
                            off = k if dr == 0 else 2 * PAD - k
                            last = pe.matmul(dst, wkT[:, dr, h, k, :], xT[:, group(th), off:off + S],
                                             start=(k == 0), stop=(k == K - 1))
                        filled(f"u{dr}{h}{th}", last)

            pe.wait_ge(pads_ok, 2)
            for g in range(2):
                wait_read(pe, f"xT{g}")
            conv(0)
            wait_read(pe, "wz_out")
            for h in range(NH):
                for th in range(2):
                    dst = to_fill(pe, f"z{h}{th}")
                    filled(f"z{h}{th}", pe.matmul(dst, wzT[:, h, :], xT[:, group(th), PAD:PAD + S],
                                                  start=True, stop=True))
            conv(1)
            pe.wait_ge(ctx_in, 16)
            for g in range(2):
                turn_group(f"ctxT{g}", [ctx_tok[:, b, :] for b in range(HB * g, HB * g + HB)])
            wait_read(pe, "qkvo")
            for g in range(2):
                wait_read(pe, f"ctxT{g}")
                dst = to_fill(pe, f"k{g}")
                filled(f"k{g}", pe.matmul(dst, qkvoT[:, 1, :], ctxT[:, half(g)], start=True, stop=True))
            for g in range(2):
                dst = to_fill(pe, f"v{g}")
                for b in range(HB):
                    t0 = TH * g + S * b
                    last = pe.matmul(dst[:, D * b:D * b + D], ctxT[:, t0:t0 + S], qkvoT[:, 2, :],
                                     start=True, stop=True)
                filled(f"v{g}", last)
            pe.wait_ge(diag_ok, 1)
            for name in held_at_scan[0:4]:
                wait_read(pe, name)
            for h in range(NH):
                for th in range(2):
                    for dr in range(2):
                        wait_read(pe, f"u{dr}{h}{th}")
                        pe.matmul(bank[:, 2 * h + th, :], diag_d[:, dr, h, :], uT[:, dr, h, half(th)],
                                  start=(dr == 0), stop=False, skip_group_check=True)

            wait_read(pe, "xproj")
            wait_read(pe, "dtw")
            for dr in range(2):
                for th in range(2):
                    dst = to_fill(pe, f"x{dr}_{th}")
                    for h in range(NH):
                        last = pe.matmul(dst[0:XM, :], xprojT[:, dr, h, :], uT[:, dr, h, half(th)],
                                         start=(h == 0), stop=(h == NH - 1))
                    filled(f"x{dr}_{th}", last)
                for h in range(NH):
                    for th in range(2):
                        pe.wait_ge(dt_rows_ok, 2 * dr + th + 1)
                        dst = to_fill(pe, f"d{dr}{h}{th}")
                        filled(f"d{dr}{h}{th}",
                               pe.matmul(dst, dtT[DT0:XM, dr, h, :], dt_rows[DT0:XM, dr, half(th)],
                                         start=True, stop=True))

            def to_all(dr, row, b0, done):
                for th in range(2):
                    last = pe.matmul(bank[:, b0 + th, :], sel[:, bass.ds(row, 1), :].rearrange("p a m -> p (a m)"),
                                     parts[:, dr, half(th)], start=True, stop=True)
                last.then_inc(done, 1)

            def add_up(g, slot, h):
                pe.wait_ge(hc_ok, NH * g + h + 1)
                for th in range(2):
                    last = pe.matmul(bank[:, 2 * h + th, :], ident[:, :], hs[slot][h][:, half(th)],
                                     start=False, stop=False, skip_group_check=True)
                last.then_inc(summed, 1)

            def scan_step(g, slot, b_ahead, c_ahead):
                if b_ahead:
                    pe.wait_ge(b_sb, g + 2)
                    to_all(b_ahead[0], b_ahead[1], 4, b_bc)
                add_up(g, slot, 0)
                pe.wait_ge(hc_ok, NH * g + NH)
                if c_ahead:
                    to_all(c_ahead[0], N + c_ahead[1], 6, c_bc)
                add_up(g, slot, 1)

            pe.wait_ge(sel_ok, 1)
            pe.wait_ge(parts_ok, 2)
            for name in held_at_scan[4:8]:
                wait_read(pe, name)
            to_all(0, 0, 4, b_bc)
            to_all(0, N, 6, c_bc)
            pe.wait_ge(b_sb, 1)
            to_all(0, 1, 4, b_bc)
            for dr in range(2):
                for j in range(2):
                    scan_step(N * dr + j, j, (dr, j + 2), (dr, j + 1))
                with pe.Fori(1, N // 2 - 1, 1) as i:
                    for j in range(2):
                        scan_step(N * dr + 2 * i + j, j, (dr, 2 * i + j + 2), (dr, 2 * i + j + 1))
                for j in range(2):
                    scan_step(N * dr + N - 2 + j, j, (1, j) if dr == 0 else None,
                              (dr, N - 1) if j == 0 else (1, 0) if dr == 0 else None)

            for g in range(2):
                pe.wait_ge(yz_ok, NH * (g + 1))
                dst = to_fill(pe, f"o{g}")
                for b in range(HB):
                    t0 = TH * g + S * b
                    for h in range(NH):
                        last = pe.matmul(dst[:, D * b:D * b + D], yzT[:, h, t0:t0 + S], woutT[:, h, :],
                                         start=(h == 0), stop=(h == NH - 1))
                filled(f"o{g}", last)
            for g in range(2):
                pe.wait_ge(x1_ok, HB * (g + 1))
                turn_group(f"x1T{g}", [x1[:, b, :] for b in range(HB * g, HB * g + HB)])
            for g in range(2):
                wait_read(pe, f"x1T{g}")
                dst = to_fill(pe, f"q{g}")
                filled(f"q{g}", pe.matmul(dst, qkvoT[:, 0, :], x1T[:, half(g)], start=True, stop=True))

            def scores(i):
                b, c = i // 2, i % 2
                to_fill(pe, f"s{i}")
                for g in (2 * c, 2 * c + 1):
                    rows = slice(32 * g, 32 * g + 32)
                    last = pe.matmul(bank[:, g, :], qT[rows, S * b:S * b + S],
                                     k_maskT[rows, b, :, :].rearrange("p j k -> p (j k)"), start=True, stop=True)
                filled(f"s{i}", last)

            def turn_probs(i):
                pe.wait_ge(exp_ok, i + 1)
                to_fill(pe, f"pT{i}")
                for h in range(CH):
                    last = turn(bank[:, 4 + h // 4, S * (h % 4):S * (h % 4) + S], prob[i % 2][:, h, :])
                filled(f"pT{i}", last)

            def weigh_values(i):
                b, c = i // 2, i % 2
                wait_read(pe, f"pT{i}")
                dst = to_fill(pe, f"av{b}")
                for h in range(CH * c, CH * c + CH):
                    last = pe.matmul(dst[:, (DH + 1) * h:(DH + 1) * (h + 1)], probT[c][:, h % CH, :],
                                     v_ext[:, b, h, :], start=True, stop=True)
                if c:
                    filled(f"av{b}", last)

            pe.wait_ge(yz_ok, 2 * NH)
            for g in range(2):
                wait_read(pe, f"q{g}")
                wait_read(pe, f"k{g}")
                wait_read(pe, f"v{g}")
            pe.wait_ge(consts_ok, 7)
            scores(0)
            for i in range(1, 2 * B + 6):
                if i < 2 * B:
                    scores(i)
                if i <= 2 * B:
                    turn_probs(i - 1)
                if 2 <= i <= 2 * B + 1:
                    weigh_values(i - 2)
                if i % 2 == 0 and 4 <= i < 2 * B + 4:
                    b = i // 2 - 2
                    wait_read(pe, f"av{b}")
                    turn_group(f"oT{b}", [attn[:, b, :]])
                if i % 2 == 1 and 5 <= i < 2 * B + 5:
                    b = i // 2 - 2
                    dst = to_fill(pe, f"wo{b}")
                    filled(f"wo{b}", pe.matmul(dst[:, 0:D], attnT[:, b, :], qkvoT[:, 3, :], start=True, stop=True))

            for g in range(2):
                pe.wait_ge(x2_ok, HB * (g + 1))
                turn_group(f"x2T{g}", [x2[:, b, :] for b in range(HB * g, HB * g + HB)])
            pe.wait_ge(moe_w_in, 48)
            dst = to_fill(pe, "logits")
            for b in range(B):
                wait_read(pe, f"x2T{b // HB}")
                last = pe.matmul(dst[:, E * b:E * b + E], x2T[:, S * b:S * b + S], gate[:, :], start=True, stop=True)
            filled("logits", last)
            pe.wait_ge(route_mask, 1)
            dst = to_fill(pe, "count")
            masks = route_mask_bf[:, :, :].rearrange("p b e -> p (b e)")
            pe.matmul(dst[:, 0:B * E], tri[:, :], masks, start=True, stop=False, skip_group_check=True)
            for ago in range(1, B):
                last = pe.matmul(dst[:, E * ago:B * E], ones[:, :], masks[:, 0:E * (B - ago)],
                                 start=False, stop=(ago == B - 1), skip_group_check=True)
            filled("count", last)

            pe.wait_ge(xe_in, 16)
            for g in range(3):
                turn_group(f"xeT{g}", [xe[:, j, :] for j in range(4 * g, min(4 * g + 4, ST))])
            for g in range(3):
                wait_read(pe, f"xeT{g}")
            for e in range(E + 1):
                if e < E:
                    to_fill(pe, f"h{e}")
                    for c in range(FC):
                        at = (BANK // 2) * (c % 2)
                        last = pe.matmul(bank[:, where[f"h{e}"][0] + c // 2, at:at + CAP],
                                         w1_sb[:, e, P * c:P * c + P], xeT[:, CAP * e:CAP * e + CAP],
                                         start=True, stop=True)
                    filled(f"h{e}", last)
                if e >= 1:
                    wait_read(pe, f"h{e - 1}")
                    dst = to_fill(pe, f"eo{e - 1}")
                    for s in range(2):
                        for c in range(FC):
                            last = pe.matmul(dst[0:HC, D * s:D * s + D], hid[(e - 1) % 2][:, c, HC * s:HC * s + HC],
                                             w2_sb[:, e - 1, c, :], start=(c == 0), stop=(c == FC - 1))
                    filled(f"eo{e - 1}", last)

        @block.vector
        def _(ve):
            steps = [0]

            def link(ins):
                steps[0] += 1
                ins.then_inc(dve, 1)
                ve.wait_ge(dve, steps[0])

            def evacuate(name, dst, rearranged=lambda ap: ap):
                was_read(name, ve.tensor_copy(dst, rearranged(to_read(ve, name))))

            ve.wait_ge(win_in, 48)
            for dr in range(2):
                for h in range(NH):
                    for k in range(K):
                        ve.tensor_scalar(wk[:, dr, h, k, :], win[:, h, :], cw[:, dr, h, k:k + 1], None,
                                         ALU.mult).then_inc(wk_ok, 1)
                if dr == 0:
                    evacuate("xT0", xT[:, group(0), PAD:PAD + S], lambda ap: tiles(ap, HB))
            evacuate("wkT01", wkT[:, 0, 1, :, :], lambda ap: tiles(ap, K))
            src = to_read(ve, "xproj")
            by_j = src[:, 0:(R + NB) * 2 * NH].rearrange("p (j m) -> p j m", j=2 * NH)
            xp_j = xprojT[:, :, :, :].rearrange("p a h m -> p (a h) m")
            for r in range(3):
                ve.tensor_copy(xp_j[:, :, NB * r:NB * r + NB], by_j[:, :, R:R + NB])
            ve.tensor_copy(xp_j[:, :, DT0:XM], by_j[:, :, 0:R])
            was_read("xproj", ve.tensor_copy(vec_cols[:, :], src[:, 256:256 + 6 * NH]))
            evacuate("wkT11", wkT[:, 1, 1, :, :], lambda ap: tiles(ap, K))
            wait_read(ve, "xproj")
            for dr in range(2):
                for h in range(NH):
                    last = ve.tensor_scalar(diag_d[:, dr, h, :], ident[:, :], col(4 + dr, h), None, ALU.mult)
            last.then_inc(diag_ok, 1)
            for r in range(3):
                last = ve.tensor_copy(sel_id[NB * r:NB * r + NB, :], ident[NB * r:NB * r + NB, NB * r:NB * r + NB])
            link(last)
            ve.tensor_copy(sel[:, :, :], sel_id[:, :].unsqueeze(2).to_broadcast([3 * NB, NB, P])).then_inc(sel_ok, 1)
            link(ve.tensor_reduce(head_mask[:, :], ident[:, :].rearrange("p (g j i) -> p j g i", g=4, j=GH),
                                  AX.XY, ALU.add))
            for g in range(2):
                src = tiles(to_read(ve, f"k{g}"), HB)
                for j in range(GH):
                    last = ve.tensor_scalar(k_maskT[:, group(g), j, :], src, head_mask[:, j:j + 1], None, ALU.mult)
                was_read(f"k{g}", last)
            ve.wait_ge(a_exp, 1)
            ve.tensor_scalar(a_neg[:, :, :, :], a_neg[:, :, :, :], -1.0, None, ALU.mult).then_inc(a_ok, 1)

            def split_rows(dr):
                for th in range(2):
                    cols = half(th)
                    src = to_read(ve, f"x{dr}_{th}")
                    link(ve.tensor_copy(parts[:, dr, cols], src[0:3 * NB, :]))
                    ve.wait_ge(dt_rows_ok, 2 * dr + th + 1)
                    was_read(f"x{dr}_{th}", ve.tensor_tensor(rests[0:2 * NB, cols], src[0:2 * NB, :],
                                                             parts[0:2 * NB, dr, cols], ALU.subtract))
                    wait_read(ve, f"x{dr}_{th}")
                    link(ve.tensor_copy(parts[0:2 * NB, dr, cols], rests[0:2 * NB, cols]))
                    link(ve.tensor_tensor(rests[0:NB, cols], rests[0:NB, cols], parts[0:NB, dr, cols], ALU.subtract))
                    last = ve.tensor_copy(parts[0:NB, dr, cols], rests[0:NB, cols])
                last.then_inc(parts_ok, 1)

            def softplus(dr):
                for h in range(NH):
                    j = NH * dr + h
                    ve.wait_ge(soft_in, j + 1)
                    e, relu, ln, t = (arena[:, 4 * (j % 2) + k, :] for k in range(4))
                    if j >= 2:
                        ve.wait_ge(delta_ok, j - 1)
                    link(ve.tensor_scalar(t, e, 1.0, -1.0, ALU.add, ALU.add))
                    link(ve.tensor_tensor(t, e, t, ALU.subtract))
                    link(ve.tensor_tensor(t, t, relu, ALU.add))
                    ve.tensor_tensor(delta[:, dr, h, :], t, ln, ALU.add).then_inc(delta_ok, 1)

            for dr in range(2):
                if dr:
                    ve.wait_ge(parts_ok, 1)
                split_rows(dr)
                softplus(dr)

            def scan_step(g, slot, dr):
                for h in range(NH):
                    ve.wait_ge(dA_ok, NH * g + h + 1)
                    ve.wait_ge(dBx_ok, NH * g + h + 1)
                    if not isinstance(g, int) or g >= 2:
                        ve.wait_ge(summed, NH * (g - 2) + h + 1)
                    o, a, v = hs[slot][h], dA[slot][h], dBx[slot][h]
                    if dr:
                        o, a, v = o[:, ::-1], a[:, ::-1], v[:, ::-1]
                    ve.tensor_tensor_scan(o, a, v, 0.0, ALU.mult, ALU.add).then_inc(scanned, 1)
                ve.wait_ge(c_bc, g + 1)
                for h in range(NH):
                    ve.wait_ge(scanned, NH * g + h + 1)
                    ve.tensor_tensor(hs[slot][h], hs[slot][h], bank[:, 6:8, :].rearrange("p a t -> p (a t)"),
                                     ALU.mult).then_inc(hc_ok, 1)

            for dr in range(2):
                for j in range(2):
                    scan_step(N * dr + j, j, dr)
                with ve.Fori(1, N // 2, 1) as i:
                    for j in range(2):
                        scan_step(N * dr + 2 * i + j, j, dr)

            ve.wait_ge(summed, 2 * NH * N)
            for th in range(2):
                for h in range(NH):
                    wait_read(ve, f"z{h}{th}")
                    ve.tensor_tensor(yzT[:, h, half(th)], bank[:, 2 * h + th, :], szT[:, h, half(th)],
                                     ALU.mult).then_inc(yz_ok, 1)

            def moments_of(res, b):
                link(ve.bn_stats(stats[:, b, :], res[:, b, :]))
                ve.bn_aggr(moments[:, b, :], stats[:, b, :]).then_inc(var_ok, 1)

            def normalize(res, dst, norm, g, done):
                ve.wait_ge(rstd_ok, 2 * norm + g + 1)
                for b in range(HB * g, HB * g + HB):
                    ve.tensor_scalar(dst[:, b, :], res[:, b, :], moments[:, b, 0:1], rstd[:, b:b + 1],
                                     ALU.subtract, ALU.mult).then_inc(done, 1)

            for g in range(2):
                src = tiles(to_read(ve, f"o{g}"), HB)
                was_read(f"o{g}", ve.tensor_tensor(res1[:, group(g), :], src, x_tok[:, group(g), :], ALU.add))
                wait_read(ve, f"o{g}")
                for b in range(HB * g, HB * g + HB):
                    moments_of(res1, b)
            for g in range(2):
                normalize(res1, x1, 0, g, x1_ok)
            evacuate("x1T0", x1T[:, half(0)])

            def shift_scores(i):
                c = i % 2
                to_read(ve, f"s{i}")
                src = bank[:, 2 * c:2 * c + 2, :].rearrange("p a (j k) -> p (a j) k", j=GH)
                if i >= 2:
                    to_read(ve, f"pT{i - 2}")
                    wait_read(ve, f"s{i - 2}")
                link(ve.tensor_reduce(rmax[:, c, :], src, AX.X, ALU.max))
                was_read(f"s{i}", ve.tensor_tensor(prob[c], src, rmax[:, c, :].unsqueeze(2).to_broadcast([P, CH, S]),
                                                   ALU.subtract))

            def normalize_heads(b):
                o = to_read(ve, f"av{b}")[:, 0:HEADS * (DH + 1)].rearrange("p (h e) -> p h e", h=HEADS)
                link(ve.reciprocal(rinv[:, :].unsqueeze(2), o[:, :, DH:DH + 1]))
                was_read(f"av{b}", ve.tensor_tensor(
                    attn[:, b, :].rearrange("p (h e) -> p h e", h=HEADS), o[:, :, 0:DH],
                    rinv[:, :].unsqueeze(2).to_broadcast([P, HEADS, DH]), ALU.mult))

            for i in range(2 * B + 6):
                if i < 2 * B:
                    shift_scores(i)
                if i % 2 == 1 and 3 <= i < 2 * B + 3:
                    normalize_heads(i // 2 - 1)
                if i % 2 == 0 and 4 <= i < 2 * B + 4:
                    b = i // 2 - 2
                    evacuate(f"oT{b}", attnT[:, b, :], lambda ap: ap[:, 0:P])
                if i % 2 == 1 and 5 <= i < 2 * B + 5:
                    b = i // 2 - 2
                    src = to_read(ve, f"wo{b}")
                    was_read(f"wo{b}", ve.tensor_tensor(res2[:, b, :], src[:, 0:D], x1[:, b, :], ALU.add))
                    wait_read(ve, f"wo{b}")
                    moments_of(res2, b)
                if i == 2 * HB + 5:
                    normalize(res2, x2, 1, 0, x2_ok)
            normalize(res2, x2, 1, 1, x2_ok)
            evacuate("x2T0", x2T[:, half(0)])

            top, chosen, total, prob_top, place, fits, slot, take = (route_b[:, k, :] for k in range(8))

            def over_e(ap):
                return ap.unsqueeze(2).to_broadcast([P, B, E])

            logits = to_read(ve, "logits")[:, 0:B * E].rearrange("p (b e) -> p b e", b=B)
            link(ve.tensor_reduce(top, logits, AX.X, ALU.max))
            ve.tensor_tensor(route[:, 0, :, :], logits, over_e(top), ALU.subtract).then_inc(gate_d, 1)
            link(ve.tensor_tensor(route[:, 2, :, :], logits, over_e(top), ALU.is_ge))
            link(ve.tensor_tensor(route[:, 2, :, :], route[:, 2, :, :], rev_e[:, :, :], ALU.mult))
            link(ve.tensor_reduce(chosen, route[:, 2, :, :], AX.X, ALU.max))
            ve.tensor_tensor(route_mask_bf[:, :, :], rev_e[:, :, :], over_e(chosen), ALU.is_equal).then_inc(route_mask, 1)
            ve.wait_ge(gate_exp, 1)
            link(ve.tensor_reduce(total, route[:, 1, :, :], AX.X, ALU.add))
            ve.reciprocal(prob_top, total)
            ve.wait_ge(route_mask, 1)
            counts = to_read(ve, "count")[:, 0:B * E].rearrange("p (b e) -> p b e", b=B)
            link(ve.tensor_tensor(route[:, 2, :, :], counts, route_mask_bf[:, :, :], ALU.mult))
            link(ve.tensor_reduce(place, route[:, 2, :, :], AX.X, ALU.add))
            ve.tensor_scalar(fits, place, float(CAP), None, ALU.is_le)
            link(ve.scalar_tensor_tensor(slot, chosen, -float(CAP), place, ALU.mult, ALU.add))
            link(ve.tensor_scalar(take, slot, float(CAP * E - 1 - SLOTS), None, ALU.add))
            link(ve.tensor_tensor(take, take, fits, ALU.mult))
            link(ve.tensor_scalar(slot, slot, float(CAP * E - 1), None, ALU.add))
            link(ve.tensor_tensor(slot, slot, dump[:, :], ALU.subtract))
            link(ve.tensor_tensor(slot, slot, fits, ALU.mult))
            link(ve.tensor_tensor(slot, slot, dump[:, :], ALU.add))
            ve.tensor_copy(slot_u[:, :], slot).then_inc(slots_ok, 1)
            link(ve.tensor_scalar(take, take, float(SLOTS), None, ALU.add))
            link(ve.tensor_tensor(prob_top, prob_top, fits, ALU.mult))
            ve.tensor_copy(take_u[:, :], take).then_inc(slots_ok, 1)

            evacuate("xeT1", xeT[:, BANK:2 * BANK])
            for e in range(E):
                evacuate(f"eo{e}", eo[0:HC, e, :, :], lambda ap: ap[0:HC, 0:2 * D].rearrange("p (s d) -> p s d", s=2))

            for b in range(B):
                ve.wait_ge(gathered, 16 * B)
                link(ve.scalar_tensor_tensor(res3[:, b, :], back[:, b, :], prob_top[:, b:b + 1], x2[:, b, :],
                                             ALU.mult, ALU.add))
                moments_of(res3, b)
            for g in range(2):
                normalize(res3, y_out, 2, g, y_ok)


_INS = ["x", "ctx_1024", "L0_attn_in_proj_w", "L0_attn_conv_w", "L0_attn_conv_bias", "L0_attn_x_proj_w",
        "L0_attn_dt_proj_w", "L0_attn_dt_proj_bias", "L0_attn_A_log", "L0_attn_D_skip", "L0_attn_convb_w",
        "L0_attn_convb_bias", "L0_attn_x_proj_b_w", "L0_attn_dt_proj_b_w", "L0_attn_dt_proj_b_bias",
        "L0_attn_A_b_log", "L0_attn_D_b_skip", "L0_attn_out_proj_w", "L0_xattn_Wq", "L0_xattn_Wk", "L0_xattn_Wv",
        "L0_xattn_Wo", "L0_ffn_gate_w", "L0_ffn_w1", "L0_ffn_w2"]


def kernel(**inputs):
    import numpy as _np
    import concourse.bacc as _bacc
    from concourse import mybir as _mybir
    from concourse.bass_utils import run_bass_kernel_spmd as _run

    nc = _bacc.Bacc("TRN2", target_bir_lowering=False, num_devices=1)
    arrays, args = {}, []
    for name in _INS:
        a = _np.ascontiguousarray(inputs[name])
        arrays[f"in_{name}"] = a
        args.append(nc.dram_tensor(f"in_{name}", a.shape, _mybir.dt.from_np(a.dtype), kind="ExternalInput").ap())
    shape = inputs["x"].shape
    args.append(nc.dram_tensor("out_0", shape, _mybir.dt.from_np(_np.dtype("float32")), kind="ExternalOutput").ap())
    decoder_layer_kernel(nc, *args)
    r = _run(nc, [arrays], core_ids=[0])
    return r.results[0]["out_0"]
```

```python
from contextlib import ExitStack

import concourse.bass as bass
from concourse import mybir

F32 = mybir.dt.float32
BF16 = mybir.dt.bfloat16
U32 = mybir.dt.uint32
ALU = mybir.AluOpType
ACT = mybir.ActivationFunctionType
AX = mybir.AxisListType
P = 128
BANK = 512
EPS = 1e-5


def decoder_layer_kernel(nc, x, ctx_1024, in_proj_w, conv_w, conv_bias, x_proj_w, dt_proj_w, dt_proj_bias,
                         A_log, D_skip, convb_w, convb_bias, x_proj_b_w, dt_proj_b_w, dt_proj_b_bias,
                         A_b_log, D_b_skip, out_proj_w, Wq, Wk, Wv, Wo, gate_w, w1, w2, out):
    B, S, D = x.shape
    T = B * S
    TH = T // 2
    HB = B // 2
    DI = in_proj_w.shape[0] // 2
    NH = DI // P
    N = A_log.shape[1]
    R = dt_proj_w.shape[1]
    K = conv_w.shape[2]
    PAD = K - 1
    SP = S + 2 * PAD
    B3, C0, DT0 = 3 * N, 64, 96
    XM = DT0 + R
    VB = 6
    HEADS = 16
    DH = D // HEADS
    GH = 4
    CH = 8
    LAST = 2 * B + 6
    E = gate_w.shape[1]
    F = w1.shape[2]
    FC = F // P
    CAP = 160
    HC = CAP // 2
    SLOTS = E * CAP
    ST = SLOTS // P
    SCALE = float(DH) ** -0.5
    assert S == P and D == P and TH == BANK and NH == 2 and CH * S == 2 * BANK

    d_slots = nc.dram_tensor("dispatched_tokens", (SLOTS + T, D), F32).ap()
    d_expert = nc.dram_tensor("expert_outputs", (SLOTS + P, D), F32).ap()

    with ExitStack() as ctx:
        def sb(name, shape, dt=F32):
            return ctx.enter_context(nc.sbuf_tensor(name, shape, dt))

        def sem(name):
            return ctx.enter_context(nc.semaphore(name))

        bank = ctx.enter_context(nc.psum_tensor("bank", [P, 8, BANK], F32))

        ident = sb("ident", [P, P])
        x_tok = sb("x_tok", [P, B, D])
        ctx_tok = sb("ctx_tok", [P, B, D])
        b_row = sb("b_row", [P, 2, T])
        early = b_row[:, :, :].rearrange("p a t -> p (a t)")
        win = early[:, 0:512].rearrange("p (c d) -> p c d", c=2 * NH)
        wqkvo = early[:, 512:1024].rearrange("p (n d) -> p n d", n=4)
        wout = early[:, 1024:1280]
        xproj = early[0:R + 2 * N, 1280:1792].rearrange("p (a d) -> p a d", a=2)
        cw = sb("cw", [P, 2, NH, K])
        a_log = sb("a_log", [P, 2, NH, N])
        a_neg = sb("a_neg", [P, 2, NH, N])
        vec_rows = sb("vec_rows", [6 * NH, P])
        vec_cols = sb("vec_cols", [P, 6 * NH])
        dtw = sb("dtw", [P, 2, NH, XM])
        gate = sb("gate", [P, E])
        w1_sb = sb("w1_sb", [P, E, F])
        w2_sb = sb("w2_sb", [P, E, FC, D])

        xT = sb("xT", [P, B, SP])
        wkT = sb("wkT", [P, 2, K, P])
        winT = sb("winT", [P, 2 * NH, P])
        woutT = sb("woutT", [P, NH, D])
        xprojT = sb("xprojT", [P, 2, NH, XM])
        dtT = sb("dtT", [P, 2, NH, P])
        qkvT = sb("qkvT", [P, 3, D])
        woT = sb("woT", [P, HEADS // GH, D])
        diag_d = sb("diag_d", [P, 2, NH, P])
        sel = sb("sel", [B3, N, P], BF16)
        uT = sb("uT", [P, 2, NH, T])
        szT = sb("szT", [P, NH, T])
        sel_id = sb("sel_id", [B3, N])
        parts = sb("parts", [B3, 2, T], BF16)
        rows = sb("rows", [P, T])
        c_col = sb("c_col", [P, 2, B, N])
        acc = sb("acc", [P, VB, DI])
        y_part = wkT[:, :, :, :].rearrange("p a k d -> p a (k d)")
        soft_t = sb("soft_t", [P, T])
        delta = sb("delta", [P, 2, NH, T])
        du = uT
        arena = sb("arena", [P, 12, T])
        head_mask = sb("head_mask", [P, GH])
        k_maskT = sb("k_maskT", [P, B, GH, S])
        k_flat = k_maskT[:, :, :, :].rearrange("p b j k -> p (b j k)")
        v_pad = delta[:, :, :, :].rearrange("p a h t -> p (a h t)").rearrange("p (b h e) -> p b h e", b=B, h=HEADS)
        x1 = x_tok
        x2 = ctx_tok
        stats = sb("stats", [P, B, 6])
        moments = sb("moments", [P, B, 2])
        rstd = sb("rstd", [P, B])
        neg_half = sb("neg_half", [P, B])
        soft = [[(arena[:, 3 * h, :], arena[:, 3 * h + 1, :], arena[:, 3 * h + 2, :]) for h in range(NH)],
                [(k_flat[:, 2 * T * h:2 * T * h + T], k_flat[:, 2 * T * h + T:2 * T * h + 2 * T],
                  k_flat[:, 2 * T * h:2 * T * h + T]) for h in range(NH)]]
        rmax = sb("rmax", [P, 2, CH])
        rsum = sb("rsum", [P, 2, CH])
        route = sb("route", [P, 3, B, E])
        route_b = sb("route_b", [P, 8, B])
        zeros = sb("zeros", [P, D])
        tri = sb("tri", [P, P], BF16)
        ones = sb("ones", [P, P], BF16)
        route_mask_bf = sb("route_mask_bf", [P, B, E], BF16)
        rev_e = sb("rev_e", [P, B, E])
        dump = sb("dump", [P, B])
        slot_u = sb("slot_u", [P, B], U32)
        take_u = sb("take_u", [P, B], U32)

        wk = arena[:, 8, :].rearrange("p (a k d) -> p a k d", a=2, k=K)
        u_pre = arena[:, 9:11, :]
        xi = k_flat[:, 0:NH * B * SP].rearrange("p (h b s) -> p h b s", h=NH, b=B)
        ctxT = arena[:, 10, :]
        dA = [[arena[:, 2 * (g % 2) + h, :] for h in range(NH)] for g in range(2)]
        dBx = [[arena[:, 4 + 2 * (g % 2) + h, :] for h in range(NH)] for g in range(2)]
        hs = [[arena[:, 8 + 2 * (g % 2) + h, :] for h in range(NH)] for g in range(2)]
        wo_pad = arena[:, 11, 0:BANK].rearrange("p (h e) -> p h e", h=HEADS)
        rests = soft_t[0:2 * N, :]
        y_rest = arena[:, 0, 0:BANK]
        yzT = uT[:, 0, :, :]
        res1 = arena[:, 8, :].rearrange("p (b d) -> p b d", b=B)
        x1T = arena[:, 9, :]
        qT = arena[:, 10, :]
        prob = [arena[:, c, :].rearrange("p (h k) -> p h k", h=CH) for c in range(3)]
        probT = [arena[:, 3 + c, :].rearrange("p (h k) -> p h k", h=CH) for c in range(2)]
        outT = [arena[:, 6, BANK * c:BANK * c + BANK] for c in range(2)]
        res2 = arena[:, 8, :].rearrange("p (b d) -> p b d", b=B)
        x2T = arena[:, 9, :]
        xe = arena[:, 0:2, :].rearrange("p a t -> p (a t)")[:, 0:SLOTS].rearrange("p (j d) -> p j d", j=ST)
        xeT = arena[:, 2:4, :].rearrange("p a t -> p (a t)")[:, 0:SLOTS]
        hid = [arena[:, 4 + e, 0:FC * CAP].rearrange("p (c s) -> p c s", c=FC) for e in range(2)]
        eo = arena[:, 6:8, :].rearrange("p a (e s d) -> p (a e) s d", s=2, d=D)
        back = arena[:, 10, :].rearrange("p (b d) -> p b d", b=B)
        res3 = arena[:, 8, :].rearrange("p (b d) -> p b d", b=B)
        y_out = arena[:, 11, :].rearrange("p (b d) -> p b d", b=B)
        mamba_in = [(conv_w, conv_bias, x_proj_w, dt_proj_w, dt_proj_bias, A_log, D_skip),
                    (convb_w, convb_bias, x_proj_b_w, dt_proj_b_w, dt_proj_b_bias, A_b_log, D_b_skip)]

        def col(vec, h):
            return vec_cols[:, NH * vec + h:NH * vec + h + 1]

        x_in, win_in, small_in, wout_in = sem("x_in"), sem("win_in"), sem("small_in"), sem("wout_in")
        conv_w_in, small_gp_in = sem("conv_w_in"), sem("small_gp_in")
        ctx_in, attn_w_in, moe_w_in = sem("ctx_in"), sem("attn_w_in"), sem("moe_w_in")
        full = [sem(f"bank{i}_full") for i in range(8)]
        read = [sem(f"bank{i}_read") for i in range(8)]
        dve, act, pool = sem("dve_steps"), sem("act_steps"), sem("pool_steps")
        ident_ok, consts_ok, dtw_ok, pads_ok = sem("ident_ok"), sem("consts_ok"), sem("dtw_ok"), sem("pads_ok")
        wk_ok, diag_ok, sel_ok, head_mask_ok = sem("wk_ok"), sem("diag_ok"), sem("sel_ok"), sem("head_mask_ok")
        dt_rows_ok, parts_ok, a_exp, a_ok = sem("dt_rows_ok"), sem("parts_ok"), sem("a_exp"), sem("a_ok")
        xpad_ok, conv_ok, silu_ok, e_used = sem("xproj_pad_ok"), sem("conv_ok"), sem("silu_ok"), sem("e_used")
        soft_in, delta_ok, du_ok = sem("softplus_terms"), sem("delta_ok"), sem("du_ok")
        b_bc, b_sb = sem("b_broadcast"), sem("b_in_sbuf")
        u_used = sem("u_used")
        dA_ok, dBx_ok, scanned = sem("dA_ok"), sem("dBx_ok"), sem("scanned")
        turned, acc_ok, part_ok, added = sem("turned"), sem("acc_ok"), sem("y_part_ok"), sem("added")
        var_ok, rstd_ok, x1_ok, x2_ok = sem("var_ok"), sem("rstd_ok"), sem("x1_ok"), sem("x2_ok")
        exp_ok, sums_ok, prob_ok = sem("exp_ok"), sem("sums_ok"), sem("prob_ok")
        av_half = sem("av_half")
        wo_pad_ok, v_zero = sem("wo_pad_ok"), sem("v_zero")
        gate_d, gate_exp, route_mask = sem("gate_shifted"), sem("gate_exp"), sem("route_mask")
        slots_ok, zero_ok, dispatched, xe_in = sem("slots_ok"), sem("zero_ok"), sem("dispatched"), sem("xe_in")
        eo_out, gathered, y_ok, stored = sem("eo_out"), sem("gathered"), sem("y_ok"), sem("stored")

        plan = [("xT0", 0), ("xT1", 1), ("winT", 2), ("wkT0", 3)]
        plan += [(f"xi{h}{th}", 2 * h + th) for h in range(NH) for th in range(2)]
        plan += [("u0_0", 4), ("u0_1", 5), ("xproj", 6), ("dtw", 7), ("wkT1", 0), ("woutT", 1), ("qkv", 2), ("woT", 4)]
        plan += [("z00", 3), ("z01", 6), ("z10", 7), ("z11", 0), ("x0_0", 2), ("x0_1", 3), ("c0", 7)]
        plan += [(f"d0{h}{th}", 2 * h + th) for h in range(NH) for th in range(2)]
        plan += [("skip0_0", 7), ("skip0_1", 4), ("skip0_2", 5), ("y_rest", 6), ("u1_0", 0), ("u1_1", 1)]
        scan_from = len(plan)
        plan += [("skip1_0", 7), ("skip1_1", 7), ("skip1_2", 7), ("x1_0", 7), ("x1_1", 7), ("c1", 7)]
        plan += [(f"d1{h}{th}", 7) for h in range(NH) for th in range(2)]
        plan += [(f"yT{h}{th}", 2 * th + h) for th in range(2) for h in range(NH)]
        plan += [("ctxT0", 6), ("ctxT1", 7)]
        plan += [("o0", 4), ("o1", 5), ("k0", 0), ("k1", 1), ("v0", 2), ("v1", 3)]
        plan += [("x1T0", 6), ("x1T1", 7), ("q0", 4), ("q1", 5)]
        plan += [("s0", 0, 2)]
        for i in range(LAST):
            if i + 1 < 2 * B:
                plan += [(f"s{i + 1}", 2 * ((i + 1) % 2), 2)]
            if 2 <= i < 2 * B + 2:
                plan += [(f"pT{i - 2}", 4, 2)]
            if i % 2 == 0 and 4 <= i < 2 * B + 4:
                plan += [(f"av{i // 2 - 2}", 6)]
            if i % 2 == 1 and 5 <= i < 2 * B + 5:
                plan += [(f"wo{i // 2 - 2}", 7)]
        plan += [("x2T0", 4), ("x2T1", 5), ("logits", 6), ("count", 7), ("xeT0", 0), ("xeT1", 1), ("xeT2", 2)]
        for e in range(E + 1):
            plan += [(f"h{e}", 2 * (e % 2), 2)] if e < E else []
            plan += [(f"eo{e - 1}", 4 + (e - 1) % 2)] if e else []
        where, before, holder, uses = {}, {}, [None] * 8, [0] * 8
        for n, (name, i, *width) in enumerate(plan):
            if n == scan_from:
                held_at_scan, holder = holder[0:6], [None] * 6 + holder[6:8]
            banks = range(i, i + (width or [1])[0])
            where[name] = (i, uses[i])
            before[name] = sorted({holder[k] for k in banks} - {None})
            uses[i] += 1
            for k in banks:
                holder[k] = name

        def wait_read(eng, name):
            i, n = where[name]
            eng.wait_ge(read[i], n + 1)

        def to_fill(pe, name):
            for old in before[name]:
                wait_read(pe, old)
            return bank[:, where[name][0], :]

        def filled(name, last):
            last.then_inc(full[where[name][0]], 1)

        def to_read(eng, name):
            i, n = where[name]
            eng.wait_ge(full[i], n + 1)
            return bank[:, i, :]

        def was_read(name, last):
            last.then_inc(read[where[name][0]], 1)

        SOFT_STEPS = ((9, 11), (10, 12), (13, 14), (14, 15))

        def half(th):
            return slice(TH * th, TH * th + TH)

        def group(g):
            return slice(HB * g, HB * g + HB)

        def tiles(ap, n):
            return ap.rearrange("p (a c) -> p a c", a=n)

        block = ctx.enter_context(nc.Block())

        @block.sync
        def _(sp):
            sp.dma_start(x_tok[:, :, :], x.rearrange("b s d -> s b d")).then_inc(x_in, 16)
            sp.dma_start(win, in_proj_w.rearrange("(c p) d -> p c d", p=P)).then_inc(win_in, 16)
            for dr in range(2):
                sp.dma_start(cw[:, dr, :, :],
                             mamba_in[dr][0].rearrange("(h p) a k -> p h (a k)", p=P)).then_inc(conv_w_in, 16)
            for dr in range(2):
                _, cb, xp, _, dtb, _, dsk = mamba_in[dr]
                for v, vec in ((dr, cb), (2 + dr, dtb), (4 + dr, dsk)):
                    sp.dma_start(vec_rows[NH * v:NH * v + NH, :],
                                 vec.rearrange("(h p) -> h p", p=P)).then_inc(small_in, 16)
                sp.dma_start(xproj[:, dr, :], xp).then_inc(small_in, 16)
            sp.dma_start(wout, out_proj_w).then_inc(wout_in, 16)
            for n, w in enumerate((Wq, Wk, Wv, Wo)):
                sp.dma_start(wqkvo[:, n, :], w).then_inc(attn_w_in, 16)
            sp.dma_start(ctx_tok[:, :, :], ctx_1024.rearrange("b s d -> s b d")).then_inc(ctx_in, 16)
            sp.dma_start(gate[:, :], gate_w).then_inc(moe_w_in, 16)
            sp.dma_start(w1_sb[:, :, :], w1.rearrange("e d f -> d e f")).then_inc(moe_w_in, 16)
            sp.dma_start(w2_sb[:, :, :, :], w2.rearrange("e (c p) d -> p e c d", p=P)).then_inc(moe_w_in, 16)
            sp.wait_ge(consts_ok, 1)
            sp.dma_start(d_slots[0:SLOTS, :].rearrange("(j p) d -> p j d", p=P),
                         zeros[:, :].unsqueeze(1).to_broadcast([P, ST, D])).then_inc(zero_ok, 16)
            sp.dma_start(d_expert[SLOTS:SLOTS + P, :], zeros[:, :]).then_inc(zero_ok, 16)
            sp.wait_ge(dispatched, 16 * B)
            sp.dma_start(xe, d_slots[0:SLOTS, :].rearrange("(j p) d -> p j d", p=P)).then_inc(xe_in, 16)
            d_eo = d_expert[0:SLOTS, :].rearrange("(e s p) d -> p e s d", e=E, s=2)
            for e in range(0, E, 2):
                wait_read(sp, f"eo{e}")
                wait_read(sp, f"eo{e + 1}")
                sp.dma_start(d_eo[:, e:e + 2, :, :], eo[0:HC, e:e + 2, :, :]).then_inc(eo_out, 16)
            for g in range(2):
                sp.wait_ge(y_ok, HB * (g + 1))
                sp.dma_start(out[HB * g:HB * g + HB].rearrange("b s d -> s b d"),
                             y_out[:, group(g), :]).then_inc(stored, 16)
            sp.wait_ge(stored, 32)

        @block.gpsimd
        def _(gp):
            steps = [0]

            def link(ins):
                steps[0] += 1
                ins.then_inc(pool, 1)
                gp.wait_ge(pool, steps[0])

            link(gp.memset(ident[:, :], 0.0))
            gp.affine_select(out=ident[:, :], in_=ident[:, :], compare_op=ALU.not_equal, fill=1.0, base=0,
                             pattern=[[-1, P]], channel_multiplier=1).then_inc(ident_ok, 1)
            for dr in range(2):
                gp.dma_start(dtw[:, dr, :, DT0:XM],
                             mamba_in[dr][3].rearrange("(h p) r -> p h r", p=P)).then_inc(small_gp_in, 16)
                gp.dma_start(a_log[:, dr, :, :],
                             mamba_in[dr][5].rearrange("(h p) n -> p h n", p=P)).then_inc(small_gp_in, 16)
            gp.memset(xT[:, :, 0:PAD], 0.0).then_inc(pads_ok, 1)
            gp.memset(xT[:, :, PAD + S:SP], 0.0).then_inc(pads_ok, 1)
            gp.memset(dtw[:, :, :, 0:DT0], 0.0).then_inc(dtw_ok, 1)
            gp.memset(xi[:, :, :, 0:PAD], 0.0).then_inc(pads_ok, 1)
            gp.memset(xi[:, :, :, PAD + S:SP], 0.0).then_inc(pads_ok, 1)
            gp.memset(xprojT[:, :, :, :], 0.0).then_inc(xpad_ok, 1)
            link(gp.memset(wo_pad, 0.0))
            gp.wait_ge(attn_w_in, 64)
            gp.tensor_copy(wo_pad[:, :, 0:DH], wqkvo[:, 3, :].rearrange("p (h e) -> p h e", h=HEADS)).then_inc(wo_pad_ok, 1)
            gp.memset(zeros[:, :], 0.0).then_inc(consts_ok, 1)
            gp.memset(neg_half[:, :], -0.5).then_inc(consts_ok, 1)
            gp.memset(ones[:, :], 1.0).then_inc(consts_ok, 1)
            link(gp.memset(tri[:, :], 1.0))
            gp.affine_select(out=tri[:, :], in_=tri[:, :], compare_op=ALU.is_ge, fill=0.0, base=0,
                             pattern=[[1, P]], channel_multiplier=-1).then_inc(consts_ok, 1)
            gp.iota(rev_e[:, :, :], pattern=[[0, B], [-1, E]], base=E, channel_multiplier=0,
                    allow_small_or_imprecise_dtypes=True).then_inc(consts_ok, 1)
            gp.iota(dump[:, :], pattern=[[S, B]], base=SLOTS, channel_multiplier=1,
                    allow_small_or_imprecise_dtypes=True).then_inc(consts_ok, 1)
            def weigh_u(dr, h):
                gp.wait_ge(delta_ok, NH * dr + h + 1)
                for th in range(2):
                    wait_read(gp, f"u{dr}_{th}")
                gp.wait_ge(silu_ok, dr + 1)
                gp.wait_ge(u_used, dr + 1)
                gp.tensor_tensor(du[:, dr, h, :], delta[:, dr, h, :], uT[:, dr, h, :], ALU.mult).then_inc(du_ok, 1)

            def dbx_step(g, slot, dr, restarts=False):
                gp.wait_ge(b_sb, g + 1)
                for h in range(NH):
                    if not isinstance(g, int) or g >= 2:
                        gp.wait_ge(scanned, NH * (g - 2) + h + 1)
                    if restarts:
                        edge = (S - 1) * dr
                        link(gp.memset(tiles(dA[slot][h], B)[:, :, edge:edge + 1], 0.0))
                    gp.tensor_tensor(dBx[slot][h], du[:, dr, h, :], b_row[:, slot, :], ALU.mult).then_inc(dBx_ok, 1)

            for h in range(NH):
                weigh_u(0, h)
            gp.wait_ge(du_ok, NH)
            for g in range(N):
                dbx_step(g, g % 2, 0, restarts=g < 2)
                if g in SOFT_STEPS[3]:
                    weigh_u(1, SOFT_STEPS[3].index(g))
            gp.wait_ge(du_ok, 2 * NH)
            for j in range(2):
                dbx_step(N + j, j, 1, restarts=True)
            with gp.Fori(1, N // 2, 1) as i:
                for j in range(2):
                    dbx_step(N + 2 * i + j, j, 1)

            def rstd_of(norm, g):
                gp.wait_ge(var_ok, B * norm + HB * g + HB)
                link(gp.tensor_scalar(rstd[:, group(g)], moments[:, group(g), 1], EPS, None, ALU.add))
                gp.tensor_tensor(rstd[:, group(g)], rstd[:, group(g)], neg_half[:, group(g)],
                                 ALU.pow).then_inc(rstd_ok, 1)

            def rstds(norm):
                for g in range(2):
                    rstd_of(norm, g)

            gp.wait_ge(dA_ok, NH * 2 * N)
            gp.memset(v_pad[:, :, :, DH:32], 0.0).then_inc(v_zero, 1)
            rstds(0)
            for i in range(2 * B):
                if i == 2 * HB + 6:
                    rstd_of(1, 0)
                gp.wait_ge(sums_ok, i + 1)
                gp.tensor_tensor(prob[i % 3], prob[i % 3], rsum[:, i % 2, :].unsqueeze(2).to_broadcast([P, CH, S]),
                                 ALU.mult).then_inc(prob_ok, 1)
            rstd_of(1, 1)
            gp.wait_ge(zero_ok, 32)
            gp.wait_ge(slots_ok, 1)
            for b in range(B):
                gp.indirect_dma_start(d_slots, bass.IndirectOffsetOnAxis(slot_u[:, b:b + 1], 0),
                                      x2[:, b, :], None).then_inc(dispatched, 16)
            gp.wait_ge(slots_ok, 2)
            gp.wait_ge(eo_out, 16 * (E // 2))
            for b in range(B):
                gp.indirect_dma_start(back[:, b, :], None, d_expert,
                                      bass.IndirectOffsetOnAxis(take_u[:, b:b + 1], 0)).then_inc(gathered, 16)
            rstds(2)

        @block.scalar
        def _(sc):
            def evacuate(name, dst, rearranged=lambda ap: ap, func=ACT.Copy, **how):
                was_read(name, sc.activation(dst, rearranged(to_read(sc, name)), func, **how))

            evacuate("xT1", xT[:, group(1), PAD:PAD + S], lambda ap: tiles(ap, HB))
            evacuate("winT", winT[:, :, :], lambda ap: tiles(ap, 2 * NH))
            evacuate("wkT0", wkT[:, 0, :, :], lambda ap: tiles(ap, K))
            for h in (1, 0):
                for th in range(2):
                    evacuate(f"xi{h}{th}", xi[:, h, group(th), PAD:PAD + S], lambda ap: tiles(ap, HB))
            evacuate("dtw", dtT[DT0:XM, :, :, :].rearrange("p a h e -> p (a h) e"),
                     lambda ap: tiles(ap, 2 * NH)[DT0:XM, :, :])

            def silu_u(dr):
                for th in range(2):
                    evacuate(f"u{dr}_{th}", uT[:, dr, 0, half(th)], func=ACT.Silu, bias=col(dr, 0))
                sc.wait_ge(conv_ok, dr + 1)
                sc.activation(uT[:, dr, 1, :], u_pre[:, dr, :], ACT.Silu, bias=col(dr, 1)).then_inc(silu_ok, 1)

            wait_read(sc, "xproj")
            silu_u(0)
            evacuate("qkv", qkvT[:, :, :], lambda ap: tiles(ap[:, 0:3 * D], 3))
            evacuate("woT", woT[:, :, :], lambda ap: tiles(ap, HEADS // GH))
            for h in range(NH):
                for th in range(2):
                    evacuate(f"z{h}{th}", szT[:, h, half(th)], func=ACT.Silu)

            def copy_rows(dr, th):
                sc.activation(rows[C0:XM, half(th)], to_read(sc, f"x{dr}_{th}")[C0:XM, :],
                              ACT.Copy).then_inc(dt_rows_ok, 1)

            def copy_c(dr):
                evacuate(f"c{dr}", c_col[:, dr, :, :], lambda ap: tiles(ap[:, 0:B * N], B))

            def abs_relu(dr, h, th):
                e, relu, _ = soft[dr][h]
                name = f"d{dr}{h}{th}"
                sc.activation(e[:, half(th)], to_read(sc, name), ACT.Abs, bias=col(2 + dr, h)).then_inc(act, 1)
                evacuate(name, relu[:, half(th)], func=ACT.Relu, bias=col(2 + dr, h))

            def exp_abs(dr, h):
                e = soft[dr][h][0]
                sc.wait_ge(act, 2 * NH * dr + 2 * h + 2)
                sc.activation(e, e, ACT.Exp, scale=-1.0).then_inc(soft_in, 1)

            def log_one_plus(dr, h):
                e, _, ln = soft[dr][h]
                sc.wait_ge(soft_in, 2 * NH * dr + NH)
                if dr:
                    sc.wait_ge(e_used, NH * dr + h + 1)
                sc.activation(ln, e, ACT.Ln, bias=1.0).then_inc(soft_in, 1)

            for th in range(2):
                copy_rows(0, th)
            copy_c(0)
            for h in range(NH):
                for th in range(2):
                    abs_relu(0, h, th)
            sc.wait_ge(small_gp_in, 16 * 4)
            sc.activation(a_neg[:, :, :, :], a_log[:, :, :, :], ACT.Exp).then_inc(a_exp, 1)
            for h in range(NH):
                exp_abs(0, h)
            for h in range(NH):
                log_one_plus(0, h)
            silu_u(1)

            def y_parts(g, n, slot, dr):
                sc.wait_ge(turned, 4 * g + 4)
                if not isinstance(g, int) or g >= 2:
                    sc.wait_ge(added, g - 1)
                for b in range(VB, B):
                    at = DI * (b - VB)
                    last = sc.activation(y_part[:, slot, at:at + DI], bank[:, 5, at:at + DI], ACT.Copy,
                                         scale=c_col[:, dr, b, bass.ds(n, 1)])
                last.then_inc(part_ok, 1)

            def scan_step(g, n, slot, dr):
                sc.wait_ge(b_bc, g + 1)
                if not isinstance(g, int) or g >= 2:
                    sc.wait_ge(dBx_ok, NH * (g - 1))
                sc.activation(b_row[:, slot, :], bank[:, 0:2, :].rearrange("p a t -> p (a t)"),
                              ACT.Copy).then_inc(b_sb, 1)
                inner = slice(1 - dr, S - dr)
                for h in range(NH):
                    if not isinstance(g, int) or g >= 2:
                        sc.wait_ge(scanned, NH * (g - 2) + h + 1)
                    sc.activation(tiles(dA[slot][h], B)[:, :, inner], tiles(delta[:, dr, h, :], B)[:, :, inner],
                                  ACT.Exp, scale=a_neg[:, dr, h, bass.ds(n, 1)]).then_inc(dA_ok, 1)

            sc.wait_ge(a_ok, 1)
            sc.wait_ge(delta_ok, NH)
            wait_read(sc, "c0")
            for g in range(N):
                scan_step(g, g, g % 2, 0)
                if g >= 2:
                    y_parts(g - 2, g - 2, g % 2, 0)
                if g in (4, 5):
                    copy_rows(1, g - 4)
                if g == 6:
                    copy_c(1)
                if 7 <= g < 11:
                    abs_relu(1, (g - 7) // 2, (g - 7) % 2)
                if g in SOFT_STEPS[0]:
                    exp_abs(1, SOFT_STEPS[0].index(g))
                if g == SOFT_STEPS[2][0]:
                    for h in range(NH):
                        log_one_plus(1, h)
            sc.wait_ge(delta_ok, 2 * NH)
            for j in range(2):
                scan_step(N + j, j, j, 1)
                y_parts(N + j - 2, N + j - 2, j, 0)
            with sc.Fori(1, N // 2, 1) as i:
                for j in range(2):
                    scan_step(N + 2 * i + j, 2 * i + j, j, 1)
                    y_parts(N + 2 * i + j - 2, 2 * i + j - 2, j, 1)
            for j in range(2):
                y_parts(2 * N - 2 + j, N - 2 + j, j, 1)

            evacuate("y_rest", y_rest)
            for g in range(2):
                evacuate(f"ctxT{g}", ctxT[:, half(g)])
            for g in range(2):
                sc.wait_ge(head_mask_ok, 1)
                src = tiles(to_read(sc, f"k{g}"), HB)
                for j in range(GH):
                    last = sc.activation(k_maskT[:, group(g), j, :], src, ACT.Copy, scale=head_mask[:, j:j + 1])
                was_read(f"k{g}", last)
            for g in range(2):
                evacuate(f"v{g}", v_pad[:, group(g), :, 0:DH].rearrange("p b h e -> p (b h) e"),
                         lambda ap: tiles(ap, HB * HEADS))
            evacuate("x1T1", x1T[:, half(1)])
            for g in range(2):
                evacuate(f"q{g}", qT[:, half(g)])
            for i in range(LAST):
                if i < 2 * B:
                    wait_read(sc, f"s{i}")
                    sc.activation(prob[i % 3], prob[i % 3], ACT.Exp, scale=SCALE).then_inc(exp_ok, 1)
                if 2 <= i < 2 * B + 2:
                    c = i - 2
                    to_read(sc, f"pT{c}")
                    if c >= 2:
                        if c % 2:
                            to_read(sc, f"av{c // 2 - 1}")
                        else:
                            sc.wait_ge(av_half, c // 2)
                    was_read(f"pT{c}", sc.activation(probT[c % 2].rearrange("p h k -> p (h k)"),
                                                     bank[:, 4:6, :].rearrange("p a t -> p (a t)"), ACT.Copy))
                if i % 2 == 0 and 4 <= i < 2 * B + 4:
                    b = i // 2 - 2
                    if b >= 2:
                        to_read(sc, f"wo{b - 2}")
                    evacuate(f"av{b}", outT[b % 2])
            evacuate("x2T1", x2T[:, half(1)])
            sc.wait_ge(gate_d, 1)
            sc.activation(route[:, 1, :, :], route[:, 0, :, :], ACT.Exp).then_inc(gate_exp, 1)
            evacuate("xeT0", xeT[:, 0:BANK])
            evacuate("xeT2", xeT[:, 2 * BANK:SLOTS], lambda ap: ap[:, 0:SLOTS - 2 * BANK])
            for e in range(E):
                to_read(sc, f"h{e}")
                if e >= 2:
                    to_read(sc, f"eo{e - 2}")
                i = where[f"h{e}"][0]
                was_read(f"h{e}", sc.activation(
                    hid[e % 2], bank[:, i:i + 2, :].rearrange("p a (c s) -> p (a c) s", c=2)[:, :, 0:CAP], ACT.Relu))

        @block.tensor
        def _(pe):
            def turn(dst, src):
                return pe.transpose(dst, src, ident[0:src.shape[0], 0:src.shape[0]])

            def turn_group(name, sources):
                dst = to_fill(pe, name)
                for n, src in enumerate(sources):
                    last = turn(dst[0:src.shape[1], src.shape[0] * n:src.shape[0] * (n + 1)], src)
                filled(name, last)

            pe.wait_ge(ident_ok, 1)
            pe.wait_ge(x_in, 16)
            for g in range(2):
                turn_group(f"xT{g}", [x_tok[:, b, :] for b in range(HB * g, HB * g + HB)])
            pe.wait_ge(win_in, 16)
            turn_group("winT", [win[:, c, :] for c in range(2 * NH)])
            pe.wait_ge(wk_ok, K)
            turn_group("wkT0", [wk[:, 0, k, :] for k in range(K)])

            pe.wait_ge(pads_ok, 4)
            for g in range(2):
                wait_read(pe, f"xT{g}")
            wait_read(pe, "winT")

            def project_in(name, c, th):
                dst = to_fill(pe, name)
                filled(name, pe.matmul(dst, winT[:, c, :], xT[:, group(th), PAD:PAD + S], start=True, stop=True))

            for h in (1, 0):
                for th in range(2):
                    project_in(f"xi{h}{th}", h, th)

            def conv(dr):
                wait_read(pe, f"wkT{dr}")
                for th in range(2):
                    dst = to_fill(pe, f"u{dr}_{th}")
                    for k in range(K):
                        off = k if dr == 0 else 2 * PAD - k
                        last = pe.matmul(dst, wkT[:, dr, k, :], xT[:, group(th), off:off + S],
                                         start=(k == 0), stop=(k == K - 1))
                    filled(f"u{dr}_{th}", last)

            conv(0)
            pe.wait_ge(small_in, 16 * 8)
            dst = to_fill(pe, "xproj")
            RX = R + 2 * N
            for j in range(2 * NH):
                turn(dst[:, RX * j:RX * (j + 1)], xproj[:, j // NH, P * (j % NH):P * (j % NH) + P])
            filled("xproj", turn(dst[:, 256:256 + 6 * NH], vec_rows[:, :]))
            pe.wait_ge(dtw_ok, 1)
            pe.wait_ge(small_gp_in, 16 * 4)
            turn_group("dtw", [dtw[:, j // NH, j % NH, :] for j in range(2 * NH)])
            pe.wait_ge(wk_ok, 2 * K)
            turn_group("wkT1", [wk[:, 1, k, :] for k in range(K)])
            pe.wait_ge(wout_in, 16)
            turn_group("woutT", [wout[:, P * h:P * h + P] for h in range(NH)])
            pe.wait_ge(attn_w_in, 64)
            turn_group("qkv", [wqkvo[:, n, :] for n in range(3)])
            pe.wait_ge(wo_pad_ok, 1)
            turn_group("woT", [wo_pad[:, GH * g:GH * g + GH, :].rearrange("p h e -> p (h e)") for g in range(HEADS // GH)])
            for h in range(NH):
                for th in range(2):
                    project_in(f"z{h}{th}", NH + h, th)

            def project_rows(dr, th):
                wait_read(pe, f"u{dr}_{th}")
                pe.wait_ge(silu_ok, dr + 1)
                dst = to_fill(pe, f"x{dr}_{th}")
                for h in range(NH):
                    last = pe.matmul(dst[0:XM, :], xprojT[:, dr, h, :], uT[:, dr, h, half(th)],
                                     start=(h == 0), stop=(h == NH - 1))
                filled(f"x{dr}_{th}", last)

            def turn_c(dr):
                pe.wait_ge(dt_rows_ok, 2 * dr + 2)
                dst = to_fill(pe, f"c{dr}")
                for b in range(B):
                    last = pe.transpose(dst[:, N * b:N * b + N], rows[C0:C0 + N, S * b:S * b + S],
                                        ident[C0:C0 + N, C0:C0 + N])
                filled(f"c{dr}", last)

            def project_delta(dr, h, th):
                pe.wait_ge(dt_rows_ok, 2 * dr + th + 1)
                dst = to_fill(pe, f"d{dr}{h}{th}")
                filled(f"d{dr}{h}{th}", pe.matmul(dst, dtT[DT0:XM, dr, h, :], rows[DT0:XM, half(th)],
                                                  start=True, stop=True))

            def skip(dr, pair):
                pe.wait_ge(diag_ok, 1)
                rest = pair == VB // 2
                if rest and dr:
                    dst = bank[:, 6, :]
                else:
                    dst = to_fill(pe, "y_rest" if rest else f"skip{dr}_{pair}")
                for n in range(2 * NH):
                    b, h = 2 * pair + n // NH, n % NH
                    last = pe.matmul(dst[:, P * n:P * n + P], uT[:, dr, h, S * b:S * b + S], diag_d[:, dr, h, :],
                                     start=(n == 0 and not (rest and dr)), stop=False, skip_group_check=True)
                if rest:
                    last.then_inc(u_used, 1)
                else:
                    filled(f"skip{dr}_{pair}", last)

            wait_read(pe, "xproj")
            wait_read(pe, "dtw")
            for th in range(2):
                project_rows(0, th)
            turn_c(0)
            for h in range(NH):
                for th in range(2):
                    project_delta(0, h, th)
            for pair in range(B // 2):
                skip(0, pair)
            conv(1)

            def to_all(dr, n, done):
                for th in range(2):
                    last = pe.matmul(bank[:, th, :], sel[:, bass.ds(n, 1), :].rearrange("p a m -> p (a m)"),
                                     parts[:, dr, half(th)], start=True, stop=True)
                last.then_inc(done, 1)

            def add_part(g, slot):
                pe.wait_ge(part_ok, g + 1)
                return pe.matmul(bank[:, 6, :], ident[:, :], y_part[:, slot, :], start=False, stop=False,
                                 skip_group_check=True)

            def scan_step(g, slot, ahead):
                static = isinstance(g, int)
                if ahead:
                    pe.wait_ge(b_sb, g + 2)
                    to_all(*ahead, b_bc)
                pe.wait_ge(scanned, NH * g + NH)
                for pair in range(B // 2):
                    if not static or g >= 1:
                        if pair < VB // 2:
                            pe.wait_ge(acc_ok, VB * (g - 1) + 2 * pair + 2)
                        else:
                            pe.wait_ge(part_ok, g)
                    for n in range(2 * NH):
                        b, h = 2 * pair + n // NH, n % NH
                        last = turn(bank[:, 2 + pair, P * n:P * n + P], hs[slot][h][:, S * b:S * b + S])
                    last.then_inc(turned, 1)
                if not static or g >= 2:
                    add_part(g - 2, slot).then_inc(added, 1)

            pe.wait_ge(sel_ok, 1)
            pe.wait_ge(parts_ok, 1)
            wait_read(pe, held_at_scan[0])
            wait_read(pe, held_at_scan[1])
            to_all(0, 0, b_bc)
            pe.wait_ge(b_sb, 1)
            to_all(0, 1, b_bc)
            for name in held_at_scan[2:6]:
                wait_read(pe, name)
            wait_read(pe, "c0")
            pieces = [lambda: skip(1, 0), lambda: skip(1, 1), lambda: (skip(1, 2), skip(1, 3)),
                      lambda: project_rows(1, 0), lambda: project_rows(1, 1), lambda: turn_c(1),
                      lambda: project_delta(1, 0, 0), lambda: project_delta(1, 0, 1),
                      lambda: project_delta(1, 1, 0), lambda: project_delta(1, 1, 1)]
            wait_read(pe, "u1_0")
            wait_read(pe, "u1_1")
            pe.wait_ge(silu_ok, 2)
            for g in range(N):
                if g == N - 2:
                    pe.wait_ge(parts_ok, 2)
                scan_step(g, g % 2, (0, g + 2) if g < N - 2 else (1, g + 2 - N))
                if g < len(pieces):
                    pieces[g]()
            with pe.Fori(0, N // 2 - 1, 1) as i:
                for j in range(2):
                    scan_step(N + 2 * i + j, j, (1, 2 * i + j + 2))
            for j in range(2):
                scan_step(2 * N - 2 + j, j, None)
            add_part(2 * N - 2, 0)
            filled("y_rest", add_part(2 * N - 1, 1))

            pe.wait_ge(b_sb, 2 * N)
            pe.wait_ge(acc_ok, VB * 2 * N)
            pe.wait_ge(part_ok, 2 * N)
            for th in range(2):
                if th:
                    wait_read(pe, "y_rest")
                for h in range(NH):
                    sources = [acc[:, b, P * h:P * h + P] if b < VB else
                               y_rest[:, DI * (b - VB) + P * h:DI * (b - VB) + P * h + P]
                               for b in range(HB * th, HB * th + HB)]
                    turn_group(f"yT{h}{th}", sources)
            pe.wait_ge(ctx_in, 16)
            for g in range(2):
                turn_group(f"ctxT{g}", [ctx_tok[:, b, :] for b in range(HB * g, HB * g + HB)])
            wait_read(pe, "woutT")
            for g in range(2):
                for h in range(NH):
                    wait_read(pe, f"yT{h}{g}")
                dst = to_fill(pe, f"o{g}")
                for b in range(HB):
                    t0 = TH * g + S * b
                    for h in range(NH):
                        last = pe.matmul(dst[:, D * b:D * b + D], yzT[:, h, t0:t0 + S], woutT[:, h, :],
                                         start=(h == 0), stop=(h == NH - 1))
                filled(f"o{g}", last)
            for g in range(2):
                wait_read(pe, f"ctxT{g}")
                dst = to_fill(pe, f"k{g}")
                filled(f"k{g}", pe.matmul(dst, qkvT[:, 1, :], ctxT[:, half(g)], start=True, stop=True))
            for g in range(2):
                dst = to_fill(pe, f"v{g}")
                for b in range(HB):
                    t0 = TH * g + S * b
                    last = pe.matmul(dst[:, D * b:D * b + D], ctxT[:, t0:t0 + S], qkvT[:, 2, :],
                                     start=True, stop=True)
                filled(f"v{g}", last)
            for g in range(2):
                pe.wait_ge(x1_ok, HB * (g + 1))
                turn_group(f"x1T{g}", [x1[:, b, :] for b in range(HB * g, HB * g + HB)])
            for g in range(2):
                wait_read(pe, f"x1T{g}")
                dst = to_fill(pe, f"q{g}")
                filled(f"q{g}", pe.matmul(dst, qkvT[:, 0, :], x1T[:, half(g)], start=True, stop=True))

            def scores(i):
                b, c = i // 2, i % 2
                to_fill(pe, f"s{i}")
                for g in (2 * c, 2 * c + 1):
                    rows = slice(32 * g, 32 * g + 32)
                    last = pe.matmul(bank[:, g, :], qT[rows, S * b:S * b + S],
                                     k_maskT[rows, b, :, :].rearrange("p j k -> p (j k)"), start=True, stop=True)
                filled(f"s{i}", last)

            def turn_probs(i):
                pe.wait_ge(prob_ok, i + 1)
                to_fill(pe, f"pT{i}")
                for h in range(CH):
                    last = turn(bank[:, 4 + h // 4, S * (h % 4):S * (h % 4) + S], prob[i % 3][:, h, :])
                filled(f"pT{i}", last)

            def weigh_values(i):
                b, c = i // 2, i % 2
                wait_read(pe, f"pT{i}")
                dst = bank[:, where[f"av{b}"][0], :] if c else to_fill(pe, f"av{b}")
                for h in range(CH * c, CH * c + CH):
                    g, j = h // GH, h % GH
                    last = pe.matmul(dst[32 * j:32 * j + 32, S * g:S * g + S], v_pad[:, b, h, :],
                                     probT[c][:, h % CH, :], start=True, stop=True)
                if not c:
                    last.then_inc(av_half, 1)
                else:
                    filled(f"av{b}", last)

            for g in range(2):
                wait_read(pe, f"q{g}")
                wait_read(pe, f"k{g}")
                wait_read(pe, f"v{g}")
            pe.wait_ge(v_zero, 1)
            scores(0)
            for i in range(LAST):
                if i + 1 < 2 * B:
                    scores(i + 1)
                if 2 <= i < 2 * B + 2:
                    turn_probs(i - 2)
                if 3 <= i < 2 * B + 3:
                    weigh_values(i - 3)
                if i % 2 == 1 and 5 <= i < 2 * B + 5:
                    b = i // 2 - 2
                    wait_read(pe, f"av{b}")
                    dst = to_fill(pe, f"wo{b}")
                    for g in range(HEADS // GH):
                        last = pe.matmul(dst[:, 0:D], outT[b % 2][:, S * g:S * g + S], woT[:, g, :],
                                         start=(g == 0), stop=(g == HEADS // GH - 1))
                    filled(f"wo{b}", last)

            for g in range(2):
                pe.wait_ge(x2_ok, HB * (g + 1))
                turn_group(f"x2T{g}", [x2[:, b, :] for b in range(HB * g, HB * g + HB)])
            pe.wait_ge(moe_w_in, 48)
            dst = to_fill(pe, "logits")
            for b in range(B):
                wait_read(pe, f"x2T{b // HB}")
                last = pe.matmul(dst[:, E * b:E * b + E], x2T[:, S * b:S * b + S], gate[:, :], start=True, stop=True)
            filled("logits", last)
            pe.wait_ge(consts_ok, 6)
            pe.wait_ge(route_mask, 1)
            dst = to_fill(pe, "count")
            masks = route_mask_bf[:, :, :].rearrange("p b e -> p (b e)")
            pe.matmul(dst[:, 0:B * E], tri[:, :], masks, start=True, stop=False, skip_group_check=True)
            for ago in range(1, B):
                last = pe.matmul(dst[:, E * ago:B * E], ones[:, :], masks[:, 0:E * (B - ago)],
                                 start=False, stop=(ago == B - 1), skip_group_check=True)
            filled("count", last)

            pe.wait_ge(xe_in, 16)
            for g in range(3):
                turn_group(f"xeT{g}", [xe[:, j, :] for j in range(4 * g, min(4 * g + 4, ST))])
            for g in range(3):
                wait_read(pe, f"xeT{g}")
            for e in range(E + 1):
                if e < E:
                    to_fill(pe, f"h{e}")
                    for c in range(FC):
                        at = (BANK // 2) * (c % 2)
                        last = pe.matmul(bank[:, where[f"h{e}"][0] + c // 2, at:at + CAP],
                                         w1_sb[:, e, P * c:P * c + P], xeT[:, CAP * e:CAP * e + CAP],
                                         start=True, stop=True)
                    filled(f"h{e}", last)
                if e >= 1:
                    wait_read(pe, f"h{e - 1}")
                    dst = to_fill(pe, f"eo{e - 1}")
                    for s in range(2):
                        for c in range(FC):
                            last = pe.matmul(dst[0:HC, D * s:D * s + D], hid[(e - 1) % 2][:, c, HC * s:HC * s + HC],
                                             w2_sb[:, e - 1, c, :], start=(c == 0), stop=(c == FC - 1))
                    filled(f"eo{e - 1}", last)

        @block.vector
        def _(ve):
            steps = [0]

            def link(ins):
                steps[0] += 1
                ins.then_inc(dve, 1)
                ve.wait_ge(dve, steps[0])

            def evacuate(name, dst, rearranged=lambda ap: ap):
                was_read(name, ve.tensor_copy(dst, rearranged(to_read(ve, name))))

            ve.wait_ge(win_in, 16)
            ve.wait_ge(conv_w_in, 32)
            for dr in range(2):
                for k in range(K):
                    ve.tensor_scalar(wk[:, dr, k, :], win[:, 0, :], cw[:, dr, 0, k:k + 1], None,
                                     ALU.mult).then_inc(wk_ok, 1)
                if dr == 0:
                    evacuate("xT0", xT[:, group(0), PAD:PAD + S], lambda ap: tiles(ap, HB))

            def conv(dr):
                pre = tiles(u_pre[:, dr, :], B)
                for k in range(K):
                    off = k if dr == 0 else 2 * PAD - k
                    src, tap = xi[:, 1, :, off:off + S], cw[:, dr, 1, k:k + 1]
                    if k == 0:
                        link(ve.tensor_scalar(pre, src, tap, None, ALU.mult))
                    else:
                        last = ve.scalar_tensor_tensor(pre, src, tap, pre, ALU.mult, ALU.add)
                        if k < K - 1:
                            link(last)
                last.then_inc(conv_ok, 1)

            for th in range(2):
                wait_read(ve, f"xi1{th}")
            ve.wait_ge(pads_ok, 4)
            conv(0)
            src = to_read(ve, "xproj")
            by_j = src[:, 0:(R + 2 * N) * 2 * NH].rearrange("p (j m) -> p j m", j=2 * NH)
            xp_j = xprojT[:, :, :, :].rearrange("p a h m -> p (a h) m")
            ve.wait_ge(xpad_ok, 1)
            for r in range(3):
                ve.tensor_copy(xp_j[:, :, N * r:N * r + N], by_j[:, :, R:R + N])
            ve.tensor_copy(xp_j[:, :, C0:C0 + N], by_j[:, :, R + N:R + 2 * N])
            ve.tensor_copy(xp_j[:, :, DT0:XM], by_j[:, :, 0:R])
            was_read("xproj", ve.tensor_copy(vec_cols[:, :], src[:, 256:256 + 6 * NH]))
            evacuate("wkT1", wkT[:, 1, :, :], lambda ap: tiles(ap, K))
            evacuate("woutT", woutT[:, :, :], lambda ap: tiles(ap[:, 0:NH * P], NH))
            wait_read(ve, "xproj")
            for dr in range(2):
                for h in range(NH):
                    last = ve.tensor_scalar(diag_d[:, dr, h, :], ident[:, :], col(4 + dr, h), None, ALU.mult)
            last.then_inc(diag_ok, 1)
            link(ve.tensor_reduce(sel_id[:, :], ident[0:B3, 0:B3].rearrange("p (r n) -> p n r", r=3), AX.X, ALU.add))
            ve.tensor_copy(sel[:, :, :], sel_id[:, :].unsqueeze(2).to_broadcast([B3, N, P])).then_inc(sel_ok, 1)
            ve.tensor_reduce(head_mask[:, :], ident[:, :].rearrange("p (g j i) -> p j g i", g=4, j=GH),
                             AX.XY, ALU.add).then_inc(head_mask_ok, 1)
            conv(1)

            def split_rows(dr, th):
                cols = half(th)
                src = to_read(ve, f"x{dr}_{th}")
                link(ve.tensor_copy(parts[:, dr, cols], src[0:B3, :]))
                ve.wait_ge(dt_rows_ok, 2 * dr + th + 1)
                was_read(f"x{dr}_{th}", ve.tensor_tensor(rests[:, cols], src[0:2 * N, :],
                                                         parts[0:2 * N, dr, cols], ALU.subtract))
                wait_read(ve, f"x{dr}_{th}")
                link(ve.tensor_copy(parts[0:2 * N, dr, cols], rests[:, cols]))
                link(ve.tensor_tensor(rests[0:N, cols], rests[0:N, cols], parts[0:N, dr, cols], ALU.subtract))
                last = ve.tensor_copy(parts[0:N, dr, cols], rests[0:N, cols])
                if th:
                    last.then_inc(parts_ok, 1)
                    ve.wait_ge(parts_ok, dr + 1)
                else:
                    link(last)

            def log1p_rest(dr, h):
                e, relu, _ = soft[dr][h]
                ve.wait_ge(soft_in, 2 * NH * dr + h + 1)
                link(ve.tensor_scalar(soft_t[:, :], e, 1.0, -1.0, ALU.add, ALU.add))
                link(ve.tensor_tensor(soft_t[:, :], e, soft_t[:, :], ALU.subtract))
                ve.tensor_tensor(relu, relu, soft_t[:, :], ALU.add).then_inc(e_used, 1)
                ve.wait_ge(e_used, NH * dr + h + 1)

            def finish_delta(dr, h):
                _, relu, ln = soft[dr][h]
                ve.wait_ge(soft_in, 2 * NH * dr + NH + h + 1)
                ve.tensor_tensor(delta[:, dr, h, :], relu, ln, ALU.add).then_inc(delta_ok, 1)

            for th in range(2):
                split_rows(0, th)
            ve.wait_ge(a_exp, 1)
            ve.tensor_scalar(a_neg[:, :, :, :], a_neg[:, :, :, :], -1.0, None, ALU.mult).then_inc(a_ok, 1)
            for h in range(NH):
                log1p_rest(0, h)
            for pair in range(VB // 2):
                evacuate(f"skip0_{pair}", acc[:, 2 * pair:2 * pair + 2, :], lambda ap: tiles(ap, 2))
            for h in range(NH):
                finish_delta(0, h)

            def scan_step(g, slot, dr):
                for h in range(NH):
                    ve.wait_ge(dA_ok, NH * g + h + 1)
                    ve.wait_ge(dBx_ok, NH * g + h + 1)
                    if not isinstance(g, int) or g >= 2:
                        ve.wait_ge(turned, 4 * (g - 1))
                    o, a, v = hs[slot][h], dA[slot][h], dBx[slot][h]
                    if dr:
                        o, a, v = o[:, ::-1], a[:, ::-1], v[:, ::-1]
                    ve.tensor_tensor_scan(o, a, v, 0.0, ALU.mult, ALU.add).then_inc(scanned, 1)

            def sum_y(g, n, dr):
                for b in range(VB):
                    ve.wait_ge(turned, 4 * g + b // 2 + 1)
                    if isinstance(g, int) and g == 0:
                        wait_read(ve, f"skip0_{b // 2}")
                    else:
                        ve.wait_ge(acc_ok, VB * (g - 1) + b + 1)
                    at = DI * (b % 2)
                    ve.scalar_tensor_tensor(acc[:, b, :], bank[:, 2 + b // 2, at:at + DI],
                                            c_col[:, dr, b, bass.ds(n, 1)], acc[:, b, :],
                                            ALU.mult, ALU.add).then_inc(acc_ok, 1)

            wait_read(ve, "c0")
            for g in range(N):
                scan_step(g, g % 2, 0)
                if g >= 1:
                    sum_y(g - 1, g - 1, 0)
                if 1 <= g <= VB // 2:
                    src = tiles(to_read(ve, f"skip1_{g - 1}"), 2)
                    ve.wait_ge(acc_ok, VB * g)
                    pair = acc[:, 2 * g - 2:2 * g, :]
                    was_read(f"skip1_{g - 1}", ve.tensor_tensor(pair, src, pair, ALU.add))
                    wait_read(ve, f"skip1_{g - 1}")
                if g in (4, 5):
                    split_rows(1, g - 4)
                if g in SOFT_STEPS[1]:
                    log1p_rest(1, SOFT_STEPS[1].index(g))
                if g in SOFT_STEPS[2]:
                    finish_delta(1, SOFT_STEPS[2].index(g))
            wait_read(ve, "c1")
            for j in range(2):
                scan_step(N + j, j, 1)
                sum_y(N + j - 1, (N + j - 1) % N, j)
            with ve.Fori(1, N // 2, 1) as i:
                for j in range(2):
                    scan_step(N + 2 * i + j, j, 1)
                    sum_y(N + 2 * i + j - 1, 2 * i + j - 1, 1)
            sum_y(2 * N - 1, N - 1, 1)

            for th in range(2):
                for h in range(NH):
                    wait_read(ve, f"z{h}{th}")
                    src = to_read(ve, f"yT{h}{th}")
                    was_read(f"yT{h}{th}", ve.tensor_tensor(yzT[:, h, half(th)], src, szT[:, h, half(th)], ALU.mult))

            def moments_of(res, b):
                link(ve.bn_stats(stats[:, b, :], res[:, b, :]))
                ve.bn_aggr(moments[:, b, :], stats[:, b, :]).then_inc(var_ok, 1)

            def normalize(res, dst, norm, g, done):
                ve.wait_ge(rstd_ok, 2 * norm + g + 1)
                for b in range(HB * g, HB * g + HB):
                    ve.tensor_scalar(dst[:, b, :], res[:, b, :], moments[:, b, 0:1], rstd[:, b:b + 1],
                                     ALU.subtract, ALU.mult).then_inc(done, 1)

            for g in range(2):
                src = tiles(to_read(ve, f"o{g}"), HB)
                was_read(f"o{g}", ve.tensor_tensor(res1[:, group(g), :], src, x_tok[:, group(g), :], ALU.add))
                wait_read(ve, f"o{g}")
                for b in range(HB * g, HB * g + HB):
                    moments_of(res1, b)
            for g in range(2):
                normalize(res1, x1, 0, g, x1_ok)
            evacuate("x1T0", x1T[:, half(0)])

            def shift_scores(i):
                c = i % 2
                to_read(ve, f"s{i}")
                src = bank[:, 2 * c:2 * c + 2, :].rearrange("p a (j k) -> p (a j) k", j=GH)
                if i >= 3:
                    to_read(ve, f"pT{i - 3}")
                if i >= 2:
                    wait_read(ve, f"s{i - 2}")
                link(ve.tensor_reduce(rmax[:, c, :], src, AX.X, ALU.max))
                was_read(f"s{i}", ve.tensor_tensor(prob[i % 3], src, rmax[:, c, :].unsqueeze(2).to_broadcast([P, CH, S]),
                                                   ALU.subtract))

            def sum_exps(i):
                ve.wait_ge(exp_ok, i + 1)
                if i >= 2:
                    ve.wait_ge(prob_ok, i - 1)
                link(ve.tensor_reduce(rsum[:, i % 2, :], prob[i % 3], AX.X, ALU.add))
                ve.reciprocal(rsum[:, i % 2, :], rsum[:, i % 2, :]).then_inc(sums_ok, 1)

            for i in range(LAST + 1):
                if i < 2 * B:
                    shift_scores(i)
                if 1 <= i <= 2 * B:
                    sum_exps(i - 1)
                if i % 2 == 0 and 6 <= i < 2 * B + 6:
                    b = i // 2 - 3
                    src = to_read(ve, f"wo{b}")
                    was_read(f"wo{b}", ve.tensor_tensor(res2[:, b, :], src[:, 0:D], x1[:, b, :], ALU.add))
                    wait_read(ve, f"wo{b}")
                    moments_of(res2, b)
                if i == 2 * HB + 6:
                    normalize(res2, x2, 1, 0, x2_ok)
            normalize(res2, x2, 1, 1, x2_ok)
            evacuate("x2T0", x2T[:, half(0)])

            top, chosen, total, prob_top, place, fits, slot, take = (route_b[:, k, :] for k in range(8))

            def over_e(ap):
                return ap.unsqueeze(2).to_broadcast([P, B, E])

            logits = to_read(ve, "logits")[:, 0:B * E].rearrange("p (b e) -> p b e", b=B)
            link(ve.tensor_reduce(top, logits, AX.X, ALU.max))
            ve.tensor_tensor(route[:, 0, :, :], logits, over_e(top), ALU.subtract).then_inc(gate_d, 1)
            link(ve.tensor_tensor(route[:, 2, :, :], logits, over_e(top), ALU.is_ge))
            link(ve.tensor_tensor(route[:, 2, :, :], route[:, 2, :, :], rev_e[:, :, :], ALU.mult))
            link(ve.tensor_reduce(chosen, route[:, 2, :, :], AX.X, ALU.max))
            ve.tensor_tensor(route_mask_bf[:, :, :], rev_e[:, :, :], over_e(chosen), ALU.is_equal).then_inc(route_mask, 1)
            ve.wait_ge(gate_exp, 1)
            link(ve.tensor_reduce(total, route[:, 1, :, :], AX.X, ALU.add))
            ve.reciprocal(prob_top, total)
            ve.wait_ge(route_mask, 1)
            counts = to_read(ve, "count")[:, 0:B * E].rearrange("p (b e) -> p b e", b=B)
            link(ve.tensor_tensor(route[:, 2, :, :], counts, route_mask_bf[:, :, :], ALU.mult))
            link(ve.tensor_reduce(place, route[:, 2, :, :], AX.X, ALU.add))
            ve.tensor_scalar(fits, place, float(CAP), None, ALU.is_le)
            link(ve.scalar_tensor_tensor(slot, chosen, -float(CAP), place, ALU.mult, ALU.add))
            link(ve.tensor_scalar(take, slot, float(CAP * E - 1 - SLOTS), None, ALU.add))
            link(ve.tensor_tensor(take, take, fits, ALU.mult))
            link(ve.tensor_scalar(slot, slot, float(CAP * E - 1), None, ALU.add))
            link(ve.tensor_tensor(slot, slot, dump[:, :], ALU.subtract))
            link(ve.tensor_tensor(slot, slot, fits, ALU.mult))
            link(ve.tensor_tensor(slot, slot, dump[:, :], ALU.add))
            ve.tensor_copy(slot_u[:, :], slot).then_inc(slots_ok, 1)
            link(ve.tensor_scalar(take, take, float(SLOTS), None, ALU.add))
            link(ve.tensor_tensor(prob_top, prob_top, fits, ALU.mult))
            ve.tensor_copy(take_u[:, :], take).then_inc(slots_ok, 1)

            evacuate("xeT1", xeT[:, BANK:2 * BANK])
            for e in range(E):
                evacuate(f"eo{e}", eo[0:HC, e, :, :], lambda ap: ap[0:HC, 0:2 * D].rearrange("p (s d) -> p s d", s=2))

            for b in range(B):
                ve.wait_ge(gathered, 16 * B)
                link(ve.scalar_tensor_tensor(res3[:, b, :], back[:, b, :], prob_top[:, b:b + 1], x2[:, b, :],
                                             ALU.mult, ALU.add))
                moments_of(res3, b)
            for g in range(2):
                normalize(res3, y_out, 2, g, y_ok)


_INS = ["x", "ctx_1024", "L0_attn_in_proj_w", "L0_attn_conv_w", "L0_attn_conv_bias", "L0_attn_x_proj_w",
        "L0_attn_dt_proj_w", "L0_attn_dt_proj_bias", "L0_attn_A_log", "L0_attn_D_skip", "L0_attn_convb_w",
        "L0_attn_convb_bias", "L0_attn_x_proj_b_w", "L0_attn_dt_proj_b_w", "L0_attn_dt_proj_b_bias",
        "L0_attn_A_b_log", "L0_attn_D_b_skip", "L0_attn_out_proj_w", "L0_xattn_Wq", "L0_xattn_Wk", "L0_xattn_Wv",
        "L0_xattn_Wo", "L0_ffn_gate_w", "L0_ffn_w1", "L0_ffn_w2"]


def kernel(**inputs):
    import numpy as _np
    import concourse.bacc as _bacc
    from concourse import mybir as _mybir
    from concourse.bass_utils import run_bass_kernel_spmd as _run

    nc = _bacc.Bacc("TRN2", target_bir_lowering=False, num_devices=1)
    arrays, args = {}, []
    for name in _INS:
        a = _np.ascontiguousarray(inputs[name])
        arrays[f"in_{name}"] = a
        args.append(nc.dram_tensor(f"in_{name}", a.shape, _mybir.dt.from_np(a.dtype), kind="ExternalInput").ap())
    shape = inputs["x"].shape
    args.append(nc.dram_tensor("out_0", shape, _mybir.dt.from_np(_np.dtype("float32")), kind="ExternalOutput").ap())
    decoder_layer_kernel(nc, *args)
    r = _run(nc, [arrays], core_ids=[0])
    return r.results[0]["out_0"]
```

```python
from contextlib import ExitStack

import concourse.bass as bass
from concourse import mybir

F32 = mybir.dt.float32
BF16 = mybir.dt.bfloat16
U32 = mybir.dt.uint32
ALU = mybir.AluOpType
ACT = mybir.ActivationFunctionType
AX = mybir.AxisListType
P = 128
BANK = 512
EPS = 1e-5


def decoder_layer_kernel(nc, x, ctx_1024, in_proj_w, conv_w, conv_bias, x_proj_w, dt_proj_w, dt_proj_bias,
                         A_log, D_skip, convb_w, convb_bias, x_proj_b_w, dt_proj_b_w, dt_proj_b_bias,
                         A_b_log, D_b_skip, out_proj_w, Wq, Wk, Wv, Wo, gate_w, w1, w2, out):
    B, S, D = x.shape
    T = B * S
    TH = T // 2
    HB = B // 2
    DI = in_proj_w.shape[0] // 2
    NH = DI // P
    N = A_log.shape[1]
    R = dt_proj_w.shape[1]
    K = conv_w.shape[2]
    PAD = K - 1
    SP = S + 2 * PAD
    B3, C0, DT0 = 3 * N, 64, 96
    XM = DT0 + R
    VB = 6
    HEADS = 16
    DH = D // HEADS
    GH = 4
    CH = 8
    LAST = 2 * B + 6
    ROUTE0 = 2 * B + 3
    E = gate_w.shape[1]
    F = w1.shape[2]
    FC = F // P
    CAP = 160
    HC = CAP // 2
    SLOTS = E * CAP
    ST = SLOTS // P
    SCALE = float(DH) ** -0.5
    assert S == P and D == P and TH == BANK and NH == 2 and CH * S == 2 * BANK

    d_slots = nc.dram_tensor("dispatched_tokens", (SLOTS + T, D), F32).ap()
    d_expert = nc.dram_tensor("expert_outputs", (SLOTS + P, D), F32).ap()

    with ExitStack() as ctx:
        def sb(name, shape, dt=F32):
            return ctx.enter_context(nc.sbuf_tensor(name, shape, dt))

        def sem(name):
            return ctx.enter_context(nc.semaphore(name))

        bank = ctx.enter_context(nc.psum_tensor("bank", [P, 8, BANK], F32))

        ident = sb("ident", [P, P])
        x_tok = sb("x_tok", [P, B, D])
        ctx_tok = sb("ctx_tok", [P, B, D])
        b_row = sb("b_row", [P, 2, T])
        early = b_row[:, :, :].rearrange("p a t -> p (a t)")
        win = early[:, 0:512].rearrange("p (c d) -> p c d", c=2 * NH)
        wqkvo = early[:, 512:1024].rearrange("p (n d) -> p n d", n=4)
        wout = early[:, 1024:1280]
        xproj = early[0:R + 2 * N, 1280:1792].rearrange("p (a d) -> p a d", a=2)
        cw = sb("cw", [P, 2, NH, K])
        a_log = sb("a_log", [P, 2, NH, N])
        a_neg = sb("a_neg", [P, 2, NH, N])
        vec_rows = sb("vec_rows", [6 * NH, P])
        vec_cols = sb("vec_cols", [P, 6 * NH])
        dtw = sb("dtw", [P, 2, NH, XM])
        gate = sb("gate", [P, E])
        w1_sb = sb("w1_sb", [P, E, F])
        w2_sb = sb("w2_sb", [P, E, FC, D])

        xT = sb("xT", [P, B, SP])
        wkT = sb("wkT", [P, 2, K, P])
        winT = sb("winT", [P, 2 * NH, P])
        woutT = sb("woutT", [P, NH, D])
        xprojT = sb("xprojT", [P, 2, NH, XM])
        dtT = sb("dtT", [P, 2, NH, P])
        qkvT = sb("qkvT", [P, 3, D])
        woT = sb("woT", [P, HEADS // GH, D])
        diag_d = sb("diag_d", [P, 2, NH, P])
        sel = sb("sel", [B3, N, P], BF16)
        uT = sb("uT", [P, 2, NH, T])
        szT = sb("szT", [P, NH, T])
        sel_id = sb("sel_id", [B3, N])
        parts = sb("parts", [B3, 2, T], BF16)
        rows = sb("rows", [P, T])
        c_col = sb("c_col", [P, 2, B, N])
        acc = sb("acc", [P, VB, DI])
        y_part = wkT[:, :, :, :].rearrange("p a k d -> p a (k d)")
        soft_t = sb("soft_t", [P, T])
        delta = sb("delta", [P, 2, NH, T])
        du = uT
        arena = sb("arena", [P, 12, T])
        head_mask = sb("head_mask", [P, GH])
        group_mask = sb("group_mask", [P, HEADS // GH])
        k_maskT = sb("k_maskT", [P, B, GH, S])
        k_flat = k_maskT[:, :, :, :].rearrange("p b j k -> p (b j k)")
        v_pad = delta[:, :, :, :].rearrange("p a h t -> p (a h t)").rearrange("p (b h e) -> p b h e", b=B, h=HEADS)
        x1 = x_tok
        x2 = ctx_tok
        stats = sb("stats", [P, B, 6])
        moments = sb("moments", [P, B, 2])
        rstd = sb("rstd", [P, B])
        neg_half = sb("neg_half", [P, B])
        soft_buf = k_flat.rearrange("p (c t) -> p c t", t=T)
        soft = [[(soft_buf[:, 2 * h, :], soft_buf[:, 2 * h + 1, :], arena[:, 8 + h, :]) for h in range(NH)],
                [(soft_buf[:, 2 * h, :], soft_buf[:, 2 * h + 1, :], soft_buf[:, 2 * h, :]) for h in range(NH)]]
        soft_rest = [[soft_t[:, :], arena[:, 10, :]], [soft_t[:, :], soft_t[:, :]]]
        rmax = sb("rmax", [P, 2, CH])
        rsum = sb("rsum", [P, 3, CH])
        route = sb("route", [P, 3, B, E])
        route_b = sb("route_b", [P, 8, B])
        zeros = sb("zeros", [P, D])
        tri = sb("tri", [P, P], BF16)
        ones = sb("ones", [P, P], BF16)
        route_mask_bf = sb("route_mask_bf", [P, B, E], BF16)
        rev_e = sb("rev_e", [P, B, E])
        dump = sb("dump", [P, B])
        slot_u = sb("slot_u", [P, B], U32)
        take_u = sb("take_u", [P, B], U32)

        wk = arena[:, 8, :].rearrange("p (a k d) -> p a k d", a=2, k=K)
        u_pre = delta[:, 1, :, :]
        xi = k_flat[:, 0:B * SP].rearrange("p (b s) -> p b s", b=B)
        ctxT = arena[:, 10, :]
        dA = [[arena[:, 2 * (g % 2) + h, :] for h in range(NH)] for g in range(2)]
        dBx = [[arena[:, 4 + 2 * (g % 2) + h, :] for h in range(NH)] for g in range(2)]
        hs = [[arena[:, 8 + 2 * (g % 2) + h, :] for h in range(NH)] for g in range(2)]
        wo_pad = arena[:, 11, 0:BANK].rearrange("p (h e) -> p h e", h=HEADS)
        rests = soft_t[0:2 * N, :]
        y_rest = arena[:, 0, 0:BANK]
        yzT = uT[:, 0, :, :]
        res1 = arena[:, 8, :].rearrange("p (b d) -> p b d", b=B)
        x1T = arena[:, 9, :]
        q_maskT = uT[:, :, :, :].rearrange("p a h t -> p (a h) t")
        prob = [arena[:, c, :].rearrange("p (h k) -> p h k", h=CH) for c in range(3)]
        probT = [arena[:, 3 + c, :].rearrange("p (h k) -> p h k", h=CH) for c in range(2)]
        outT = [arena[:, 6, BANK * c:BANK * c + BANK] for c in range(2)]
        res2 = arena[:, 8, :].rearrange("p (b d) -> p b d", b=B)
        x2T = arena[:, 9, :]
        xe = arena[:, 0:2, :].rearrange("p a t -> p (a t)")[:, 0:SLOTS].rearrange("p (j d) -> p j d", j=ST)
        xeT = arena[:, 2:4, :].rearrange("p a t -> p (a t)")[:, 0:SLOTS]
        eoT = [arena[:, 9, CAP * k:CAP * k + CAP] for k in range(2)]
        hid = [arena[:, 4 + e, 0:FC * CAP].rearrange("p (c s) -> p c s", c=FC) for e in range(2)]
        eo = arena[:, 6:8, :].rearrange("p a (e s d) -> p (a e) s d", s=2, d=D)
        back = arena[:, 10, :].rearrange("p (b d) -> p b d", b=B)
        res3 = arena[:, 8, :].rearrange("p (b d) -> p b d", b=B)
        y_out = arena[:, 11, :].rearrange("p (b d) -> p b d", b=B)
        mamba_in = [(conv_w, conv_bias, x_proj_w, dt_proj_w, dt_proj_bias, A_log, D_skip),
                    (convb_w, convb_bias, x_proj_b_w, dt_proj_b_w, dt_proj_b_bias, A_b_log, D_b_skip)]

        def col(vec, h):
            return vec_cols[:, NH * vec + h:NH * vec + h + 1]

        x_in, win_in, small_in, wout_in = sem("x_in"), sem("win_in"), sem("small_in"), sem("wout_in")
        conv_w_in, small_gp_in = sem("conv_w_in"), sem("small_gp_in")
        ctx_in, attn_w_in, moe_w_in = sem("ctx_in"), sem("attn_w_in"), sem("moe_w_in")
        full = [sem(f"bank{i}_full") for i in range(8)]
        read = [sem(f"bank{i}_read") for i in range(8)]
        dve, act, pool = sem("dve_steps"), sem("act_steps"), sem("pool_steps")
        ident_ok, consts_ok, dtw_ok, pads_ok = sem("ident_ok"), sem("consts_ok"), sem("dtw_ok"), sem("pads_ok")
        wk_ok, diag_ok, sel_ok, head_mask_ok = sem("wk_ok"), sem("diag_ok"), sem("sel_ok"), sem("head_mask_ok")
        dt_rows_ok, parts_ok, a_exp, a_ok = sem("dt_rows_ok"), sem("parts_ok"), sem("a_exp"), sem("a_ok")
        rest_added, sel_id_ok = sem("rest_added"), sem("sel_id_ok")
        xpad_ok, conv_ok, silu_ok, e_used = sem("xproj_pad_ok"), sem("conv_ok"), sem("silu_ok"), sem("e_used")
        soft_in, delta_ok, du_ok = sem("softplus_terms"), sem("delta_ok"), sem("du_ok")
        b_bc, b_sb = sem("b_broadcast"), sem("b_in_sbuf")
        u_used = sem("u_used")
        dA_ok, dBx_ok, scanned = sem("dA_ok"), sem("dBx_ok"), sem("scanned")
        turned, acc_ok, part_ok, added = sem("turned"), sem("acc_ok"), sem("y_part_ok"), sem("added")
        var_ok, rstd_ok, x1_ok, x2_ok = sem("var_ok"), sem("rstd_ok"), sem("x1_ok"), sem("x2_ok")
        q_first_ok = sem("q_first_ok")
        exp_ok, sums_ok, prob_ok = sem("exp_ok"), sem("sums_ok"), sem("prob_ok")
        av_half = sem("av_half")
        wo_pad_ok, v_zero = sem("wo_pad_ok"), sem("v_zero")
        gate_d, gate_exp, route_mask = sem("gate_shifted"), sem("gate_exp"), sem("route_mask")
        slots_ok, zero_ok, dispatched = sem("slots_ok"), sem("zero_ok"), sem("dispatched")
        xe_in = [sem(f"xe_in{k}") for k in range(2)]
        take_ok, eo_out, y_ok, stored = sem("take_ok"), sem("eo_out"), sem("y_ok"), sem("stored")
        gathered = [sem(f"gathered_pair{k}") for k in range(B // 2)]

        plan = [("xT0", 0), ("xT1", 1), ("winT", 2), ("wkT0", 3)]
        plan += [("xi0", 0), ("xi1", 1), ("xproj", 6), ("u0_0", 4), ("u0_1", 5), ("dtw", 7), ("wkT1", 0), ("woutT", 1)]
        plan += [("x0_0", 2), ("x0_1", 3), ("qkv", 6), ("z00", 0), ("z01", 1), ("z10", 7), ("z11", 4), ("woT", 5)]
        plan += [("c0", 4)]
        plan += [(f"d0{h}{th}", 2 * h + th) for h in range(NH) for th in range(2)]
        plan += [("skip0_0", 7), ("skip0_1", 4), ("skip0_2", 5), ("y_rest", 6), ("u1_0", 2), ("u1_1", 3)]
        scan_from = len(plan)
        plan += [("x1_0", 7), ("x1_1", 7)]
        plan += [(f"d1{h}{th}", 7) for h in range(NH) for th in range(2)]
        plan += [("c1", 7), ("skip1_0", 7), ("skip1_1", 7), ("skip1_2", 7)]
        plan += [(f"yT{h}{th}", 2 * th + h) for th in range(2) for h in range(NH)]
        plan += [("ctxT0", 6), ("ctxT1", 7)]
        plan += [("o0", 4), ("o1", 5), ("k0", 0), ("v0", 1), ("k1", 2), ("v1", 3)]
        plan += [("x1T0", 6), ("q0", 4), ("x1T1", 7), ("s0", 0, 2), ("q1", 7), ("s1", 2, 2)]
        for i in range(LAST):
            if 1 <= i < 2 * B - 1:
                plan += [(f"s{i + 1}", 2 * ((i + 1) % 2), 2)]
            if 2 <= i < 2 * B + 2:
                plan += [(f"pT{i - 2}", 4, 2)]
            if i % 2 == 0 and 4 <= i < 2 * B + 4:
                plan += [(f"av{i // 2 - 2}", 6)]
            if i % 2 == 1 and 5 <= i < 2 * B + 5:
                plan += [(f"wo{i // 2 - 2}", 7)]
            if i == ROUTE0:
                plan += [("x2T0", 0), ("logits0", 1)]
        plan += [("count0", 2), ("x2T1", 3), ("logits1", 4), ("count1", 5)]
        plan += [("xeT0", 0), ("xeT1", 1), ("xeT2", 2)]
        for e in range(E + 2):
            plan += [(f"h{e}", 2 * (e % 2), 2)] if e < E else []
            plan += [(f"eoT{e - 1}", 4 + (e - 1) % 2)] if 1 <= e <= E else []
            plan += [(f"eo{e - 2}", 6 + e % 2)] if e >= 2 else []
        where, before, holder, uses = {}, {}, [None] * 8, [0] * 8
        for n, (name, i, *width) in enumerate(plan):
            if n == scan_from:
                held_at_scan, holder = holder[0:6], [None] * 6 + holder[6:8]
            banks = range(i, i + (width or [1])[0])
            where[name] = (i, uses[i])
            before[name] = sorted({holder[k] for k in banks} - {None})
            uses[i] += 1
            for k in banks:
                holder[k] = name

        def wait_read(eng, name):
            i, n = where[name]
            eng.wait_ge(read[i], n + 1)

        def to_fill(pe, name):
            for old in before[name]:
                wait_read(pe, old)
            return bank[:, where[name][0], :]

        def filled(name, last):
            last.then_inc(full[where[name][0]], 1)

        def to_read(eng, name):
            i, n = where[name]
            eng.wait_ge(full[i], n + 1)
            return bank[:, i, :]

        def was_read(name, last):
            last.then_inc(read[where[name][0]], 1)

        ROWS_AT, C_AT, D_AT, SKIP_AT = (1, 2), 9, (5, 6, 7, 8), (10, 11, 12)
        EXP_AT, REST_AT, ADD_AT, LN_AT, DELTA_AT, DU_AT = (7, 9), (8, 9), (9, 11), 11, (11, 13), 13

        def half(th):
            return slice(TH * th, TH * th + TH)

        def group(g):
            return slice(HB * g, HB * g + HB)

        def tiles(ap, n):
            return ap.rearrange("p (a c) -> p a c", a=n)

        def split_rests(eng, link, dr, th):
            cols = half(th)
            link(eng.tensor_copy(parts[0:2 * N, dr, cols], rests[:, cols]))
            link(eng.tensor_tensor(rests[0:N, cols], rests[0:N, cols], parts[0:N, dr, cols], ALU.subtract))
            eng.tensor_copy(parts[0:N, dr, cols], rests[0:N, cols]).then_inc(parts_ok, 1)

        def weigh_u(eng, dr, h):
            eng.wait_ge(delta_ok, NH * dr + h + 1)
            eng.wait_ge(u_used, dr + 1)
            eng.tensor_tensor(du[:, dr, h, :], delta[:, dr, h, :], uT[:, dr, h, :], ALU.mult).then_inc(du_ok, 1)

        block = ctx.enter_context(nc.Block())

        @block.sync
        def _(sp):
            sp.dma_start(x_tok[:, :, :], x.rearrange("b s d -> s b d")).then_inc(x_in, 16)
            sp.dma_start(win, in_proj_w.rearrange("(c p) d -> p c d", p=P)).then_inc(win_in, 16)
            for dr in range(2):
                sp.dma_start(cw[:, dr, :, :],
                             mamba_in[dr][0].rearrange("(h p) a k -> p h (a k)", p=P)).then_inc(conv_w_in, 16)
            for dr in range(2):
                _, cb, xp, _, dtb, _, dsk = mamba_in[dr]
                for v, vec in ((dr, cb), (2 + dr, dtb), (4 + dr, dsk)):
                    sp.dma_start(vec_rows[NH * v:NH * v + NH, :],
                                 vec.rearrange("(h p) -> h p", p=P)).then_inc(small_in, 16)
                sp.dma_start(xproj[:, dr, :], xp).then_inc(small_in, 16)
            sp.dma_start(wout, out_proj_w).then_inc(wout_in, 16)
            for n, w in enumerate((Wq, Wk, Wv, Wo)):
                sp.dma_start(wqkvo[:, n, :], w).then_inc(attn_w_in, 16)
            sp.dma_start(ctx_tok[:, :, :], ctx_1024.rearrange("b s d -> s b d")).then_inc(ctx_in, 16)
            sp.dma_start(gate[:, :], gate_w).then_inc(moe_w_in, 16)
            sp.dma_start(w1_sb[:, :, :], w1.rearrange("e d f -> d e f")).then_inc(moe_w_in, 16)
            sp.dma_start(w2_sb[:, :, :, :], w2.rearrange("e (c p) d -> p e c d", p=P)).then_inc(moe_w_in, 16)
            sp.wait_ge(consts_ok, 1)
            sp.dma_start(d_slots[0:SLOTS, :].rearrange("(j p) d -> p j d", p=P),
                         zeros[:, :].unsqueeze(1).to_broadcast([P, ST, D])).then_inc(zero_ok, 16)
            sp.dma_start(d_expert[SLOTS:SLOTS + P, :], zeros[:, :]).then_inc(zero_ok, 16)
            sp.wait_ge(dispatched, 16 * B)
            d_xe = d_slots[0:SLOTS, :].rearrange("(j p) d -> p j d", p=P)
            sp.dma_start(xe[:, 0:4, :], d_xe[:, 0:4, :]).then_inc(xe_in[0], 16)
            sp.dma_start(xe[:, 4:ST, :], d_xe[:, 4:ST, :]).then_inc(xe_in[1], 16)
            d_eo = d_expert[0:SLOTS, :].rearrange("(e s p) d -> p e s d", e=E, s=2)
            for e in range(0, E, 2):
                wait_read(sp, f"eo{e}")
                wait_read(sp, f"eo{e + 1}")
                sp.dma_start(d_eo[:, e:e + 2, :, :], eo[0:HC, e:e + 2, :, :]).then_inc(eo_out, 16)
            for g in range(2):
                sp.wait_ge(y_ok, HB * (g + 1))
                sp.dma_start(out[HB * g:HB * g + HB].rearrange("b s d -> s b d"),
                             y_out[:, group(g), :]).then_inc(stored, 16)
            sp.wait_ge(stored, 32)

        @block.gpsimd
        def _(gp):
            steps = [0]

            def link(ins):
                steps[0] += 1
                ins.then_inc(pool, 1)
                gp.wait_ge(pool, steps[0])

            link(gp.memset(ident[:, :], 0.0))
            gp.affine_select(out=ident[:, :], in_=ident[:, :], compare_op=ALU.not_equal, fill=1.0, base=0,
                             pattern=[[-1, P]], channel_multiplier=1).then_inc(ident_ok, 1)
            for dr in range(2):
                gp.dma_start(dtw[:, dr, :, DT0:XM],
                             mamba_in[dr][3].rearrange("(h p) r -> p h r", p=P)).then_inc(small_gp_in, 16)
                gp.dma_start(a_log[:, dr, :, :],
                             mamba_in[dr][5].rearrange("(h p) n -> p h n", p=P)).then_inc(small_gp_in, 16)
            gp.memset(xT[:, :, 0:PAD], 0.0).then_inc(pads_ok, 1)
            gp.memset(xT[:, :, PAD + S:SP], 0.0).then_inc(pads_ok, 1)
            gp.memset(dtw[:, :, :, 0:DT0], 0.0).then_inc(dtw_ok, 1)
            gp.memset(xi[:, :, 0:PAD], 0.0).then_inc(pads_ok, 1)
            gp.memset(xi[:, :, PAD + S:SP], 0.0).then_inc(pads_ok, 1)
            gp.memset(xprojT[:, :, :, :], 0.0).then_inc(xpad_ok, 1)
            link(gp.memset(wo_pad, 0.0))
            gp.wait_ge(attn_w_in, 64)
            gp.tensor_copy(wo_pad[:, :, 0:DH], wqkvo[:, 3, :].rearrange("p (h e) -> p h e", h=HEADS)).then_inc(wo_pad_ok, 1)
            gp.memset(zeros[:, :], 0.0).then_inc(consts_ok, 1)
            gp.memset(neg_half[:, :], -0.5).then_inc(consts_ok, 1)
            gp.memset(ones[:, :], 1.0).then_inc(consts_ok, 1)
            link(gp.memset(tri[:, :], 1.0))
            gp.affine_select(out=tri[:, :], in_=tri[:, :], compare_op=ALU.is_ge, fill=0.0, base=0,
                             pattern=[[1, P]], channel_multiplier=-1).then_inc(consts_ok, 1)
            gp.iota(rev_e[:, :, :], pattern=[[0, B], [-1, E]], base=E, channel_multiplier=0,
                    allow_small_or_imprecise_dtypes=True).then_inc(consts_ok, 1)
            gp.iota(dump[:, :], pattern=[[S, B]], base=SLOTS, channel_multiplier=1,
                    allow_small_or_imprecise_dtypes=True).then_inc(consts_ok, 1)

            wait_read(gp, "xproj")
            for dr in range(2):
                for h in range(NH):
                    last = gp.tensor_scalar(diag_d[:, dr, h, :], ident[:, :], col(4 + dr, h), None, ALU.mult)
            last.then_inc(diag_ok, 1)
            gp.wait_ge(sel_id_ok, 1)
            gp.tensor_copy(sel[:, :, :], sel_id[:, :].unsqueeze(2).to_broadcast([B3, N, P])).then_inc(sel_ok, 1)
            for th in range(2):
                wait_read(gp, f"x0_{th}")
                split_rests(gp, link, 0, th)

            def add_rest(dr, h):
                gp.wait_ge(e_used, NH * dr + h + 1)
                relu = soft[dr][h][1]
                if dr == 0:
                    for th in range(2):
                        wait_read(gp, f"d0{h}{th}")
                gp.tensor_tensor(relu, relu, soft_rest[dr][h], ALU.add).then_inc(rest_added, 1)

            add_rest(0, 0)

            def dbx_step(g, slot, dr, restarts=False):
                gp.wait_ge(b_sb, g + 1)
                for h in range(NH):
                    if isinstance(g, int) and g == 0:
                        gp.wait_ge(du_ok, h + 1)
                    if not isinstance(g, int) or g >= 2:
                        gp.wait_ge(scanned, NH * (g - 2) + h + 1)
                    if restarts:
                        edge = (S - 1) * dr
                        link(gp.memset(tiles(dA[slot][h], B)[:, :, edge:edge + 1], 0.0))
                    gp.tensor_tensor(dBx[slot][h], du[:, dr, h, :], b_row[:, slot, :], ALU.mult).then_inc(dBx_ok, 1)

            for g in range(N):
                dbx_step(g, g % 2, 0, restarts=g < 2)
                if g in ADD_AT:
                    h = ADD_AT.index(g)
                    add_rest(1, h)
                if g == DU_AT:
                    weigh_u(gp, 1, 0)
            gp.wait_ge(du_ok, 2 * NH)
            for j in range(2):
                dbx_step(N + j, j, 1, restarts=True)
            with gp.Fori(1, N // 2, 1) as i:
                for j in range(2):
                    dbx_step(N + 2 * i + j, j, 1)

            def rstd_of(norm, g):
                gp.wait_ge(var_ok, B * norm + HB * g + HB)
                link(gp.tensor_scalar(rstd[:, group(g)], moments[:, group(g), 1], EPS, None, ALU.add))
                gp.tensor_tensor(rstd[:, group(g)], rstd[:, group(g)], neg_half[:, group(g)],
                                 ALU.pow).then_inc(rstd_ok, 1)

            def rstds(norm):
                for g in range(2):
                    rstd_of(norm, g)

            gp.wait_ge(dA_ok, NH * 2 * N)
            gp.memset(v_pad[:, :, :, DH:32], 0.0).then_inc(v_zero, 1)
            rstds(0)
            for i in range(2 * B):
                gp.wait_ge(sums_ok, i + 1)
                gp.tensor_tensor(prob[i % 3], prob[i % 3], rsum[:, i % 3, :].unsqueeze(2).to_broadcast([P, CH, S]),
                                 ALU.mult).then_inc(prob_ok, 1)
            rstds(1)
            gp.wait_ge(zero_ok, 32)
            for g in range(2):
                gp.wait_ge(slots_ok, g + 1)
                for b in range(HB * g, HB * g + HB):
                    gp.indirect_dma_start(d_slots, bass.IndirectOffsetOnAxis(slot_u[:, b:b + 1], 0),
                                          x2[:, b, :], None).then_inc(dispatched, 16)
            gp.wait_ge(take_ok, 2)
            gp.wait_ge(eo_out, 16 * (E // 2))
            for b in range(B):
                gp.indirect_dma_start(back[:, b, :], None, d_expert,
                                      bass.IndirectOffsetOnAxis(take_u[:, b:b + 1], 0)).then_inc(gathered[b // 2], 16)
            rstds(2)

        @block.scalar
        def _(sc):
            def evacuate(name, dst, rearranged=lambda ap: ap, func=ACT.Copy, **how):
                was_read(name, sc.activation(dst, rearranged(to_read(sc, name)), func, **how))

            evacuate("xT1", xT[:, group(1), PAD:PAD + S], lambda ap: tiles(ap, HB))
            evacuate("winT", winT[:, :, :], lambda ap: tiles(ap, 2 * NH))
            evacuate("wkT0", wkT[:, 0, :, :], lambda ap: tiles(ap, K))
            for th in range(2):
                evacuate(f"xi{th}", xi[:, group(th), PAD:PAD + S], lambda ap: tiles(ap, HB))

            def silu_u(dr):
                for th in range(2):
                    evacuate(f"u{dr}_{th}", uT[:, dr, 0, half(th)], func=ACT.Silu, bias=col(dr, 0))
                sc.wait_ge(conv_ok, dr + 1)
                sc.activation(uT[:, dr, 1, :], u_pre[:, dr, :], ACT.Silu, bias=col(dr, 1)).then_inc(silu_ok, 1)

            wait_read(sc, "xproj")
            silu_u(0)
            evacuate("dtw", dtT[DT0:XM, :, :, :].rearrange("p a h e -> p (a h) e"),
                     lambda ap: tiles(ap, 2 * NH)[DT0:XM, :, :])

            def copy_rows(dr, th):
                sc.activation(rows[C0:XM, half(th)], to_read(sc, f"x{dr}_{th}")[C0:XM, :],
                              ACT.Copy).then_inc(dt_rows_ok, 1)

            def copy_c(dr):
                evacuate(f"c{dr}", c_col[:, dr, :, :], lambda ap: tiles(ap[:, 0:B * N], B))

            def absolute(dr, h, th):
                sc.activation(soft[dr][h][0][:, half(th)], to_read(sc, f"d{dr}{h}{th}"), ACT.Abs,
                              bias=col(2 + dr, h)).then_inc(act, 1)

            def exp_abs(dr, h):
                e = soft[dr][h][0]
                sc.wait_ge(act, 2 * NH * dr + 2 * h + 2)
                sc.activation(e, e, ACT.Exp, scale=-1.0).then_inc(soft_in, 1)

            def log_one_plus(dr, h):
                e, _, ln = soft[dr][h]
                sc.wait_ge(soft_in, 2 * NH * dr + NH)
                if dr:
                    sc.wait_ge(e_used, NH * dr + h + 1)
                sc.activation(ln, e, ACT.Ln, bias=1.0).then_inc(soft_in, 1)

            for th in range(2):
                copy_rows(0, th)
            evacuate("qkv", qkvT[:, :, :], lambda ap: tiles(ap[:, 0:3 * D], 3))
            for h in range(NH):
                for th in range(2):
                    evacuate(f"z{h}{th}", szT[:, h, half(th)], func=ACT.Silu)
            evacuate("woT", woT[:, :, :], lambda ap: tiles(ap, HEADS // GH))
            copy_c(0)
            sc.wait_ge(conv_ok, 2)
            for h in range(NH):
                for th in range(2):
                    absolute(0, h, th)
            sc.wait_ge(small_gp_in, 16 * 4)
            sc.activation(a_neg[:, :, :, :], a_log[:, :, :, :], ACT.Exp).then_inc(a_exp, 1)
            for h in range(NH):
                exp_abs(0, h)
            for h in range(NH):
                log_one_plus(0, h)

            def y_parts(g, n, slot, dr):
                sc.wait_ge(turned, 4 * g + 4)
                if not isinstance(g, int) or g >= 2:
                    sc.wait_ge(added, g - 1)
                for b in range(VB, B):
                    at = DI * (b - VB)
                    last = sc.activation(y_part[:, slot, at:at + DI], bank[:, 5, at:at + DI], ACT.Copy,
                                         scale=c_col[:, dr, b, bass.ds(n, 1)])
                last.then_inc(part_ok, 1)

            def copy_b(g, slot):
                sc.wait_ge(b_bc, g + 1)
                if not isinstance(g, int) or g >= 2:
                    sc.wait_ge(dBx_ok, NH * (g - 1))
                sc.activation(b_row[:, slot, :], bank[:, 0:2, :].rearrange("p a t -> p (a t)"),
                              ACT.Copy).then_inc(b_sb, 1)

            def scan_step(g, n, slot, dr, ahead=True):
                inner = slice(1 - dr, S - dr)
                for h in range(NH):
                    if isinstance(g, int) and g == 0:
                        sc.wait_ge(delta_ok, h + 1)
                    if not isinstance(g, int) or g >= 2:
                        sc.wait_ge(scanned, NH * (g - 2) + h + 1)
                    sc.activation(tiles(dA[slot][h], B)[:, :, inner], tiles(delta[:, dr, h, :], B)[:, :, inner],
                                  ACT.Exp, scale=a_neg[:, dr, h, bass.ds(n, 1)]).then_inc(dA_ok, 1)
                if ahead:
                    copy_b(g + 1, 1 - slot)

            copy_b(0, 0)
            sc.wait_ge(a_ok, 1)
            wait_read(sc, "c0")
            for pair in range(VB // 2):
                evacuate(f"skip0_{pair}", acc[:, 2 * pair:2 * pair + 2, :], lambda ap: tiles(ap, 2))
            for g in range(N):
                scan_step(g, g, g % 2, 0)
                if g == 1:
                    silu_u(1)
                if g >= 2:
                    y_parts(g - 2, g - 2, g % 2, 0)
                if g - 1 in ROWS_AT:
                    copy_rows(1, ROWS_AT.index(g - 1))
                if g - 1 == C_AT:
                    copy_c(1)
                if g - 1 in D_AT:
                    h, th = D_AT.index(g - 1) // 2, D_AT.index(g - 1) % 2
                    absolute(1, h, th)
                    evacuate(f"d1{h}{th}", soft[1][h][1][:, half(th)], func=ACT.Relu, bias=col(3, h))
                if g in EXP_AT:
                    exp_abs(1, EXP_AT.index(g))
                if g == LN_AT:
                    for h in range(NH):
                        log_one_plus(1, h)
            sc.wait_ge(delta_ok, 2 * NH)
            for j in range(2):
                scan_step(N + j, j, j, 1)
                y_parts(N + j - 2, N + j - 2, j, 0)
            with sc.Fori(1, N // 2 - 1, 1) as i:
                for j in range(2):
                    scan_step(N + 2 * i + j, 2 * i + j, j, 1)
                    y_parts(N + 2 * i + j - 2, 2 * i + j - 2, j, 1)
            for j in range(2):
                scan_step(2 * N - 2 + j, N - 2 + j, j, 1, ahead=(j == 0))
                y_parts(2 * N - 4 + j, N - 4 + j, j, 1)
            for j in range(2):
                y_parts(2 * N - 2 + j, N - 2 + j, j, 1)

            evacuate("y_rest", y_rest)
            for g in range(2):
                evacuate(f"ctxT{g}", ctxT[:, half(g)])

            for g in range(2):
                sc.wait_ge(head_mask_ok, 2)
                src = tiles(to_read(sc, f"k{g}"), HB)
                for j in range(GH):
                    last = sc.activation(k_maskT[:, group(g), j, :], src, ACT.Copy, scale=head_mask[:, j:j + 1])
                was_read(f"k{g}", last)
                evacuate(f"v{g}", v_pad[:, group(g), :, 0:DH].rearrange("p b h e -> p (b h) e"),
                         lambda ap: tiles(ap, HB * HEADS))

            sc.wait_ge(q_first_ok, 1)
            src = to_read(sc, "q0")
            for g in range(2, HEADS // GH):
                last = sc.activation(q_maskT[:, g, half(0)], src, ACT.Copy, scale=group_mask[:, g:g + 1])
            was_read("q0", last)
            evacuate("x1T1", x1T[:, half(1)])

            def route_exp(g):
                sc.wait_ge(gate_d, g + 1)
                sc.activation(route[:, 1, group(g), :], route[:, 0, group(g), :], ACT.Exp).then_inc(gate_exp, 1)

            for i in range(LAST):
                if i < 2 * B:
                    wait_read(sc, f"s{i}")
                    for h in range(CH):
                        last = sc.activation(prob[i % 3][:, h, :], prob[i % 3][:, h, :], ACT.Exp, scale=SCALE,
                                             accum_out=rsum[:, i % 3, h:h + 1])
                    last.then_inc(exp_ok, 1)
                if 2 <= i < 2 * B + 2:
                    c = i - 2
                    to_read(sc, f"pT{c}")
                    if c >= 2:
                        if c % 2:
                            to_read(sc, f"av{c // 2 - 1}")
                        else:
                            sc.wait_ge(av_half, c // 2)
                    was_read(f"pT{c}", sc.activation(probT[c % 2].rearrange("p h k -> p (h k)"),
                                                     bank[:, 4:6, :].rearrange("p a t -> p (a t)"), ACT.Copy))
                if i % 2 == 0 and 4 <= i < 2 * B + 4:
                    b = i // 2 - 2
                    if b >= 2:
                        to_read(sc, f"wo{b - 2}")
                    evacuate(f"av{b}", outT[b % 2])
                if i == ROUTE0 + 1:
                    route_exp(0)
            evacuate("x2T1", x2T[:, half(1)])
            route_exp(1)
            evacuate("xeT0", xeT[:, 0:BANK])
            evacuate("xeT2", xeT[:, 2 * BANK:SLOTS], lambda ap: ap[:, 0:SLOTS - 2 * BANK])
            for e in range(E):
                to_read(sc, f"h{e}")
                if e >= 2:
                    to_read(sc, f"eoT{e - 2}")
                i = where[f"h{e}"][0]
                was_read(f"h{e}", sc.activation(
                    hid[e % 2], bank[:, i:i + 2, :].rearrange("p a (c s) -> p (a c) s", c=2)[:, :, 0:CAP], ACT.Relu))

        @block.tensor
        def _(pe):
            def turn(dst, src):
                return pe.transpose(dst, src, ident[0:src.shape[0], 0:src.shape[0]])

            def turn_group(name, sources):
                dst = to_fill(pe, name)
                for n, src in enumerate(sources):
                    last = turn(dst[0:src.shape[1], src.shape[0] * n:src.shape[0] * (n + 1)], src)
                filled(name, last)

            pe.wait_ge(ident_ok, 1)
            pe.wait_ge(x_in, 16)
            for g in range(2):
                turn_group(f"xT{g}", [x_tok[:, b, :] for b in range(HB * g, HB * g + HB)])
            pe.wait_ge(win_in, 16)
            turn_group("winT", [win[:, c, :] for c in range(2 * NH)])
            pe.wait_ge(wk_ok, K)
            turn_group("wkT0", [wk[:, 0, k, :] for k in range(K)])

            pe.wait_ge(pads_ok, 4)
            for g in range(2):
                wait_read(pe, f"xT{g}")
            wait_read(pe, "winT")

            def project_in(name, c, th):
                dst = to_fill(pe, name)
                filled(name, pe.matmul(dst, winT[:, c, :], xT[:, group(th), PAD:PAD + S], start=True, stop=True))

            for th in range(2):
                project_in(f"xi{th}", 1, th)

            def conv(dr):
                wait_read(pe, f"wkT{dr}")
                for th in range(2):
                    dst = to_fill(pe, f"u{dr}_{th}")
                    for k in range(K):
                        off = k if dr == 0 else 2 * PAD - k
                        last = pe.matmul(dst, wkT[:, dr, k, :], xT[:, group(th), off:off + S],
                                         start=(k == 0), stop=(k == K - 1))
                    filled(f"u{dr}_{th}", last)

            pe.wait_ge(small_in, 16 * 8)
            dst = to_fill(pe, "xproj")
            RX = R + 2 * N
            for j in range(2 * NH):
                turn(dst[:, RX * j:RX * (j + 1)], xproj[:, j // NH, P * (j % NH):P * (j % NH) + P])
            filled("xproj", turn(dst[:, 256:256 + 6 * NH], vec_rows[:, :]))
            conv(0)
            pe.wait_ge(dtw_ok, 1)
            pe.wait_ge(small_gp_in, 16 * 4)
            turn_group("dtw", [dtw[:, j // NH, j % NH, :] for j in range(2 * NH)])
            pe.wait_ge(wk_ok, 2 * K)
            turn_group("wkT1", [wk[:, 1, k, :] for k in range(K)])
            pe.wait_ge(wout_in, 16)
            turn_group("woutT", [wout[:, P * h:P * h + P] for h in range(NH)])

            def project_rows(dr, th):
                wait_read(pe, f"u{dr}_{th}")
                pe.wait_ge(silu_ok, dr + 1)
                dst = to_fill(pe, f"x{dr}_{th}")
                for h in range(NH):
                    last = pe.matmul(dst[0:XM, :], xprojT[:, dr, h, :], uT[:, dr, h, half(th)],
                                     start=(h == 0), stop=(h == NH - 1))
                filled(f"x{dr}_{th}", last)

            def turn_c(dr):
                pe.wait_ge(dt_rows_ok, 2 * dr + 2)
                dst = to_fill(pe, f"c{dr}")
                for b in range(B):
                    last = pe.transpose(dst[:, N * b:N * b + N], rows[C0:C0 + N, S * b:S * b + S],
                                        ident[C0:C0 + N, C0:C0 + N])
                filled(f"c{dr}", last)

            def project_delta(dr, h, th):
                pe.wait_ge(dt_rows_ok, 2 * dr + th + 1)
                dst = to_fill(pe, f"d{dr}{h}{th}")
                filled(f"d{dr}{h}{th}", pe.matmul(dst, dtT[DT0:XM, dr, h, :], rows[DT0:XM, half(th)],
                                                  start=True, stop=True))

            def skip(dr, pair):
                pe.wait_ge(diag_ok, 1)
                rest = pair == VB // 2
                if rest and dr:
                    dst = bank[:, 6, :]
                else:
                    dst = to_fill(pe, "y_rest" if rest else f"skip{dr}_{pair}")
                for n in range(2 * NH):
                    b, h = 2 * pair + n // NH, n % NH
                    last = pe.matmul(dst[:, P * n:P * n + P], uT[:, dr, h, S * b:S * b + S], diag_d[:, dr, h, :],
                                     start=(n == 0 and not (rest and dr)), stop=False, skip_group_check=True)
                if rest:
                    last.then_inc(u_used, 1)
                else:
                    filled(f"skip{dr}_{pair}", last)

            wait_read(pe, "xproj")
            wait_read(pe, "dtw")
            for th in range(2):
                project_rows(0, th)
            pe.wait_ge(attn_w_in, 64)
            turn_group("qkv", [wqkvo[:, n, :] for n in range(3)])
            for h in range(NH):
                for th in range(2):
                    project_in(f"z{h}{th}", NH + h, th)
            pe.wait_ge(wo_pad_ok, 1)
            turn_group("woT", [wo_pad[:, GH * g:GH * g + GH, :].rearrange("p h e -> p (h e)") for g in range(HEADS // GH)])
            turn_c(0)
            for h in range(NH):
                for th in range(2):
                    project_delta(0, h, th)
            for pair in range(B // 2):
                skip(0, pair)

            def to_all(dr, n, done):
                for th in range(2):
                    last = pe.matmul(bank[:, th, :], sel[:, bass.ds(n, 1), :].rearrange("p a m -> p (a m)"),
                                     parts[:, dr, half(th)], start=True, stop=True)
                last.then_inc(done, 1)

            def add_part(g, slot):
                pe.wait_ge(part_ok, g + 1)
                return pe.matmul(bank[:, 6, :], ident[:, :], y_part[:, slot, :], start=False, stop=False,
                                 skip_group_check=True)

            def b_ahead(g, dr, n):
                pe.wait_ge(b_sb, g + 2)
                to_all(dr, n, b_bc)

            def scan_step(g, slot):
                static = isinstance(g, int)
                pe.wait_ge(scanned, NH * g + NH)
                if static and g == 0:
                    wait_read(pe, "u1_0")
                    wait_read(pe, "u1_1")
                for pair in range(B // 2):
                    if not static or g >= 1:
                        if pair < VB // 2:
                            pe.wait_ge(acc_ok, VB * (g - 1) + 2 * pair + 2)
                        else:
                            pe.wait_ge(part_ok, g)
                    for n in range(2 * NH):
                        b, h = 2 * pair + n // NH, n % NH
                        last = turn(bank[:, 2 + pair, P * n:P * n + P], hs[slot][h][:, S * b:S * b + S])
                    last.then_inc(turned, 1)
                if not static or g >= 2:
                    add_part(g - 2, slot).then_inc(added, 1)

            pe.wait_ge(sel_ok, 1)
            pe.wait_ge(parts_ok, 2)
            wait_read(pe, held_at_scan[0])
            wait_read(pe, held_at_scan[1])
            to_all(0, 0, b_bc)
            pe.wait_ge(b_sb, 1)
            to_all(0, 1, b_bc)
            conv(1)
            for name in held_at_scan[4:6]:
                wait_read(pe, name)
            wait_read(pe, "c0")
            for g in range(N):
                if g == N - 2:
                    pe.wait_ge(parts_ok, 4)
                b_ahead(g, (g + 2) // N, (g + 2) % N)
                if g in ROWS_AT:
                    project_rows(1, ROWS_AT.index(g))
                if g == C_AT:
                    turn_c(1)
                if g in D_AT:
                    project_delta(1, D_AT.index(g) // 2, D_AT.index(g) % 2)
                if g in SKIP_AT:
                    pair = SKIP_AT.index(g)
                    skip(1, pair)
                    if pair == VB // 2 - 1:
                        skip(1, VB // 2)
                scan_step(g, g % 2)
            with pe.Fori(0, N // 2 - 1, 1) as i:
                for j in range(2):
                    b_ahead(N + 2 * i + j, 1, 2 * i + j + 2)
                    scan_step(N + 2 * i + j, j)
            for j in range(2):
                scan_step(2 * N - 2 + j, j)
            add_part(2 * N - 2, 0)
            filled("y_rest", add_part(2 * N - 1, 1))

            pe.wait_ge(b_sb, 2 * N)
            pe.wait_ge(part_ok, 2 * N)
            for th in range(2):
                pe.wait_ge(acc_ok, VB * (2 * N - 1) + min(HB * (th + 1), VB))
                if th:
                    wait_read(pe, "y_rest")
                for h in range(NH):
                    sources = [acc[:, b, P * h:P * h + P] if b < VB else
                               y_rest[:, DI * (b - VB) + P * h:DI * (b - VB) + P * h + P]
                               for b in range(HB * th, HB * th + HB)]
                    turn_group(f"yT{h}{th}", sources)
            pe.wait_ge(ctx_in, 16)
            for g in range(2):
                turn_group(f"ctxT{g}", [ctx_tok[:, b, :] for b in range(HB * g, HB * g + HB)])
            wait_read(pe, "woutT")
            for g in range(2):
                for h in range(NH):
                    wait_read(pe, f"yT{h}{g}")
                dst = to_fill(pe, f"o{g}")
                for b in range(HB):
                    t0 = TH * g + S * b
                    for h in range(NH):
                        last = pe.matmul(dst[:, D * b:D * b + D], yzT[:, h, t0:t0 + S], woutT[:, h, :],
                                         start=(h == 0), stop=(h == NH - 1))
                filled(f"o{g}", last)

            def turn_x1(g):
                pe.wait_ge(x1_ok, HB * (g + 1))
                turn_group(f"x1T{g}", [x1[:, b, :] for b in range(HB * g, HB * g + HB)])

            def queries(g):
                wait_read(pe, f"x1T{g}")
                dst = to_fill(pe, f"q{g}")
                filled(f"q{g}", pe.matmul(dst, qkvT[:, 0, :], x1T[:, half(g)], start=True, stop=True))

            for g in range(2):
                wait_read(pe, f"ctxT{g}")
                dst = to_fill(pe, f"k{g}")
                filled(f"k{g}", pe.matmul(dst, qkvT[:, 1, :], ctxT[:, half(g)], start=True, stop=True))
                dst = to_fill(pe, f"v{g}")
                for b in range(HB):
                    t0 = TH * g + S * b
                    last = pe.matmul(dst[:, D * b:D * b + D], ctxT[:, t0:t0 + S], qkvT[:, 2, :],
                                     start=True, stop=True)
                filled(f"v{g}", last)

            def scores(i):
                b, c = i // 2, i % 2
                to_fill(pe, f"s{i}")
                wait_read(pe, f"k{b // HB}")
                if i:
                    wait_read(pe, f"q{b // HB}")
                else:
                    pe.wait_ge(q_first_ok, 1)
                for g in (2 * c, 2 * c + 1):
                    last = pe.matmul(bank[:, g, :], q_maskT[:, g, S * b:S * b + S],
                                     k_maskT[:, b, :, :].rearrange("p j k -> p (j k)"), start=True, stop=True)
                filled(f"s{i}", last)

            def turn_probs(i):
                pe.wait_ge(prob_ok, i + 1)
                to_fill(pe, f"pT{i}")
                for h in range(CH):
                    last = turn(bank[:, 4 + h // 4, S * (h % 4):S * (h % 4) + S], prob[i % 3][:, h, :])
                filled(f"pT{i}", last)

            def weigh_values(i):
                b, c = i // 2, i % 2
                wait_read(pe, f"v{b // HB}")
                wait_read(pe, f"pT{i}")
                dst = bank[:, where[f"av{b}"][0], :] if c else to_fill(pe, f"av{b}")
                for h in range(CH * c, CH * c + CH):
                    g, j = h // GH, h % GH
                    last = pe.matmul(dst[32 * j:32 * j + 32, S * g:S * g + S], v_pad[:, b, h, :],
                                     probT[c][:, h % CH, :], start=True, stop=True)
                if not c:
                    last.then_inc(av_half, 1)
                else:
                    filled(f"av{b}", last)

            def gate_logits(g):
                pe.wait_ge(x2_ok, HB * (g + 1))
                turn_group(f"x2T{g}", [x2[:, b, :] for b in range(HB * g, HB * g + HB)])
                pe.wait_ge(moe_w_in, 48)
                dst = to_fill(pe, f"logits{g}")
                wait_read(pe, f"x2T{g}")
                for b in range(HB):
                    t0 = TH * g + S * b
                    last = pe.matmul(dst[:, E * b:E * b + E], x2T[:, t0:t0 + S], gate[:, :], start=True, stop=True)
                filled(f"logits{g}", last)

            def count_tokens(g):
                pe.wait_ge(consts_ok, 6)
                pe.wait_ge(route_mask, g + 1)
                dst = to_fill(pe, f"count{g}")
                masks = route_mask_bf[:, :, :].rearrange("p b e -> p (b e)")
                first = HB * g
                pe.matmul(dst[:, 0:HB * E], tri[:, :], masks[:, E * first:E * (first + HB)], start=True, stop=False,
                          skip_group_check=True)
                for ago in range(1, first + HB):
                    skipped = max(ago - first, 0)
                    last = pe.matmul(dst[:, E * skipped:E * HB], ones[:, :],
                                     masks[:, E * (first + skipped - ago):E * (first + HB - ago)],
                                     start=False, stop=(ago == first + HB - 1), skip_group_check=True)
                filled(f"count{g}", last)

            pe.wait_ge(v_zero, 1)
            turn_x1(0)
            queries(0)
            turn_x1(1)
            scores(0)
            queries(1)
            scores(1)
            for i in range(LAST):
                if 1 <= i < 2 * B - 1:
                    scores(i + 1)
                if 2 <= i < 2 * B + 2:
                    turn_probs(i - 2)
                if 3 <= i < 2 * B + 3:
                    weigh_values(i - 3)
                if i % 2 == 1 and 5 <= i < 2 * B + 5:
                    b = i // 2 - 2
                    wait_read(pe, f"av{b}")
                    dst = to_fill(pe, f"wo{b}")
                    for g in range(HEADS // GH):
                        last = pe.matmul(dst[:, 0:D], outT[b % 2][:, S * g:S * g + S], woT[:, g, :],
                                         start=(g == 0), stop=(g == HEADS // GH - 1))
                    filled(f"wo{b}", last)
                if i == ROUTE0:
                    gate_logits(0)
            count_tokens(0)
            gate_logits(1)
            count_tokens(1)

            for g in range(3):
                pe.wait_ge(xe_in[min(g, 1)], 16)
                turn_group(f"xeT{g}", [xe[:, j, :] for j in range(4 * g, min(4 * g + 4, ST))])
            for g in range(3):
                wait_read(pe, f"xeT{g}")
            for e in range(E + 2):
                if e < E:
                    to_fill(pe, f"h{e}")
                    for c in range(FC):
                        at = (BANK // 2) * (c % 2)
                        last = pe.matmul(bank[:, where[f"h{e}"][0] + c // 2, at:at + CAP],
                                         w1_sb[:, e, P * c:P * c + P], xeT[:, CAP * e:CAP * e + CAP],
                                         start=True, stop=True)
                    filled(f"h{e}", last)
                if 1 <= e <= E:
                    wait_read(pe, f"h{e - 1}")
                    dst = to_fill(pe, f"eoT{e - 1}")
                    for c in range(FC):
                        last = pe.matmul(dst[:, 0:CAP], w2_sb[:, e - 1, c, :], hid[(e - 1) % 2][:, c, :],
                                         start=(c == 0), stop=(c == FC - 1))
                    filled(f"eoT{e - 1}", last)
                if e >= 2:
                    wait_read(pe, f"eoT{e - 2}")
                    dst = to_fill(pe, f"eo{e - 2}")
                    for s in range(2):
                        last = turn(dst[0:HC, D * s:D * s + D], eoT[e % 2][:, HC * s:HC * s + HC])
                    filled(f"eo{e - 2}", last)

        @block.vector
        def _(ve):
            steps = [0]

            def link(ins):
                steps[0] += 1
                ins.then_inc(dve, 1)
                ve.wait_ge(dve, steps[0])

            def evacuate(name, dst, rearranged=lambda ap: ap):
                was_read(name, ve.tensor_copy(dst, rearranged(to_read(ve, name))))

            ve.wait_ge(win_in, 16)
            ve.wait_ge(conv_w_in, 32)
            for dr in range(2):
                for k in range(K):
                    ve.tensor_scalar(wk[:, dr, k, :], win[:, 0, :], cw[:, dr, 0, k:k + 1], None,
                                     ALU.mult).then_inc(wk_ok, 1)
                if dr == 0:
                    evacuate("xT0", xT[:, group(0), PAD:PAD + S], lambda ap: tiles(ap, HB))

            def conv(dr):
                pre = tiles(u_pre[:, dr, :], B)
                for k in range(K):
                    off = k if dr == 0 else 2 * PAD - k
                    src, tap = xi[:, :, off:off + S], cw[:, dr, 1, k:k + 1]
                    if k == 0:
                        link(ve.tensor_scalar(pre, src, tap, None, ALU.mult))
                    else:
                        last = ve.scalar_tensor_tensor(pre, src, tap, pre, ALU.mult, ALU.add)
                        if k < K - 1:
                            link(last)
                last.then_inc(conv_ok, 1)

            for th in range(2):
                wait_read(ve, f"xi{th}")
            ve.wait_ge(pads_ok, 4)
            conv(0)
            src = to_read(ve, "xproj")
            by_j = src[:, 0:(R + 2 * N) * 2 * NH].rearrange("p (j m) -> p j m", j=2 * NH)
            xp_j = xprojT[:, :, :, :].rearrange("p a h m -> p (a h) m")
            ve.wait_ge(xpad_ok, 1)
            for r in range(3):
                ve.tensor_copy(xp_j[:, :, N * r:N * r + N], by_j[:, :, R:R + N])
            ve.tensor_copy(xp_j[:, :, C0:C0 + N], by_j[:, :, R + N:R + 2 * N])
            ve.tensor_copy(xp_j[:, :, DT0:XM], by_j[:, :, 0:R])
            was_read("xproj", ve.tensor_copy(vec_cols[:, :], src[:, 256:256 + 6 * NH]))
            evacuate("wkT1", wkT[:, 1, :, :], lambda ap: tiles(ap, K))
            evacuate("woutT", woutT[:, :, :], lambda ap: tiles(ap[:, 0:NH * P], NH))
            wait_read(ve, "xproj")
            ve.tensor_reduce(sel_id[:, :], ident[0:B3, 0:B3].rearrange("p (r n) -> p n r", r=3), AX.X,
                             ALU.add).then_inc(sel_id_ok, 1)
            ve.tensor_reduce(head_mask[:, :], ident[:, :].rearrange("p (g j i) -> p j g i", g=4, j=GH),
                             AX.XY, ALU.add).then_inc(head_mask_ok, 1)
            ve.tensor_reduce(group_mask[:, :], ident[:, :].rearrange("p (g r) -> p g r", r=GH * DH),
                             AX.X, ALU.add).then_inc(head_mask_ok, 1)
            ve.wait_ge(head_mask_ok, 2)
            conv(1)

            def split_rows(dr, th):
                cols = half(th)
                src = to_read(ve, f"x{dr}_{th}")
                link(ve.tensor_copy(parts[:, dr, cols], src[0:B3, :]))
                ve.wait_ge(dt_rows_ok, 2 * dr + th + 1)
                was_read(f"x{dr}_{th}", ve.tensor_tensor(rests[:, cols], src[0:2 * N, :],
                                                         parts[0:2 * N, dr, cols], ALU.subtract))
                if dr:
                    wait_read(ve, f"x{dr}_{th}")
                    split_rests(ve, link, dr, th)

            def log1p_rest(dr, h):
                ve.wait_ge(parts_ok, 2 * dr + 2)
                e, rest = soft[dr][h][0], soft_rest[dr][h]
                ve.wait_ge(soft_in, 2 * NH * dr + h + 1)
                link(ve.tensor_scalar(rest, e, 1.0, -1.0, ALU.add, ALU.add))
                ve.tensor_tensor(rest, e, rest, ALU.subtract).then_inc(e_used, 1)

            def sum_delta(dr, h):
                _, relu, ln = soft[dr][h]
                ve.wait_ge(soft_in, 2 * NH * dr + NH + h + 1)
                ve.tensor_tensor(delta[:, dr, h, :], relu, ln, ALU.add).then_inc(delta_ok, 1)

            for th in range(2):
                split_rows(0, th)
            for h in range(NH):
                for th in range(2):
                    src = to_read(ve, f"d0{h}{th}")
                    ve.wait_ge(act, 2 * h + th + 1)
                    was_read(f"d0{h}{th}", ve.tensor_scalar(soft[0][h][1][:, half(th)], src, col(2, h), 0.0,
                                                            ALU.add, ALU.max))
            ve.wait_ge(a_exp, 1)
            ve.tensor_scalar(a_neg[:, :, :, :], a_neg[:, :, :, :], -1.0, None, ALU.mult).then_inc(a_ok, 1)
            for h in range(NH):
                log1p_rest(0, h)
            ve.wait_ge(e_used, NH)
            relu = soft[0][1][1]
            link(ve.tensor_tensor(relu, relu, soft_rest[0][1], ALU.add))
            for h in range(NH):
                if h == 0:
                    ve.wait_ge(rest_added, 1)
                sum_delta(0, h)
                weigh_u(ve, 0, h)

            def scan_step(g, slot, dr):
                for h in range(NH):
                    ve.wait_ge(dA_ok, NH * g + h + 1)
                    ve.wait_ge(dBx_ok, NH * g + h + 1)
                    if not isinstance(g, int) or g >= 2:
                        ve.wait_ge(turned, 4 * (g - 1))
                    o, a, v = hs[slot][h], dA[slot][h], dBx[slot][h]
                    if dr:
                        o, a, v = o[:, ::-1], a[:, ::-1], v[:, ::-1]
                    ve.tensor_tensor_scan(o, a, v, 0.0, ALU.mult, ALU.add).then_inc(scanned, 1)

            def sum_y(g, n, dr):
                for b in range(VB):
                    ve.wait_ge(turned, 4 * g + b // 2 + 1)
                    if isinstance(g, int) and g == 0:
                        wait_read(ve, f"skip0_{b // 2}")
                    else:
                        ve.wait_ge(acc_ok, VB * (g - 1) + b + 1)
                    at = DI * (b % 2)
                    ve.scalar_tensor_tensor(acc[:, b, :], bank[:, 2 + b // 2, at:at + DI],
                                            c_col[:, dr, b, bass.ds(n, 1)], acc[:, b, :],
                                            ALU.mult, ALU.add).then_inc(acc_ok, 1)

            wait_read(ve, "c0")
            for g in range(N):
                scan_step(g, g % 2, 0)
                if g >= 1:
                    sum_y(g - 1, g - 1, 0)
                if g - 1 in ROWS_AT:
                    split_rows(1, ROWS_AT.index(g - 1))
                if g in SKIP_AT:
                    k = SKIP_AT.index(g)
                    src = tiles(to_read(ve, f"skip1_{k}"), 2)
                    ve.wait_ge(acc_ok, VB * g)
                    pair = acc[:, 2 * k:2 * k + 2, :]
                    was_read(f"skip1_{k}", ve.tensor_tensor(pair, src, pair, ALU.add))
                    wait_read(ve, f"skip1_{k}")
                if g in REST_AT:
                    h = REST_AT.index(g)
                    if h:
                        ve.wait_ge(rest_added, 1 + h)
                    log1p_rest(1, h)
                if g in DELTA_AT:
                    h = DELTA_AT.index(g)
                    ve.wait_ge(rest_added, 1 + h + 1)
                    sum_delta(1, h)
                    if h:
                        weigh_u(ve, 1, h)
            wait_read(ve, "c1")
            for j in range(2):
                scan_step(N + j, j, 1)
                sum_y(N + j - 1, (N + j - 1) % N, j)
            with ve.Fori(1, N // 2, 1) as i:
                for j in range(2):
                    scan_step(N + 2 * i + j, j, 1)
                    sum_y(N + 2 * i + j - 1, 2 * i + j - 1, 1)
            sum_y(2 * N - 1, N - 1, 1)

            for th in range(2):
                for h in range(NH):
                    wait_read(ve, f"z{h}{th}")
                    src = to_read(ve, f"yT{h}{th}")
                    was_read(f"yT{h}{th}", ve.tensor_tensor(yzT[:, h, half(th)], src, szT[:, h, half(th)], ALU.mult))

            def moments_of(res, b):
                link(ve.bn_stats(stats[:, b, :], res[:, b, :]))
                ve.bn_aggr(moments[:, b, :], stats[:, b, :]).then_inc(var_ok, 1)

            def normalize(res, dst, norm, g, done):
                ve.wait_ge(rstd_ok, 2 * norm + g + 1)
                for b in range(HB * g, HB * g + HB):
                    ve.tensor_scalar(dst[:, b, :], res[:, b, :], moments[:, b, 0:1], rstd[:, b:b + 1],
                                     ALU.subtract, ALU.mult).then_inc(done, 1)

            for g in range(2):
                src = tiles(to_read(ve, f"o{g}"), HB)
                was_read(f"o{g}", ve.tensor_tensor(res1[:, group(g), :], src, x_tok[:, group(g), :], ALU.add))
                wait_read(ve, f"o{g}")
                for b in range(HB * g, HB * g + HB):
                    if b == HB + 2:
                        normalize(res1, x1, 0, 0, x1_ok)
                    moments_of(res1, b)
            evacuate("x1T0", x1T[:, half(0)])
            normalize(res1, x1, 0, 1, x1_ok)

            def mask_queries(th, groups):
                src = to_read(ve, f"q{th}")
                for g in groups:
                    last = ve.tensor_scalar(q_maskT[:, g, half(th)], src, group_mask[:, g:g + 1], None, ALU.mult)
                return last

            mask_queries(0, range(2)).then_inc(q_first_ok, 1)

            def shift_scores(i):
                c = i % 2
                to_read(ve, f"s{i}")
                src = bank[:, 2 * c:2 * c + 2, :].rearrange("p a (j k) -> p (a j) k", j=GH)
                if i >= 3:
                    to_read(ve, f"pT{i - 3}")
                if i >= 2:
                    wait_read(ve, f"s{i - 2}")
                link(ve.tensor_reduce(rmax[:, c, :], src, AX.X, ALU.max))
                was_read(f"s{i}", ve.tensor_tensor(prob[i % 3], src, rmax[:, c, :].unsqueeze(2).to_broadcast([P, CH, S]),
                                                   ALU.subtract))

            def invert_sums(i):
                ve.wait_ge(exp_ok, i + 1)
                ve.reciprocal(rsum[:, i % 3, :], rsum[:, i % 3, :]).then_inc(sums_ok, 1)

            def over_e(ap):
                return ap.unsqueeze(2).to_broadcast([P, HB, E])

            def choose_expert(g):
                bs = group(g)
                top, chosen = (route_b[:, k, bs] for k in (0, 1))
                shifted, scratch = route[:, 0, bs, :], route[:, 2, bs, :]
                logits = tiles(to_read(ve, f"logits{g}")[:, 0:HB * E], HB)
                link(ve.tensor_reduce(top, logits, AX.X, ALU.max))
                ve.tensor_tensor(shifted, logits, over_e(top), ALU.subtract).then_inc(gate_d, 1)
                was_read(f"logits{g}", ve.tensor_tensor(scratch, logits, over_e(top), ALU.is_ge))
                wait_read(ve, f"logits{g}")
                link(ve.tensor_tensor(scratch, scratch, rev_e[:, bs, :], ALU.mult))
                link(ve.tensor_reduce(chosen, scratch, AX.X, ALU.max))
                ve.tensor_tensor(route_mask_bf[:, bs, :], rev_e[:, bs, :], over_e(chosen),
                                 ALU.is_equal).then_inc(route_mask, 1)

            def place_tokens(g):
                bs = group(g)
                chosen, total, p_top, place, fits, slot, take = (route_b[:, k, bs] for k in range(1, 8))
                e_exp, scratch = route[:, 1, bs, :], route[:, 2, bs, :]
                ve.wait_ge(route_mask, g + 1)
                counts = tiles(to_read(ve, f"count{g}")[:, 0:HB * E], HB)
                was_read(f"count{g}", ve.tensor_tensor(scratch, counts, route_mask_bf[:, bs, :], ALU.mult))
                wait_read(ve, f"count{g}")
                link(ve.tensor_reduce(place, scratch, AX.X, ALU.add))
                ve.tensor_scalar(fits, place, float(CAP), None, ALU.is_le)
                link(ve.scalar_tensor_tensor(slot, chosen, -float(CAP), place, ALU.mult, ALU.add))
                link(ve.tensor_scalar(take, slot, float(CAP * E - 1 - SLOTS), None, ALU.add))
                link(ve.scalar_tensor_tensor(slot, slot, float(CAP * E - 1), dump[:, bs], ALU.add, ALU.subtract))
                link(ve.tensor_tensor(slot, slot, fits, ALU.mult))
                ve.tensor_tensor(slot_u[:, bs], slot, dump[:, bs], ALU.add).then_inc(slots_ok, 1)
                link(ve.tensor_tensor(take, take, fits, ALU.mult))
                ve.tensor_scalar(take_u[:, bs], take, float(SLOTS), None, ALU.add).then_inc(take_ok, 1)
                ve.wait_ge(gate_exp, g + 1)
                link(ve.tensor_reduce(total, e_exp, AX.X, ALU.add))
                link(ve.reciprocal(p_top, total))
                link(ve.tensor_tensor(p_top, p_top, fits, ALU.mult))

            for i in range(LAST + 1):
                if i < 2 * B:
                    shift_scores(i)
                if 1 <= i <= 2 * B:
                    invert_sums(i - 1)
                if i == 3:
                    was_read("q1", mask_queries(1, range(HEADS // GH)))
                if i % 2 == 0 and 6 <= i < 2 * B + 6:
                    b = i // 2 - 3
                    src = to_read(ve, f"wo{b}")
                    was_read(f"wo{b}", ve.tensor_tensor(res2[:, b, :], src[:, 0:D], x1[:, b, :], ALU.add))
                    wait_read(ve, f"wo{b}")
                    moments_of(res2, b)
                if i == 2 * B + 1:
                    normalize(res2, x2, 1, 0, x2_ok)
                if i == ROUTE0:
                    evacuate("x2T0", x2T[:, half(0)])
            choose_expert(0)
            normalize(res2, x2, 1, 1, x2_ok)
            place_tokens(0)
            choose_expert(1)
            place_tokens(1)

            evacuate("xeT1", xeT[:, BANK:2 * BANK])
            for e in range(E + 1):
                if e < E:
                    if e >= 2:
                        to_read(ve, f"eo{e - 2}")
                    evacuate(f"eoT{e}", eoT[e % 2], lambda ap: ap[:, 0:CAP])
                if e == 0:
                    continue
                evacuate(f"eo{e - 1}", eo[0:HC, e - 1, :, :], lambda ap: ap[0:HC, 0:2 * D].rearrange("p (s d) -> p s d", s=2))

            for b in range(B):
                ve.wait_ge(gathered[b // 2], 32)
                link(ve.scalar_tensor_tensor(res3[:, b, :], back[:, b, :], route_b[:, 3, b:b + 1], x2[:, b, :],
                                             ALU.mult, ALU.add))
                moments_of(res3, b)
            for g in range(2):
                normalize(res3, y_out, 2, g, y_ok)


_INS = ["x", "ctx_1024", "L0_attn_in_proj_w", "L0_attn_conv_w", "L0_attn_conv_bias", "L0_attn_x_proj_w",
        "L0_attn_dt_proj_w", "L0_attn_dt_proj_bias", "L0_attn_A_log", "L0_attn_D_skip", "L0_attn_convb_w",
        "L0_attn_convb_bias", "L0_attn_x_proj_b_w", "L0_attn_dt_proj_b_w", "L0_attn_dt_proj_b_bias",
        "L0_attn_A_b_log", "L0_attn_D_b_skip", "L0_attn_out_proj_w", "L0_xattn_Wq", "L0_xattn_Wk", "L0_xattn_Wv",
        "L0_xattn_Wo", "L0_ffn_gate_w", "L0_ffn_w1", "L0_ffn_w2"]


def kernel(**inputs):
    import numpy as _np
    import concourse.bacc as _bacc
    from concourse import mybir as _mybir
    from concourse.bass_utils import run_bass_kernel_spmd as _run

    nc = _bacc.Bacc("TRN2", target_bir_lowering=False, num_devices=1)
    arrays, args = {}, []
    for name in _INS:
        a = _np.ascontiguousarray(inputs[name])
        arrays[f"in_{name}"] = a
        args.append(nc.dram_tensor(f"in_{name}", a.shape, _mybir.dt.from_np(a.dtype), kind="ExternalInput").ap())
    shape = inputs["x"].shape
    args.append(nc.dram_tensor("out_0", shape, _mybir.dt.from_np(_np.dtype("float32")), kind="ExternalOutput").ap())
    decoder_layer_kernel(nc, *args)
    r = _run(nc, [arrays], core_ids=[0])
    return r.results[0]["out_0"]
```
